# Optimizing a Trainium2 kernel written in Bass

```python
import numpy as np
import jax
import jax.numpy as jnp

def _softmax(x, axis=-1):
    return jax.nn.softmax(x, axis=axis)
def _gelu(x):
    return jax.nn.gelu(x, approximate=True)
def _silu(x):
    return jax.nn.silu(x)
def _sigmoid(x):
    return jax.nn.sigmoid(x)
def _layernorm(x, axis=-1, eps=1e-5):
    m = jnp.mean(x, axis=axis, keepdims=True)
    v = jnp.var(x, axis=axis, keepdims=True)
    return (x - m) / jnp.sqrt(v + eps)
def _scatter_add(tgt, idx, src, axis=0):
    return tgt.at[idx].add(src)
def _segment_sum(src, seg, n):
    return jax.ops.segment_sum(src, seg, n)

kernel_name = 'mk_conv_preact_d4_conv_nchw128_c5f77c'

def setup_inputs(seed: int = 0):
    np.random.seed(seed)
    _w = jnp.asarray
    def _rec_inputs():
        import jax
        import jax.numpy as jnp
        _gk = jax.random.key(seed)
        x = -0.0005153 + 1.001 * jax.random.normal(jax.random.fold_in(_gk, 1), (8, 128, 56, 56), jnp.float32)
        return x
    x = _rec_inputs()
    def _L0_conv_setup():
        import jax, jax.numpy as jnp
        import numpy as np
        NW = 7
        HEADS = 8
        QK = 128
        DIM = 128
        TOPK = 4
        SCALE = QK ** (-0.5)

        def _forward(x, W_qkv, b_qkv, lepe_w, lepe_b, W_o, b_o):
            N, C, H, W = x.shape
            hh, ww = (H // NW, W // NW)
            p2, w2 = (NW * NW, hh * ww)
            hd = DIM // HEADS
            xh = x.transpose(0, 2, 3, 1)
            xw = xh.reshape(N, NW, hh, NW, ww, C).transpose(0, 1, 3, 2, 4, 5)
            xw = xw.reshape(N, p2, hh, ww, C)
            proj = xw @ W_qkv + b_qkv
            q = proj[..., :QK]
            kv = proj[..., QK:]
            q_pix = q.reshape(N, p2, w2, QK)
            kv_pix = kv.reshape(N, p2, w2, QK + DIM)
            q_win = jax.lax.stop_gradient(q.mean((2, 3)))
            k_win = jax.lax.stop_gradient(kv[..., :QK].mean((2, 3)))
            v_img = kv[..., QK:].reshape(N, NW, NW, hh, ww, C)
            v_img = v_img.transpose(0, 5, 1, 3, 2, 4).reshape(N, C, H, W)
            lepe = jax.lax.conv_general_dilated(v_img, lepe_w, window_strides=(1, 1), padding='SAME', feature_group_count=C, dimension_numbers=('NCHW', 'OIHW', 'NCHW')) + lepe_b[None, :, None, None]
            lepe = lepe.transpose(0, 2, 3, 1)
            logit = jnp.einsum('npc,nqc->npq', q_win * SCALE, k_win)
            topk_logit, r_idx = jax.lax.top_k(logit, TOPK)
            r_weight = jax.nn.softmax(topk_logit, axis=-1)
            kv_sel = jax.vmap(lambda kvn, idx: kvn[idx])(kv_pix, r_idx)
            k_sel = kv_sel[..., :QK].reshape(N * p2, TOPK * w2, HEADS, hd).transpose(0, 2, 1, 3)
            v_sel = kv_sel[..., QK:].reshape(N * p2, TOPK * w2, HEADS, hd).transpose(0, 2, 1, 3)
            q_h = q_pix.reshape(N * p2, w2, HEADS, hd).transpose(0, 2, 1, 3)
            attn = jax.nn.softmax(jnp.einsum('bmqc,bmkc->bmqk', q_h * SCALE, k_sel), axis=-1)
            o = jnp.einsum('bmqk,bmkc->bmqc', attn, v_sel)
            o = o.transpose(0, 2, 1, 3).reshape(N, NW, NW, hh, ww, C)
            o = o.transpose(0, 1, 3, 2, 4, 5).reshape(N, H, W, C)
            out = (o + lepe) @ W_o + b_o
            return out.transpose(0, 3, 1, 2)
        key = jax.random.key(seed)
        ks = jax.random.split(key, 8)
        N, C, H, W = (8, DIM, 56, 56)
        x = jax.random.normal(ks[0], (N, C, H, W), dtype=jnp.float32)
        W_qkv = jax.random.normal(ks[1], (DIM, 2 * QK + DIM), dtype=jnp.float32) * DIM ** (-0.5)
        b_qkv = jnp.zeros((2 * QK + DIM,), dtype=jnp.float32)
        lepe_w = jax.random.normal(ks[2], (DIM, 1, 3, 3), dtype=jnp.float32) * 0.1
        lepe_b = jnp.zeros((DIM,), dtype=jnp.float32)
        W_o = jax.random.normal(ks[3], (DIM, DIM), dtype=jnp.float32) * DIM ** (-0.5)
        b_o = jnp.zeros((DIM,), dtype=jnp.float32)
        return {'x': x, 'W_qkv': W_qkv, 'b_qkv': b_qkv, 'lepe_w': lepe_w, 'lepe_b': lepe_b, 'W_o': W_o, 'b_o': b_o}
    _L0_conv_all = _L0_conv_setup()
    _L0_conv_in = {k: v for k, v in _L0_conv_all.items() if k in ('W_qkv', 'b_qkv', 'lepe_w', 'lepe_b', 'W_o', 'b_o', )}
    del _L0_conv_all

    def _L1_conv_setup():
        import jax, jax.numpy as jnp
        import numpy as np
        BN_EPS = 1e-05

        def tanhshrink(x):
            return x - jnp.tanh(x)
        key = jax.random.key(seed)
        ks = jax.random.split(key, 10)
        B, C, H, W = (32, 128, 32, 32)
        RIN, RH, OC = (256, 512, 128)
        s = lambda k, shape, fan: jax.random.normal(k, shape, dtype=jnp.float32) * (1.0 / np.sqrt(fan))
        return {'x': jax.random.normal(ks[0], (B, C, H, W), dtype=jnp.float32), 'gamma': jnp.ones((C,), jnp.float32), 'beta': jnp.zeros((C,), jnp.float32), 'w_in': s(ks[1], (RIN, C), C), 'b_in': jnp.zeros((RIN,), jnp.float32), 'w_ih': s(ks[2], (RH, RIN), RIN), 'b_ih': jnp.zeros((RH,), jnp.float32), 'w_hh': s(ks[3], (RH, RH), RH), 'b_hh': jnp.zeros((RH,), jnp.float32), 'w_out': s(ks[4], (OC, RH), RH), 'b_out': jnp.zeros((OC,), jnp.float32)}
    _L1_conv_all = _L1_conv_setup()
    _L1_conv_in = {k: v for k, v in _L1_conv_all.items() if k in ('gamma', 'beta', 'w_in', 'b_in', 'w_ih', 'b_ih', 'w_hh', 'b_hh', 'w_out', 'b_out', )}
    del _L1_conv_all

    def _L2_conv_setup():
        import jax, jax.numpy as jnp
        import numpy as np
        key = jax.random.key(seed)
        k1, k2, k3, k4 = jax.random.split(key, 4)
        B, I, O, H, W, p = (16, 128, 128, 128, 128, 4)
        x = jax.random.normal(k1, (B, I, H, W), dtype=jnp.float32)
        w3 = jax.random.normal(k2, (O, I, 3, 3), dtype=jnp.float32) * 0.05
        w1 = jax.random.normal(k3, (O, I), dtype=jnp.float32) * 0.05
        b = jax.random.normal(k4, (O, I), dtype=jnp.float32) * 0.05
        return {'x': x, 'w3': w3, 'w1': w1, 'b': b, 'p': p}
    _L2_conv_all = _L2_conv_setup()
    _L2_conv_in = {k: v for k, v in _L2_conv_all.items() if k in ('w3', 'w1', 'b', )}
    del _L2_conv_all

    def _L3_conv_setup():
        import jax, jax.numpy as jnp
        import numpy as np
        EPS = 1e-05

        def _conv3x3(x, w, stride=1):
            return jax.lax.conv_general_dilated(x, w, window_strides=(stride, stride), padding=((1, 1), (1, 1)), dimension_numbers=('NCHW', 'OIHW', 'NCHW'))

        def _bn(x, gamma, beta, mean, var):
            inv = jax.lax.rsqrt(var + EPS)
            return (x - mean[None, :, None, None]) * (gamma * inv)[None, :, None, None] + beta[None, :, None, None]
        key = jax.random.key(seed)
        ks = jax.random.split(key, 8)
        C = 128
        x = jax.random.normal(ks[0], (64, C, 56, 56), dtype=jnp.float32)
        w1 = jax.random.normal(ks[1], (C, C, 3, 3), dtype=jnp.float32) * 0.05
        w2 = jax.random.normal(ks[2], (C, C, 3, 3), dtype=jnp.float32) * 0.05
        gamma1 = jnp.ones((C,), jnp.float32)
        beta1 = jnp.zeros((C,), jnp.float32)
        mean1 = jax.random.normal(ks[3], (C,), dtype=jnp.float32) * 0.1
        var1 = jax.random.uniform(ks[4], (C,), minval=0.5, maxval=1.5, dtype=jnp.float32)
        gamma2 = jnp.ones((C,), jnp.float32)
        beta2 = jnp.zeros((C,), jnp.float32)
        mean2 = jax.random.normal(ks[5], (C,), dtype=jnp.float32) * 0.1
        var2 = jax.random.uniform(ks[6], (C,), minval=0.5, maxval=1.5, dtype=jnp.float32)
        return {'x': x, 'w1': w1, 'w2': w2, 'gamma1': gamma1, 'beta1': beta1, 'mean1': mean1, 'var1': var1, 'gamma2': gamma2, 'beta2': beta2, 'mean2': mean2, 'var2': var2}
    _L3_conv_all = _L3_conv_setup()
    _L3_conv_in = {k: v for k, v in _L3_conv_all.items() if k in ('w1', 'w2', 'gamma1', 'beta1', 'mean1', 'var1', 'gamma2', 'beta2', 'mean2', 'var2', )}
    del _L3_conv_all

    return {
        "x": x,
        "L0_conv_W_qkv": _L0_conv_in["W_qkv"],
        "L0_conv_b_qkv": _L0_conv_in["b_qkv"],
        "L0_conv_lepe_w": _L0_conv_in["lepe_w"],
        "L0_conv_lepe_b": _L0_conv_in["lepe_b"],
        "L0_conv_W_o": _L0_conv_in["W_o"],
        "L0_conv_b_o": _L0_conv_in["b_o"],
        "L1_conv_gamma": _L1_conv_in["gamma"],
        "L1_conv_beta": _L1_conv_in["beta"],
        "L1_conv_w_in": _L1_conv_in["w_in"],
        "L1_conv_b_in": _L1_conv_in["b_in"],
        "L1_conv_w_ih": _L1_conv_in["w_ih"],
        "L1_conv_b_ih": _L1_conv_in["b_ih"],
        "L1_conv_w_hh": _L1_conv_in["w_hh"],
        "L1_conv_b_hh": _L1_conv_in["b_hh"],
        "L1_conv_w_out": _L1_conv_in["w_out"],
        "L1_conv_b_out": _L1_conv_in["b_out"],
        "L2_conv_w3": _L2_conv_in["w3"],
        "L2_conv_w1": _L2_conv_in["w1"],
        "L2_conv_b": _L2_conv_in["b"],
        "L3_conv_w1": _L3_conv_in["w1"],
        "L3_conv_w2": _L3_conv_in["w2"],
        "L3_conv_gamma1": _L3_conv_in["gamma1"],
        "L3_conv_beta1": _L3_conv_in["beta1"],
        "L3_conv_mean1": _L3_conv_in["mean1"],
        "L3_conv_var1": _L3_conv_in["var1"],
        "L3_conv_gamma2": _L3_conv_in["gamma2"],
        "L3_conv_beta2": _L3_conv_in["beta2"],
        "L3_conv_mean2": _L3_conv_in["mean2"],
        "L3_conv_var2": _L3_conv_in["var2"],
    }

def reference(x, L0_conv_W_qkv, L0_conv_b_qkv, L0_conv_lepe_w, L0_conv_lepe_b, L0_conv_W_o, L0_conv_b_o, L1_conv_gamma, L1_conv_beta, L1_conv_w_in, L1_conv_b_in, L1_conv_w_ih, L1_conv_b_ih, L1_conv_w_hh, L1_conv_b_hh, L1_conv_w_out, L1_conv_b_out, L2_conv_w3, L2_conv_w1, L2_conv_b, L3_conv_w1, L3_conv_w2, L3_conv_gamma1, L3_conv_beta1, L3_conv_mean1, L3_conv_var1, L3_conv_gamma2, L3_conv_beta2, L3_conv_mean2, L3_conv_var2):
    import jax
    import jax.numpy as jnp
    def _L0_conv_ref(x, W_qkv, b_qkv, lepe_w, lepe_b, W_o, b_o):
        import jax, jax.numpy as jnp
        import numpy as np
        NW = 7
        HEADS = 8
        QK = 128
        DIM = 128
        TOPK = 4
        SCALE = QK ** (-0.5)

        def _forward(x, W_qkv, b_qkv, lepe_w, lepe_b, W_o, b_o):
            N, C, H, W = x.shape
            hh, ww = (H // NW, W // NW)
            p2, w2 = (NW * NW, hh * ww)
            hd = DIM // HEADS
            xh = x.transpose(0, 2, 3, 1)
            xw = xh.reshape(N, NW, hh, NW, ww, C).transpose(0, 1, 3, 2, 4, 5)
            xw = xw.reshape(N, p2, hh, ww, C)
            proj = xw @ W_qkv + b_qkv
            q = proj[..., :QK]
            kv = proj[..., QK:]
            q_pix = q.reshape(N, p2, w2, QK)
            kv_pix = kv.reshape(N, p2, w2, QK + DIM)
            q_win = jax.lax.stop_gradient(q.mean((2, 3)))
            k_win = jax.lax.stop_gradient(kv[..., :QK].mean((2, 3)))
            v_img = kv[..., QK:].reshape(N, NW, NW, hh, ww, C)
            v_img = v_img.transpose(0, 5, 1, 3, 2, 4).reshape(N, C, H, W)
            lepe = jax.lax.conv_general_dilated(v_img, lepe_w, window_strides=(1, 1), padding='SAME', feature_group_count=C, dimension_numbers=('NCHW', 'OIHW', 'NCHW')) + lepe_b[None, :, None, None]
            lepe = lepe.transpose(0, 2, 3, 1)
            logit = jnp.einsum('npc,nqc->npq', q_win * SCALE, k_win)
            topk_logit, r_idx = jax.lax.top_k(logit, TOPK)
            r_weight = jax.nn.softmax(topk_logit, axis=-1)
            kv_sel = jax.vmap(lambda kvn, idx: kvn[idx])(kv_pix, r_idx)
            k_sel = kv_sel[..., :QK].reshape(N * p2, TOPK * w2, HEADS, hd).transpose(0, 2, 1, 3)
            v_sel = kv_sel[..., QK:].reshape(N * p2, TOPK * w2, HEADS, hd).transpose(0, 2, 1, 3)
            q_h = q_pix.reshape(N * p2, w2, HEADS, hd).transpose(0, 2, 1, 3)
            attn = jax.nn.softmax(jnp.einsum('bmqc,bmkc->bmqk', q_h * SCALE, k_sel), axis=-1)
            o = jnp.einsum('bmqk,bmkc->bmqc', attn, v_sel)
            o = o.transpose(0, 2, 1, 3).reshape(N, NW, NW, hh, ww, C)
            o = o.transpose(0, 1, 3, 2, 4, 5).reshape(N, H, W, C)
            out = (o + lepe) @ W_o + b_o
            return out.transpose(0, 3, 1, 2)
        return _forward(x, W_qkv, b_qkv, lepe_w, lepe_b, W_o, b_o)

    def _L1_conv_ref(x, gamma, beta, w_in, b_in, w_ih, b_ih, w_hh, b_hh, w_out, b_out):
        import jax, jax.numpy as jnp
        import numpy as np
        BN_EPS = 1e-05

        def tanhshrink(x):
            return x - jnp.tanh(x)
        B, C, H, W = x.shape
        RH = w_hh.shape[0]
        mean = jnp.mean(x, axis=(0, 2, 3), keepdims=True)
        var = jnp.var(x, axis=(0, 2, 3), keepdims=True)
        xn = (x - mean) * jax.lax.rsqrt(var + BN_EPS)
        xn = xn * gamma[None, :, None, None] + beta[None, :, None, None]
        seq = jnp.transpose(xn, (0, 2, 3, 1)).reshape(B, H * W, C)
        inp = tanhshrink(jnp.einsum('blc,ic->bli', seq, w_in) + b_in)
        xgate = jnp.einsum('bli,hi->blh', inp, w_ih) + b_ih + b_hh
        xgate_t = jnp.transpose(xgate, (1, 0, 2))

        def step(h, xg):
            h_new = jnp.tanh(xg + h @ w_hh.T)
            return (h_new, h_new)
        h0 = jnp.zeros((B, RH), x.dtype)
        _, hs = jax.lax.scan(step, h0, xgate_t)
        outputs = jnp.transpose(hs, (1, 0, 2))
        out_seq = jnp.einsum('blh,oh->blo', outputs, w_out) + b_out
        out = jnp.transpose(out_seq.reshape(B, H, W, -1), (0, 3, 1, 2))
        return out

    def _L2_conv_ref(x, w3, w1, b, p):
        import jax, jax.numpy as jnp
        import numpy as np
        O, I = (w3.shape[0], w3.shape[1])
        i = jnp.arange(O)[:, None]
        j = jnp.arange(I)[None, :]
        m3 = (j - i) % p == 0
        w3m = w3 * m3[:, :, None, None].astype(w3.dtype)
        out = jax.lax.conv_general_dilated(x, w3m, window_strides=(1, 1), padding=((1, 1), (1, 1)), dimension_numbers=('NCHW', 'OIHW', 'NCHW'))
        w1m = w1 * (~m3).astype(w1.dtype)
        out = out + jnp.einsum('oi,bihw->bohw', w1m, x)
        out = out + b.sum(axis=1)[None, :, None, None]
        return out

    def _L3_conv_ref(x, w1, w2, gamma1, beta1, mean1, var1, gamma2, beta2, mean2, var2):
        import jax, jax.numpy as jnp
        import numpy as np
        EPS = 1e-05

        def _conv3x3(x, w, stride=1):
            return jax.lax.conv_general_dilated(x, w, window_strides=(stride, stride), padding=((1, 1), (1, 1)), dimension_numbers=('NCHW', 'OIHW', 'NCHW'))

        def _bn(x, gamma, beta, mean, var):
            inv = jax.lax.rsqrt(var + EPS)
            return (x - mean[None, :, None, None]) * (gamma * inv)[None, :, None, None] + beta[None, :, None, None]
        residual = x
        out = _conv3x3(x, w1, stride=1)
        out = jax.nn.relu(_bn(out, gamma1, beta1, mean1, var1))
        out = _conv3x3(out, w2, stride=1)
        out = _bn(out, gamma2, beta2, mean2, var2)
        return jax.nn.relu(out + residual)

    def _gn(v, G=32, eps=1e-5):
        B_, C_, H_, W_ = v.shape
        g = v.reshape(B_, G, C_ // G, H_, W_)
        m = jnp.mean(g, axis=(2, 3, 4), keepdims=True)
        s = jnp.var(g, axis=(2, 3, 4), keepdims=True)
        return ((g - m) / jnp.sqrt(s + eps)).reshape(v.shape)

    def _ln_c(v, eps=1e-6):
        m = jnp.mean(v, axis=1, keepdims=True)
        s = jnp.var(v, axis=1, keepdims=True)
        return (v - m) / jnp.sqrt(s + eps)

    def _ln_t(v, eps=1e-5):
        m = jnp.mean(v, axis=-1, keepdims=True)
        s = jnp.var(v, axis=-1, keepdims=True)
        return (v - m) / jnp.sqrt(s + eps)

    def _to_tokens(v):
        B_, C_, H_, W_ = v.shape
        return v.reshape(B_, C_, H_ * W_).transpose(0, 2, 1)
    def _from_tokens(t, like):
        B_, C_, H_, W_ = like.shape
        return t.transpose(0, 2, 1).reshape(B_, C_, H_, W_)

    x = x + _L0_conv_ref(_gn(x), L0_conv_W_qkv, L0_conv_b_qkv, L0_conv_lepe_w, L0_conv_lepe_b, L0_conv_W_o, L0_conv_b_o)
    x = x + _L1_conv_ref(_gn(x), L1_conv_gamma, L1_conv_beta, L1_conv_w_in, L1_conv_b_in, L1_conv_w_ih, L1_conv_b_ih, L1_conv_w_hh, L1_conv_b_hh, L1_conv_w_out, L1_conv_b_out)
    x = x + _L2_conv_ref(_gn(x), L2_conv_w3, L2_conv_w1, L2_conv_b, 4)
    x = x + _L3_conv_ref(_gn(x), L3_conv_w1, L3_conv_w2, L3_conv_gamma1, L3_conv_beta1, L3_conv_mean1, L3_conv_var1, L3_conv_gamma2, L3_conv_beta2, L3_conv_mean2, L3_conv_var2)
    return x


_drawn_inputs = setup_inputs


def setup_inputs(seed=0):
    import zlib

    import numpy as np

    out = dict(_drawn_inputs(seed))
    spreads = {'L0_conv_b_qkv': (0.0, 0.1),
     'L0_conv_lepe_b': (0.0, 0.1),
     'L0_conv_b_o': (0.0, 0.1),
     'L1_conv_gamma': (1.0, 0.2),
     'L1_conv_beta': (0.0, 0.1),
     'L1_conv_b_in': (0.0, 0.1),
     'L1_conv_b_ih': (0.0, 0.1),
     'L1_conv_b_hh': (0.0, 0.1),
     'L1_conv_b_out': (0.0, 0.1),
     'L3_conv_gamma1': (1.0, 0.2),
     'L3_conv_beta1': (0.0, 0.1),
     'L3_conv_gamma2': (1.0, 0.2),
     'L3_conv_beta2': (0.0, 0.315)}
    factors = {}
    for name, (base, spread) in spreads.items():
        noise = np.random.default_rng([zlib.crc32(name.encode()), seed]).standard_normal(out[name].shape)
        drawn = base * np.exp(spread * noise) if base else spread * noise
        out[name] = jnp.asarray(drawn.astype(out[name].dtype))
    for name, factor in factors.items():
        out[name] = (out[name] * factor).astype(out[name].dtype)
    return out
```

```python
import concourse.bass as bass
from concourse import mybir
from contextlib import ExitStack

F32 = mybir.dt.float32
U32 = mybir.dt.uint32
ACT = mybir.ActivationFunctionType
ALU = mybir.AluOpType
AXX = mybir.AxisListType.X

B, C, H, W = 8, 128, 56, 56
HW = H * W
ROWS = 8
BLK = ROWS * W
NBLK = H // ROWS
GROUP = 4
GN_EPS = 1e-5
NWIN = 7
WIN = H // NWIN
P2 = NWIN * NWIN
W2 = WIN * WIN
HEADS = 8
HD = C // HEADS
TOPK = 4
KEYS = TOPK * W2
PAIRS = HEADS // 2
QSCALE = float(C) ** -0.5
RIN, RH = 256, 512
NI, NH = RIN // 128, RH // 128
SEG = 16
L = HW // SEG
WARM = 64
COLS = B * SEG
PAD = WARM
HANDOVER_TOL = 2.0 ** -17
PW = WARM // 2
PM = L // 2
BN_EPS = 1e-5
BN_STEPS = 23


GN_DVE, GN_PE = 11, 2


def rsqrt_vector(e, r, v, tmp, done, d0):
    e.wait_ge(done, d0)
    e.reciprocal(r, r).then_inc(done, 1)
    e.wait_ge(done, d0 + 1)
    e.tensor_tensor(tmp, v, r, ALU.mult).then_inc(done, 1)
    e.wait_ge(done, d0 + 2)
    e.tensor_tensor(tmp, tmp, r, ALU.mult).then_inc(done, 1)
    e.wait_ge(done, d0 + 3)
    e.tensor_scalar(tmp, tmp, -0.5, 1.5, ALU.mult, ALU.add).then_inc(done, 1)
    e.wait_ge(done, d0 + 4)
    e.tensor_tensor(r, r, tmp, ALU.mult).then_inc(done, 1)
    e.wait_ge(done, d0 + 5)


def rnn(nc, mk, a, X, bank, A, Bb, gn_tensor, gn_vector, gn_scalar, x1_dram, s_gd, passed):
    CH = 2 * COLS
    with ExitStack() as ctx:
        sb, _, sem = mk(ctx)
        w_in = sb("w_in", [C, RIN])
        w_ih = sb("w_ih", [128, NI, RH])
        w_hh = sb("w_hh", [128, NH, RH])
        w_out = sb("w_out", [128, NH, C])
        vecs = sb("vecs", [C, 3])
        b_in = sb("b_in", [128, NI])
        bg = sb("bg", [128, 2, NH])
        ones = sb("ones", [128, 1])
        e1, e2, mu = sb("e1", [C, B]), sb("e2", [C, B]), sb("mu", [C, 4])
        A2 = sb("A2", [C, B, SEG])
        B2 = sb("B2", [C, B, SEG])
        mvp = sb("mvp", [C, B, 2])
        xa = sb("xa", [C, 2, 2, COLS])
        tz = sb("tz", [128, 2, NI, CH])
        inp = sb("inp", [128, 2, NI, CH])
        h = sb("h", [128, 4, NH, COLS])
        start = sb("start", [128, NH, COLS])
        okc = sb("okc", [128, 2])
        flag = sb("flag", [1, 1], U32)
        s_w = sem("rnn_weights_loaded")
        s_bn = sem("batchnorm_steps")
        s_bnr = sem("batchnorm_root")
        s_xm = sem("x_scaled")
        s_xa = sem("x_normalised")
        s_pre, s_tz, s_inp = sem("pre_product"), sem("pre_tanh"), sem("input_ready")
        s_g, s_h = sem("gates_product"), sem("state_ready")
        s_y, s_yd = sem("y_product"), sem("y_added")
        s_seed = sem("start_states")
        s_ver, s_verp, s_flag = sem("verify_steps"), sem("verify_product"), sem("verdict_ready")
        s_rel = sem("x1_reloaded")
        mvi = a["_mv"]

        def xcols(tok, k=2):
            return X[:, bass.ds(tok, COLS * L)].rearrange("p (c l) -> p l c", l=L)[:, 0:k, :]

        def pre_product(pe, P, q):
            pe.wait_ge(s_xa, P + 1)
            pe.wait_ge(s_inp, P * 2 + 2)
            for i in range(NI):
                ins = pe.matmul(bank[4 + q][:, i * CH:(i + 1) * CH], w_in[:, i * 128:(i + 1) * 128],
                                xa[:, q].rearrange("p t c -> p (t c)"), start=True, stop=True)
            ins.then_inc(s_pre, 1)

        def y_product(pe, Y, q):
            pe.wait_ge(s_yd, Y + 1)
            for k in range(NH):
                ins = pe.matmul(bank[6 + q][:, 0:CH], w_out[:, k, :], h[:, 2 * q:2 * q + 2, k, :],
                                start=(k == 0), stop=(k == NH - 1))
            ins.then_inc(s_y, 1)

        def tensor_pair(pe, P, q, y=None, more=True, seed=None):
            if more:
                pre_product(pe, P + 1, 1 - q)
            pe.wait_ge(s_inp, P * 2 + 6)
            if seed is not None:
                pe.wait_ge(s_seed, seed)
            for tt in range(2):
                prev = (2 * q + tt - 1) % 4
                for m in range(NH):
                    if m == 0:
                        pe.wait_ge(s_h, P * 8 + tt * 4 + 1)
                    for i in range(NI):
                        pe.matmul(bank[m][:, 0:COLS], w_ih[:, i, m * 128:(m + 1) * 128],
                                  inp[:, q, i, tt * COLS:(tt + 1) * COLS], start=(i == 0), stop=False)
                    for k in range(NH):
                        if m == 0:
                            pe.wait_ge(s_h, P * 8 + tt * 4 + k + 1)
                        ins = pe.matmul(bank[m][:, 0:COLS], w_hh[:, k, m * 128:(m + 1) * 128], h[:, prev, k, :],
                                        start=False, stop=(k == NH - 1))
                    ins.then_inc(s_g, 1)
                if tt == 0 and y is not None:
                    y_product(pe, y, 1 - q)

        def pre_tanh(act, P, q):
            act.wait_ge(s_pre, P + 3)
            act.wait_ge(s_inp, P * 2 + 2)
            for i in range(NI):
                act.activation(tz[:, q, i, :], bank[4 + q][:, i * CH:(i + 1) * CH], ACT.Tanh, bias=b_in[:, i:i + 1])\
                    .then_inc(s_tz, 1)

        def scalar_pair(act, P, q, more=True):
            if more:
                pre_tanh(act, P + 1, 1 - q)
            for tt in range(2):
                for m in range(NH):
                    act.wait_ge(s_g, P * 8 + tt * 4 + m + 17)
                    act.activation(h[:, 2 * q + tt, m, :], bank[m][:, 0:COLS], ACT.Tanh, bias=bg[:, 0, m:m + 1])\
                        .then_inc(s_h, 1)

        def normalise(dve, P, q, tok):
            dve.wait_ge(s_pre, P + 1)
            dve.tensor_tensor(xa[:, q], xcols(tok), A2[:].rearrange("p n s -> p (n s)").unsqueeze(1)
                              .to_broadcast([C, 2, COLS]), ALU.mult).then_inc(s_xm, 1)
            dve.wait_ge(s_xm, P + 1)
            dve.tensor_tensor(xa[:, q], xa[:, q], B2[:].rearrange("p n s -> p (n s)").unsqueeze(1)
                              .to_broadcast([C, 2, COLS]), ALU.add).then_inc(s_xa, 1)

        def shrink(dve, P, q):
            dve.wait_ge(s_g, P * 8 + 8)
            dve.wait_ge(s_tz, P * 2 + 2)
            for i in range(NI):
                dve.scalar_tensor_tensor(inp[:, q, i, :], bank[4 + q][:, i * CH:(i + 1) * CH], b_in[:, i:i + 1],
                                         tz[:, q, i, :], ALU.add, ALU.subtract).then_inc(s_inp, 1)

        def add_y(dve, Y, q, tok):
            dve.wait_ge(s_y, Y + 1)
            dve.scalar_tensor_tensor(xcols(tok), bank[6 + q][:, 0:CH].rearrange("p (t c) -> p t c", t=2), vecs[:, 2:3],
                                     xcols(tok), ALU.add, ALU.add).then_inc(s_yd, 1)

        def vector_pair(dve, P, q, tok, y=None, more=2):
            if more > 1:
                normalise(dve, P + 2, q, tok + 4)
            if more > 0:
                shrink(dve, P + 1, 1 - q)
            if y is not None:
                add_y(dve, y, 1 - q, tok - 2)

        PA = PW + PM
        RND, RNDW = PA // 2, PW // 2

        def run(e, first, P0, Y0, tok0, warm, seed, lead, body, tail):
            lead()
            if warm:
                with e.Fori(0, warm) as k:
                    body(k, False, False, None, False)
            body(warm, False, True, seed, False)
            with e.Fori(warm + 1, warm + PM // 2 - 1) as k:
                body(k, True, True, None, False)
            body(warm + PM // 2 - 1, True, True, None, True)
            tail(warm + PM // 2 - 1)

        def run_tensor(pe, P0, Y0, warm, seed):
            def body(k, y0, y1, sd, last):
                P = P0 + k * 2
                Y = Y0 + k * 2 - 2 * warm
                tensor_pair(pe, P, 0, Y - 1 if y0 else None, True, sd)
                tensor_pair(pe, P + 1, 1, Y if y1 else None, not last)

            def tail(k):
                pe.wait_ge(s_h, (P0 + 2 * k + 2) * 8 + 4)
                y_product(pe, Y0 + 2 * k - 2 * warm + 1, 1)
            run(pe, None, P0, Y0, None, warm, seed, lambda: pre_product(pe, P0, 0), body, tail)

        def run_scalar(act, P0, Y0, warm):
            def body(k, y0, y1, sd, last):
                P = P0 + k * 2
                scalar_pair(act, P, 0)
                scalar_pair(act, P + 1, 1, not last)
            run(act, None, P0, Y0, None, warm, None, lambda: pre_tanh(act, P0, 0), body, lambda k: None)

        def run_vector(dve, P0, Y0, warm, tok0, at_seed):
            def lead():
                normalise(dve, P0, 0, tok0)
                normalise(dve, P0 + 1, 1, tok0 + 2)
                shrink(dve, P0, 0)

            def body(k, y0, y1, sd, last):
                P = P0 + k * 2
                Y = Y0 + k * 2 - 2 * warm
                tok = tok0 + k * 4
                if sd and at_seed:
                    at_seed()
                vector_pair(dve, P, 0, tok, Y - 1 if y0 else None, 1 if last else 2)
                vector_pair(dve, P + 1, 1, tok + 2, Y if y1 else None, 0 if last else 2)

            def tail(k):
                add_y(dve, Y0 + 2 * k - 2 * warm + 1, 1, tok0 + 4 * k + 2)
            run(dve, None, P0, Y0, None, warm, 1, lead, body, tail)

        SEEDS, NWL = 2, 10
        hs = h[:].rearrange("p t k (n s) -> p t k n s", s=SEG)
        st4 = start[:].rearrange("p k (n s) -> p k n s", s=SEG)

        with nc.Block() as block:
            @block.sync
            def _(sp):
                for dst, src in ((w_in[:], a["w_in"]), (w_ih[:], a["w_ih"]), (w_hh[:], a["w_hh"]), (w_out[:], a["w_out"]),
                                 (vecs[:, 0:1], a["gamma"]), (vecs[:, 1:2], a["beta"]), (vecs[:, 2:3], a["b_out"]),
                                 (b_in[:], a["b_in"]), (bg[:, 0, :], a["b_ih"]), (bg[:, 1, :], a["b_hh"])):
                    sp.dma_start(dst, src, allow_slow_non_contiguous=True).then_inc(s_w, 16)
                sp.wait_ge(s_flag, 1)
                bad = sp.value_load(flag[0:1, 0:1], min_val=0, max_val=1)
                with sp.If(bad > 0):
                    with sp.Fori(0, SEG - 1) as r:
                        sp.wait_ge(s_yd, r * PM + PM + 2)
                        passed(sp)
                        sp.dma_start(X[:, PAD:PAD + B * HW].rearrange("p (n k) -> p n k", n=B),
                                     x1_dram.rearrange("n c k -> c n k")).then_inc(s_rel, 16)

            @block.gpsimd
            def _(pool):
                pool.sem_inc(s_g, 16)
                pool.sem_inc(s_pre, 2)
                pool.sem_inc(s_inp, 4)
                pool.sem_inc(s_yd, 2)
                pool.memset(ones[:], 1.0).then_inc(s_verp, 1)

            @block.scalar
            def _(act):
                gn_scalar(act, 1)
                act.wait_ge(s_bn, 11)
                act.activation(mu[:, 2:3], mu[:, 1:2], ACT.Sqrt).then_inc(s_bnr, 1)
                act.wait_ge(s_w, 16 * NWL)
                act.wait_ge(s_bn, BN_STEPS)
                run_scalar(act, 0, 0, RNDW)
                act.wait_ge(s_flag, 1)
                bad = act.value_load(flag[0:1, 0:1], min_val=0, max_val=1)
                with act.If(bad > 0):
                    with act.Fori(0, SEG - 1) as r:
                        run_scalar(act, r * PM + PA, r * PM + PM, 0)

            @block.vector
            def _(dve):
                gn_vector(dve, 1)
                dve.wait_ge(s_w, 16 * NWL)
                n_bn = [0]

                def link(ins):
                    n_bn[0] += 1
                    ins.then_inc(s_bn, 1)
                    dve.wait_ge(s_bn, n_bn[0])
                link(dve.tensor_tensor(e1[:], A[:], mvi[:, :, 0], ALU.mult))
                link(dve.tensor_tensor(e1[:], e1[:], Bb[:], ALU.add))
                link(dve.tensor_reduce(mu[:, 0:1], e1[:], AXX, ALU.add))
                link(dve.tensor_scalar(mu[:, 0:1], mu[:, 0:1], 1.0 / B, None, ALU.mult))
                link(dve.tensor_scalar(e1[:], e1[:], mu[:, 0:1], None, ALU.subtract))
                link(dve.tensor_tensor(e1[:], e1[:], e1[:], ALU.mult))
                link(dve.tensor_tensor(e2[:], A[:], A[:], ALU.mult))
                link(dve.tensor_tensor(e2[:], e2[:], mvi[:, :, 1], ALU.mult))
                link(dve.tensor_tensor(e2[:], e2[:], e1[:], ALU.add))
                link(dve.tensor_reduce(mu[:, 1:2], e2[:], AXX, ALU.add))
                link(dve.tensor_scalar(mu[:, 1:2], mu[:, 1:2], 1.0 / B, BN_EPS, ALU.mult, ALU.add))
                dve.wait_ge(s_bnr, 1)
                rsqrt_vector(dve, mu[:, 2:3], mu[:, 1:2], mu[:, 3:4], s_bn, n_bn[0])
                n_bn[0] += 5
                link(dve.tensor_tensor(mu[:, 2:3], mu[:, 2:3], vecs[:, 0:1], ALU.mult))
                link(dve.tensor_scalar(e1[:], A[:], mu[:, 2:3], None, ALU.mult))
                link(dve.tensor_scalar(e2[:], Bb[:], mu[:, 0:1], mu[:, 2:3], ALU.subtract, ALU.mult))
                link(dve.tensor_scalar(e2[:], e2[:], vecs[:, 1:2], None, ALU.add))
                link(dve.tensor_copy(A2[:], e1[:].unsqueeze(2).to_broadcast([C, B, SEG])))
                link(dve.tensor_copy(B2[:], e2[:].unsqueeze(2).to_broadcast([C, B, SEG])))
                link(dve.tensor_tensor(bg[:, 0, :], bg[:, 0, :], bg[:, 1, :], ALU.add))
                assert n_bn[0] == BN_STEPS
                dve.memset(h[:, 3], 0.0).then_inc(s_h, NH)

                def at_seed():
                    dve.wait_ge(s_h, 4 + NH * WARM)
                    dve.tensor_copy(start[:], h[:, 3]).then_inc(s_seed, 1)
                    dve.wait_ge(s_seed, 1)
                    dve.memset(hs[:, 3, :, :, 0:1], 0.0).then_inc(s_seed, 1)

                run_vector(dve, 0, 0, RNDW, 0, at_seed)
                d = inp[:].rearrange("p a b c -> p (a b c)")[:, 0:NH * B * (SEG - 1)]
                d4 = d.rearrange("p (k n s) -> p k n s", k=NH, n=B)
                dve.wait_ge(s_h, 4 + NH * 2 * PA)
                dve.wait_ge(s_g, 16 + NH * 2 * PA)
                for k in range(NH):
                    ins = dve.tensor_tensor(d4[:, k], hs[:, 3, k, :, 0:SEG - 1], st4[:, k, :, 1:SEG], ALU.subtract)
                ins.then_inc(s_ver, 1)
                dve.wait_ge(s_ver, 1)
                dve.tensor_tensor(d, d, d, ALU.mult).then_inc(s_ver, 1)
                dve.wait_ge(s_ver, 2)
                dve.tensor_scalar(d, d, HANDOVER_TOL ** 2, None, ALU.is_le).then_inc(s_ver, 1)
                dve.wait_ge(s_ver, 3)
                dve.tensor_reduce(okc[:, 0:1], d, AXX, ALU.min).then_inc(s_ver, 1)
                dve.wait_ge(s_verp, 2)
                dve.tensor_scalar(flag[:], bank[0][0:1, 0:1], 127.5, None, ALU.is_lt).then_inc(s_flag, 1)
                dve.wait_ge(s_flag, 1)
                bad = dve.value_load(flag[0:1, 0:1], min_val=0, max_val=1)
                with dve.If(bad > 0):
                    with dve.Fori(0, SEG - 1) as r:
                        dve.wait_ge(s_h, r * (NH * L) + 4 + NH * 2 * PA)
                        dve.wait_ge(s_yd, r * PM + PM + 2)
                        dve.tensor_copy(start[:], h[:, 3]).then_inc(s_seed, 1)
                        dve.wait_ge(s_seed, r * 3 + 3)
                        dve.tensor_copy(h[:, 3, :, 1:COLS], start[:, :, 0:COLS - 1]).then_inc(s_seed, 1)
                        dve.wait_ge(s_seed, r * 3 + 4)
                        dve.memset(hs[:, 3, :, :, 0:1], 0.0).then_inc(s_seed, 1)
                        dve.wait_ge(s_rel, r * 16 + 16)
                        run_vector(dve, r * PM + PA, r * PM + PM, 0, PAD, None)

            @block.tensor
            def _(pe):
                gn_tensor(pe, 1)
                pe.wait_ge(s_w, 16 * NWL)
                run_tensor(pe, 0, 0, RNDW, SEEDS)
                pe.wait_ge(s_ver, 4)
                pe.wait_ge(s_verp, 1)
                pe.matmul(bank[0][0:1, 0:1], okc[:, 0:1], ones[:], start=True, stop=True).then_inc(s_verp, 1)
                pe.wait_ge(s_flag, 1)
                bad = pe.value_load(flag[0:1, 0:1], min_val=0, max_val=1)
                with pe.If(bad > 0):
                    with pe.Fori(0, SEG - 1) as r:
                        run_tensor(pe, r * PM + PA, r * PM + PM, 0, r * 3 + 5)


def pad_blocks(b):
    return min(b + 1, NBLK - 1)


def masked_conv(nc, mk, a, X, bank, A, Bb, gn_tensor, gn_vector, gn_scalar, s_gd, bn, s_bst, s_mvw,
                image_stats, xblk, passed):
    with ExitStack() as ctx:
        sb, _, sem = mk(ctx)
        w3 = sb("w3", [C, 9, C])
        w1 = sb("w1", [C, C])
        on, off = sb("on_grid", [C, C]), sb("off_grid", [C, C])
        b2 = sb("b2", [C, C])
        bsum = sb("bsum", [C, 1])
        pad = sb("pad", [C, 2, H + 2, W + 2])
        s_w, s_wr, s_z = sem("conv_weights_loaded"), sem("conv_weights_masked"), sem("pad_zero")
        s_pad, s_cv, s_ev = sem("pad_ready"), sem("conv_product"), sem("conv_added")

        with nc.Block() as block:
            @block.sync
            def _(sp):
                for dst, src in ((w3[:], a["w3"]), (w1[:], a["w1"]), (on[:], a["on_grid"]), (off[:], a["off_grid"]),
                                 (b2[:], a["b2"])):
                    sp.dma_start(dst, src).then_inc(s_w, 16)

            @block.gpsimd
            def _(pool):
                pool.sem_inc(s_cv, 15)
                pool.sem_inc(s_ev, 8)
                pool.memset(pad[:], 0.0).then_inc(s_z, 1)

            @block.scalar
            def _(act):
                gn_scalar(act, 2)
                act.wait_ge(s_gd, 3 * GN_DVE)
                act.wait_ge(s_z, 1)
                with act.Fori(0, B // 2) as g:
                    for u in range(2):
                        n = g * 2 + u
                        act.wait_ge(s_cv, n * NBLK + 8)
                        for b in range(NBLK):
                            act.activation(pad[:, u, 1 + b * ROWS:1 + (b + 1) * ROWS, 1:1 + W],
                                           xblk(n, b).rearrange("p (r c) -> p r c", c=W), ACT.Identity,
                                           bias=Bb[:, bass.ds(n, 1)], scale=A[:, bass.ds(n, 1)]).then_inc(s_pad, 1)

            @block.vector
            def _(dve):
                with dve.Fori(0, B) as n:
                    dve.wait_ge(s_mvw, n + 2 * B)
                    passed(dve)
                    for b in range(NBLK):
                        ins = dve.bn_stats(bn[:, b, :], xblk(n, b))
                    ins.then_inc(s_bst, 1)
                    image_stats(dve, n, n + 2 * B)
                gn_vector(dve, 2)
                dve.wait_ge(s_w, 80)
                dve.tensor_tensor(w3[:], w3[:], on[:].unsqueeze(1).to_broadcast([C, 9, C]), ALU.mult).then_inc(s_wr, 1)
                dve.tensor_tensor(w1[:], w1[:], off[:], ALU.mult).then_inc(s_wr, 1)
                dve.wait_ge(s_wr, 2)
                dve.tensor_tensor(w3[:, 4, :], w3[:, 4, :], w1[:], ALU.add).then_inc(s_wr, 1)
                dve.tensor_reduce(bsum[:], b2[:], AXX, ALU.add).then_inc(s_wr, 1)
                dve.wait_ge(s_wr, 4)
                with dve.Fori(0, B) as n:
                    dve.wait_ge(s_mvw, n + 3 * B)
                    for b in range(NBLK):
                        dve.wait_ge(s_cv, n * NBLK + b + 16)
                        dve.scalar_tensor_tensor(xblk(n, b), bank[b][:, 0:BLK], bsum[:], xblk(n, b), ALU.add, ALU.add)\
                            .then_inc(s_ev, 1)
                        dve.wait_ge(s_ev, n * NBLK + b + 9)
                        passed(dve)
                        ins = dve.bn_stats(bn[:, b, :], xblk(n, b))
                    ins.then_inc(s_bst, 1)
                    image_stats(dve, n, n + 3 * B)

            @block.tensor
            def _(pe):
                gn_tensor(pe, 2)
                pe.wait_ge(s_wr, 4)
                with pe.Fori(0, B // 2) as g:
                    for u in range(2):
                        n = g * 2 + u
                        for b in range(NBLK):
                            pe.wait_ge(s_pad, n * NBLK + pad_blocks(b) + 1)
                            pe.wait_ge(s_ev, n * NBLK + b + 2)
                            for k in range(9):
                                dy, dx = divmod(k, 3)
                                ins = pe.matmul(bank[b][:, 0:BLK], w3[:, k, :],
                                                pad[:, u, b * ROWS + dy:b * ROWS + dy + ROWS, dx:dx + W],
                                                start=(k == 0), stop=(k == 8))
                            ins.then_inc(s_cv, 1)


def conv_pair(nc, mk, a, X, bank, A, Bb, gn_tensor, gn_vector, gn_scalar, xblk, passed, s_gd, out):
    with ExitStack() as ctx:
        sb, _, sem = mk(ctx)
        c1, c2 = sb("c1", [C, 9, C]), sb("c2", [C, 9, C])
        bnv = sb("bnv", [C, 8])
        sv = sb("sv", [C, 2])
        tv = sb("tv", [C, 2])
        root, tmp = sb("root", [C, 2]), sb("tmp", [C, 2])
        padz = sb("padz", [C, 2, H + 2, W + 2])
        padm = sb("padm", [C, H + 2, W + 2])
        res = sb("res", [C, 2, BLK])
        s_w, s_z = sem("pair_weights_loaded"), sem("pair_pads_zero")
        s_k, s_kr = sem("pair_bn_steps"), sem("pair_bn_root")
        s_pz, s_c1, s_m, s_c2 = sem("z_ready"), sem("conv1_product"), sem("mid_ready"), sem("conv2_product")
        s_r, s_rl, s_add, s_st = sem("residual_added"), sem("relu_done"), sem("x_added"), sem("stored")
        o = out.rearrange("n c h w -> n c (h w)")
        v4 = bnv[:].rearrange("p (j q) -> p j q", j=2)

        with nc.Block() as block:
            @block.sync
            def _(sp):
                for dst, src in ((c1[:], a["c1"]), (c2[:], a["c2"])) + tuple(
                        (bnv[:, i:i + 1], a[k]) for i, k in enumerate(("g1", "h1", "m1", "v1", "g2", "h2", "m2", "v2"))):
                    sp.dma_start(dst, src, allow_slow_non_contiguous=True).then_inc(s_w, 16)
                with sp.Fori(0, B) as n:
                    sp.wait_ge(s_add, n * NBLK + NBLK + 2)
                    passed(sp)
                    sp.dma_start(o[bass.ds(n, 1)].rearrange("u c k -> (u c) k"), X[:, bass.ds(PAD + n * HW, HW)])\
                        .then_inc(s_st, 16)
                sp.wait_ge(s_st, 16 * B)

            @block.gpsimd
            def _(pool):
                pool.sem_inc(s_c1, 8)
                pool.sem_inc(s_c2, 15)
                pool.sem_inc(s_m, 8)
                pool.sem_inc(s_r, 8)
                pool.sem_inc(s_rl, 2)
                pool.sem_inc(s_add, 2)
                pool.memset(padz[:], 0.0).then_inc(s_z, 1)
                pool.memset(padm[:], 0.0).then_inc(s_z, 1)

            @block.scalar
            def _(act):
                gn_scalar(act, 3)
                act.wait_ge(s_k, 1)
                act.activation(root[:], tmp[:], ACT.Sqrt).then_inc(s_kr, 1)
                act.wait_ge(s_gd, 4 * GN_DVE)
                act.wait_ge(s_k, 9)
                act.wait_ge(s_z, 2)

                def z_block(n, u, b):
                    act.activation(padz[:, u, 1 + b * ROWS:1 + (b + 1) * ROWS, 1:1 + W],
                                   xblk(n, b).rearrange("p (r c) -> p r c", c=W), ACT.Identity,
                                   bias=Bb[:, bass.ds(n, 1)], scale=A[:, bass.ds(n, 1)]).then_inc(s_pz, 1)

                for b in range(NBLK):
                    z_block(0, 0, b)

                def image(n, u, more):
                    for b in range(NBLK):
                        act.wait_ge(s_c1, n * NBLK + b + 9)
                        act.activation(padm[:, 1 + b * ROWS:1 + (b + 1) * ROWS, 1:1 + W],
                                       bank[b][:, 0:BLK].rearrange("p (r c) -> p r c", c=W), ACT.Relu,
                                       bias=tv[:, 0:1], scale=sv[:, 0:1]).then_inc(s_m, 1)
                    if more:
                        act.wait_ge(s_r, n * NBLK + 8)
                    for b in range(NBLK):
                        if more:
                            z_block(n + 1, 1 - u, b)
                        act.wait_ge(s_r, n * NBLK + b + 9)
                        act.activation(res[:, b % 2, :], res[:, b % 2, :], ACT.Relu, bias=tv[:, 1:2]).then_inc(s_rl, 1)

                with act.Fori(0, B // 2 - 1) as g:
                    image(g * 2, 0, True)
                    image(g * 2 + 1, 1, True)
                image(B - 2, 0, True)
                image(B - 1, 1, False)

            @block.vector
            def _(dve):
                gn_vector(dve, 3)
                dve.wait_ge(s_w, 160)
                dve.tensor_scalar(tmp[:], v4[:, :, 3], BN_EPS, None, ALU.add).then_inc(s_k, 1)
                dve.wait_ge(s_kr, 1)
                rsqrt_vector(dve, root[:], tmp[:], sv[:], s_k, 1)
                dve.tensor_tensor(sv[:], root[:], v4[:, :, 0], ALU.mult).then_inc(s_k, 1)
                dve.wait_ge(s_k, 7)
                dve.tensor_tensor(tmp[:], sv[:], v4[:, :, 2], ALU.mult).then_inc(s_k, 1)
                dve.wait_ge(s_k, 8)
                dve.tensor_tensor(tv[:], v4[:, :, 1], tmp[:], ALU.subtract).then_inc(s_k, 1)
                dve.wait_ge(s_k, 9)

                def add_x(n, b):
                    dve.wait_ge(s_rl, n * NBLK + b + 3)
                    dve.tensor_tensor(xblk(n, b), xblk(n, b), res[:, b % 2, :], ALU.add).then_inc(s_add, 1)

                with dve.Fori(0, B // 2) as g:
                    for u in range(2):
                        n = g * 2 + u
                        for b in range(NBLK):
                            dve.wait_ge(s_c2, n * NBLK + b + 16)
                            dve.wait_ge(s_add, n * NBLK + b + (1 if b else 2))
                            dve.scalar_tensor_tensor(
                                res[:, b % 2, :].rearrange("p (r c) -> p r c", c=W),
                                bank[b][:, 0:BLK].rearrange("p (r c) -> p r c", c=W), sv[:, 1:2],
                                padz[:, u, 1 + b * ROWS:1 + (b + 1) * ROWS, 1:1 + W], ALU.mult, ALU.add).then_inc(s_r, 1)
                            if b:
                                add_x(n, b - 1)
                        add_x(n, NBLK - 1)

            @block.tensor
            def _(pe):
                gn_tensor(pe, 3)
                pe.wait_ge(s_w, 160)

                def conv(b, w, src):
                    for k in range(9):
                        dy, dx = divmod(k, 3)
                        ins = pe.matmul(bank[b][:, 0:BLK], w[:, k, :],
                                        src[:, b * ROWS + dy:b * ROWS + dy + ROWS, dx:dx + W],
                                        start=(k == 0), stop=(k == 8))
                    return ins

                with pe.Fori(0, B // 2) as g:
                    for u in range(2):
                        n = g * 2 + u
                        for b in range(NBLK):
                            pe.wait_ge(s_pz, n * NBLK + pad_blocks(b) + 1)
                            pe.wait_ge(s_r, n * NBLK + b + 2)
                            conv(b, c1, padz[:, u]).then_inc(s_c1, 1)
                        for b in range(NBLK):
                            pe.wait_ge(s_m, n * NBLK + pad_blocks(b) + 9)
                            conv(b, c2, padm[:]).then_inc(s_c2, 1)


def program(nc, a, out, last_stage=4):
    root = ExitStack()
    with root:
        def mk(ctx):
            def sb(n, s, d=F32):
                return ctx.enter_context(nc.sbuf_tensor(n, s, d))

            def ps(n, s, d=F32):
                return ctx.enter_context(nc.psum_tensor(n, s, d))

            def sem(n):
                return ctx.enter_context(nc.semaphore(n))
            return sb, ps, sem

        sb, psm, sem = mk(root)
        x_in = a["x"].rearrange("n c h w -> n c (h w)")
        x1_dram = nc.dram_tensor("x1_backup", [B, C, HW], F32, kind="Internal").ap()
        v_dram = nc.dram_tensor("v_windows", [B * P2, W2, C], F32, kind="Internal").ap()

        s_root = sem("groupnorm_root")
        s_passed = sem("waits_passed")
        s_w4 = sem("group_matrix_loaded")
        X = sb("X", [C, PAD + B * HW + L])
        bank = [psm(f"bank{i}", [128, 512]) for i in range(8)]
        t = {k: sb(k, [C, B]) for k in ("gn_gm", "gn_d", "gn_v")}
        t["group4"] = sb("group4", [C, C])
        mv = sb("mv", [C, B, 2])
        A = sb("A", [C, B])
        Bb = sb("Bb", [C, B])
        bn = sb("bn", [C, NBLK, 6])
        mv1 = sb("mv1", [C, 2])
        gm, gd, gv, group4 = t["gn_gm"], t["gn_d"], t["gn_v"], t["group4"]
        s_gd = sem("groupnorm_vector")
        s_gp = sem("groupnorm_tensor")
        s_mv1 = sem("image_aggregated")
        s_bst = sem("block_stats")
        s_mvw = sem("image_stats")

        def passed(e):
            e.sem_inc(s_passed, 1)

        def gn_tensor(e, g):
            e.wait_ge(s_mvw, B * (g + 1))
            e.wait_ge(s_w4, 16)
            e.matmul(bank[7][:, 0:B], group4[:], mv[:, :, 0], start=True, stop=True).then_inc(s_gp, 1)
            e.wait_ge(s_gd, GN_DVE * g + 4)
            e.matmul(bank[7][:, 0:B], group4[:], gv[:], start=True, stop=True).then_inc(s_gp, 1)

        def gn_vector(e, g):
            d0 = GN_DVE * g
            e.wait_ge(s_mvw, B * (g + 1))
            e.wait_ge(s_gp, GN_PE * g + 1)
            e.tensor_copy(gm[:], bank[7][:, 0:B]).then_inc(s_gd, 1)
            e.wait_ge(s_gd, d0 + 1)
            e.tensor_tensor(gd[:], mv[:, :, 0], gm[:], ALU.subtract).then_inc(s_gd, 1)
            e.wait_ge(s_gd, d0 + 2)
            e.tensor_tensor(gv[:], gd[:], gd[:], ALU.mult).then_inc(s_gd, 1)
            e.wait_ge(s_gd, d0 + 3)
            e.tensor_tensor(gv[:], gv[:], mv[:, :, 1], ALU.add).then_inc(s_gd, 1)
            e.wait_ge(s_gp, GN_PE * g + 2)
            e.tensor_scalar(gv[:], bank[7][:, 0:B], GN_EPS, None, ALU.add).then_inc(s_gd, 1)
            e.wait_ge(s_root, g + 1)
            rsqrt_vector(e, A[:], gv[:], gd[:], s_gd, d0 + 5)
            e.scalar_tensor_tensor(Bb[:], gm[:], -1.0, A[:], ALU.mult, ALU.mult).then_inc(s_gd, 1)
            e.wait_ge(s_gd, d0 + 11)

        def gn_scalar(e, g):
            e.wait_ge(s_gd, GN_DVE * g + 5)
            e.activation(A[:], gv[:], ACT.Sqrt).then_inc(s_root, 1)

        def image_stats(e, n, done):
            e.wait_ge(s_bst, done + 1)
            passed(e)
            e.bn_aggr(mv1[:], bn[:].rearrange("p b s -> p (b s)")).then_inc(s_mv1, 1)
            e.wait_ge(s_mv1, done + 1)
            e.tensor_copy(mv[:, bass.ds(n, 1), :], mv1[:].unsqueeze(1)).then_inc(s_mvw, 1)

        def xblk(n, b):
            return X[:, bass.ds(PAD + n * HW + b * BLK, BLK)]

        with ExitStack() as c0:
            sb, _, sem = mk(c0)
            s_ldx = [sem(f"x_loaded{n}") for n in range(B)]
            s_w = sem("weights_loaded")
            s_padz = sem("pads_zero")
            s_xb = sem("xb_ready")
            s_pq, s_pk, s_pv, s_pV = sem("q_product"), sem("k_product"), sem("v_product"), sem("vtok_product")
            s_q, s_k, s_v, s_V = sem("q_ready"), sem("k_ready"), sem("v_ready"), sem("vtok_ready")
            s_vst = [sem("v_stored_even"), sem("v_stored_odd")]
            s_qs = sem("window_sums")
            s_lg = sem("logits_product")
            s_tk = sem("topk_steps")
            s_row = sem("routes_ready")
            s_kg, s_Q, s_vg = sem("keys_gathered"), sem("queries_spread"), [sem(f"values_gathered{i}") for i in range(3)]
            s_S = sem("scores_product")
            s_mx, s_ex, s_rd = sem("score_max"), sem("exp_done"), sem("sum_reciprocal")
            s_nP = sem("probs_normalised")
            s_T, s_Tc = sem("probs_turned"), sem("turned_copied")
            s_O, s_o, s_om = sem("attended_product"), sem("attended_ready"), sem("attended_half")
            s_out, s_ev = sem("out_product"), sem("out_added")
            s_cst, s_cp = sem("consts_ready"), sem("consts_product")
            s_bak = sem("x1_saved")

            w_qkv = sb("w_qkv", [C, 3 * C])
            w_o = sb("w_o", [C, C])
            lw = sb("lw", [C, 9])
            w_tap = sb("w_tap", [C, 9, C])
            vec = sb("vec", [C, 6])
            cb = sb("cb", [C, 2])
            eo = sb("eo", [C, 2])
            hmask = sb("hmask", [C, HEADS, W2])
            ident = sb("ident", [C, C])
            qT = sb("qT", [C, HW])
            kT = sb("kT", [C, HW])
            oT = sb("oT", [C, HW])
            vpad = sb("vpad", [C, H + 2, W + 2])
            xb = sb("xb", [C, 2, BLK])
            vst = sb("vst", [C, 2, 4, C])
            qs = sb("qs", [C, P2])
            ks = sb("ks", [C, P2])
            lg = sb("lg", [P2, P2])
            m8 = sb("m8", [P2, 8])
            ix = sb("ix", [P2, 8], U32)
            row = sb("row", [1, P2 * TOPK], U32)
            Qs = sb("Qs", [C, 2, HEADS * W2])
            kg = sb("kg", [C, 2, KEYS])
            vg = sb("vg", [C, 3, 2, C])
            Pr = sb("Pr", [C, 2, PAIRS, KEYS])
            PT = sb("PT", [C, 2, PAIRS * 2 * C])
            nmx = sb("nmx", [C, 2, PAIRS])
            den = sb("den", [C, 2, PAIRS])
            rden = sb("rden", [C, 2, PAIRS])
            oh = sb("oh", [C, W2])

            NW = 10
            STORED = 32

            with nc.Block() as block:
                @block.sync
                def _(sp):
                    sp.dma_start(group4[:], a["group4"]).then_inc(s_w4, 16)
                    for n in range(B):
                        sp.dma_start(X[:, PAD + n * HW:PAD + (n + 1) * HW], x_in[n]).then_inc(s_ldx[n], 16)
                    for dst, src in ((w_qkv[:], a["w_qkv"]), (w_o[:], a["w_o"]), (lw[:], a["lepe_w"]),
                                     (vec[:, 0:3], a["b_qkv"]), (vec[:, 3:4], a["lepe_b"]), (vec[:, 4:5], a["b_o"]),
                                     (eo[:], a["even_odd"]), (hmask[:, :, 0], a["head_mask"]),
                                     (ident[:], a["ident"]),
                                     (vec[:, 5:6], a["b_q"])):
                        sp.dma_start(dst, src, allow_slow_non_contiguous=True).then_inc(s_w, 16)
                    with sp.Fori(0, B) as n:
                        for b in range(NBLK):
                            sp.wait_ge(s_V, n * NBLK + b + 2)
                            passed(sp)
                            sp.dma_start(v_dram[bass.ds(n * P2 + b * NWIN, 6)].rearrange("(i u) k c -> (u k) i c", u=2),
                                         vst[:, b % 2, 0:3, :]).then_inc(s_vst[b % 2], 16)
                            sp.dma_start(v_dram[bass.ds(n * P2 + b * NWIN + 6, 1)].rearrange("u k c -> (u k) c"),
                                         vst[0:64, b % 2, 3, :]).then_inc(s_vst[b % 2], 16)
                        sp.wait_ge(s_tk, n * 3 + 4)
                        passed(sp)
                        sp.wait_ge(s_kg, (n * P2) + 1)
                        passed(sp)
                        sp.dma_start(row[0:1, :], ix[:, 0:TOPK]).then_inc(s_row, 16)
                        sp.wait_ge(s_vst[0], n * (STORED * 4) + STORED * 4 + 16)
                        passed(sp)
                        sp.wait_ge(s_vst[1], n * (STORED * 3) + STORED * 3 + 16)
                        passed(sp)
                        sp.wait_ge(s_row, n * 16 + 32)
                        passed(sp)
                        sp.wait_ge(s_O, n * P2 + 3)
                        passed(sp)

                        def gather(w, slot):
                            idx = [sp.value_load(row[0:1, bass.ds(w * TOPK + r, 1)], min_val=0, max_val=P2 - 1)
                                   for r in range(TOPK)]
                            sp.wait_ge(s_O, n * P2 + w + 1)
                            passed(sp)
                            for r in range(TOPK):
                                sp.dma_start(vg[64 * (r % 2):64 * (r % 2) + 64, slot, r // 2, :],
                                             v_dram[bass.ds(idx[r] + n * P2, 1)].rearrange("u k c -> (u k) c"))\
                                    .then_inc(s_vg[slot], 16)

                        with sp.Fori(0, P2 // 3) as k:
                            for i in range(3):
                                gather(k * 3 + i, i)
                        gather(P2 - 1, (P2 - 1) % 3)
                        sp.wait_ge(s_ev, n * NBLK + NBLK + 1)
                        passed(sp)
                        sp.dma_start(x1_dram[bass.ds(n, 1)].rearrange("u c k -> (u c) k"),
                                     X[:, bass.ds(PAD + n * HW, HW)]).then_inc(s_bak, 16)
                    sp.wait_ge(s_bak, 16 * B)

                @block.gpsimd
                def _(pool):
                    pool.memset(X[:, 0:PAD], 0.0).then_inc(s_padz, 1)
                    pool.memset(vpad[:], 0.0).then_inc(s_padz, 1)
                    for sm in (s_xb, s_V, s_tk, s_kg, s_S, s_O, s_T, s_ev, s_nP, s_ex, s_o, s_Tc, s_mx, s_Q):
                        pool.sem_inc(sm, 1)
                    pool.sem_inc(s_O, 2)
                    pool.sem_inc(s_pV, 2)
                    pool.sem_inc(s_vst[0], 16)
                    pool.sem_inc(s_vst[1], 16)
                    pool.sem_inc(s_row, 16)
                    pool.wait_ge(s_cst, 12)
                    with pool.Fori(0, B) as n:
                        pool.wait_ge(s_row, n * 16 + 32)
                        pool.wait_ge(s_q, n * NBLK + NBLK)
                        pool.wait_ge(s_k, n * NBLK + NBLK)
                        passed(pool)

                        def window(w, par):
                            if not isinstance(w, int):
                                pool.wait_ge(s_S, n * P2 + w)
                            passed(pool)
                            for r in range(TOPK):
                                i = pool.value_load(row[0:1, bass.ds(w * TOPK + r, 1)], min_val=0, max_val=P2 - 1)
                                ins = pool.tensor_copy(kg[:, par, r * W2:(r + 1) * W2], kT[:, bass.ds(i * W2, W2)])
                            ins.then_inc(s_kg, 1)
                            pool.tensor_tensor(Qs[:, par, :].rearrange("p (h k) -> p h k", h=HEADS),
                                               qT[:, bass.ds(w * W2, W2)].unsqueeze(1).to_broadcast([C, HEADS, W2]),
                                               hmask[:], ALU.mult).then_inc(s_Q, 1)

                        pool.wait_ge(s_S, n * P2 + 1)
                        passed(pool)
                        window(0, 0)
                        with pool.Fori(0, (P2 - 1) // 2) as k:
                            window(k * 2 + 1, 1)
                            window(k * 2 + 2, 0)
                    pool.wait_ge(s_S, B * P2 + 1)

                @block.scalar
                def _(act):
                    def evac_act(act, n, b):
                        par = b % 2
                        act.wait_ge(s_pq, n * NBLK + b + 1)
                        act.wait_ge(s_Q, n * P2 + 1)
                        act.activation(qT[:, b * BLK:(b + 1) * BLK], bank[4 * par][:, 0:BLK], ACT.Identity,
                                       bias=vec[:, 5:6], scale=QSCALE).then_inc(s_q, 1)
                        act.wait_ge(s_pV, n * NBLK + b + 3)
                        act.wait_ge(s_vst[par], n * (STORED * (4 - par)) + STORED * (b // 2) + 16)
                        act.activation(vst[:, par, 0:3, :], bank[4 * par + 3][:, 0:384].rearrange("p (i c) -> p i c", c=C),
                                       ACT.Copy)
                        act.activation(vst[0:64, par, 3, :], bank[4 * par + 3][0:64, 384:512], ACT.Copy).then_inc(s_V, 1)

                    gn_scalar(act, 0)
                    act.wait_ge(s_cst, 12)
                    act.wait_ge(s_gd, GN_DVE)
                    with act.Fori(0, B) as n:
                        for b in range(NBLK):
                            act.wait_ge(s_pV, n * NBLK + b + 1)
                            xw = xblk(n, b).rearrange("p (r w c) -> p w r c", r=ROWS, c=WIN)
                            act.activation(xb[:, b % 2, :].rearrange("p (w r c) -> p w r c", r=ROWS, c=WIN), xw,
                                           ACT.Identity, bias=Bb[:, bass.ds(n, 1)], scale=A[:, bass.ds(n, 1)])\
                                .then_inc(s_xb, 1)
                            if b >= 1:
                                evac_act(act, n, b - 1)
                        evac_act(act, n, NBLK - 1)

                        def exps(w, par):
                            if not isinstance(w, int):
                                act.wait_ge(s_T, n * P2 + w)
                            for j in range(PAIRS):
                                act.wait_ge(s_mx, (n * P2 + w) * PAIRS + j + 2)
                                act.activation(Pr[:, par, j, :], bank[j][:, 0:KEYS], ACT.Exp,
                                               bias=nmx[:, par, j:j + 1], accum_out=den[:, par, j:j + 1])\
                                    .then_inc(s_ex, 1)

                        def turned(w, par):
                            act.wait_ge(s_T, n * P2 + w + 2)
                            act.wait_ge(s_O, n * P2 + w + 2)
                            act.activation(PT[:, par, 0:512], bank[4][:], ACT.Copy).then_inc(s_Tc, 1)

                        act.wait_ge(s_T, n * P2 + 1)
                        exps(0, 0)
                        with act.Fori(0, (P2 - 1) // 2) as k:
                            exps(k * 2 + 1, 1)
                            turned(k * 2, 0)
                            exps(k * 2 + 2, 0)
                            turned(k * 2 + 1, 1)
                        turned(P2 - 1, 0)

                @block.vector
                def _(dve):
                    for n in range(B):
                        dve.wait_ge(s_ldx[n], 16)
                        if n:
                            dve.wait_ge(s_mvw, n)
                        for b in range(NBLK):
                            ins = dve.bn_stats(bn[:, b, :], X[:, PAD + n * HW + b * BLK:PAD + n * HW + (b + 1) * BLK])
                        ins.then_inc(s_bst, 1)
                        image_stats(dve, n, n)
                    dve.wait_ge(s_mvw, B)
                    dve.wait_ge(s_w, 16 * NW)
                    dve.tensor_scalar(vec[:, 5:6], vec[:, 5:6], QSCALE, None, ALU.mult).then_inc(s_cst, 1)
                    dve.tensor_copy(hmask[:, :, 1:W2], hmask[:, :, 0:1].to_broadcast([C, HEADS, W2 - 1]))\
                        .then_inc(s_cst, 1)
                    for k in range(9):
                        dve.tensor_scalar(w_tap[:, k, :], w_o[:], lw[:, k:k + 1], None, ALU.mult).then_inc(s_cst, 1)
                    dve.tensor_tensor(cb[:, 0:1], vec[:, 2:3], vec[:, 3:4], ALU.add).then_inc(s_cst, 1)
                    gn_vector(dve, 0)
                    dve.wait_ge(s_cp, 1)
                    dve.tensor_tensor(cb[:, 1:2], bank[1][:, 0:1], vec[:, 4:5], ALU.add).then_inc(s_cst, 1)
                    dve.wait_ge(s_cst, 13)
                    dve.wait_ge(s_padz, 2)
                    with dve.Fori(0, B) as n:
                        for b in range(NBLK):
                            par = b % 2
                            dve.wait_ge(s_pk, n * NBLK + b + 1)
                            dve.wait_ge(s_kg, n * P2 + 1)
                            dve.tensor_scalar(kT[:, b * BLK:(b + 1) * BLK], bank[4 * par + 1][:, 0:BLK], vec[:, 1:2],
                                              None, ALU.add).then_inc(s_k, 1)
                            dve.wait_ge(s_pv, n * NBLK + b + 1)
                            dve.tensor_scalar(
                                vpad[:, 1 + b * ROWS:1 + (b + 1) * ROWS, 1:1 + W].rearrange("p r (w c) -> p w r c", c=WIN),
                                bank[4 * par + 2][:, 0:BLK].rearrange("p (w r c) -> p w r c", r=ROWS, c=WIN),
                                vec[:, 2:3], None, ALU.add).then_inc(s_v, 1)
                        dve.wait_ge(s_k, n * NBLK + NBLK)
                        dve.tensor_reduce(ks[:], kT[:].rearrange("p (w k) -> p w k", k=W2), AXX, ALU.add)\
                            .then_inc(s_qs, 1)
                        dve.wait_ge(s_q, n * NBLK + NBLK)
                        dve.tensor_reduce(qs[:], qT[:].rearrange("p (w k) -> p w k", k=W2), AXX, ALU.add)\
                            .then_inc(s_qs, 1)
                        dve.wait_ge(s_lg, n + 1)
                        dve.tensor_scalar(lg[:], bank[0][0:P2, 0:P2], 1.0 / (W2 * W2), None, ALU.mult).then_inc(s_tk, 1)
                        dve.wait_ge(s_tk, n * 3 + 2)
                        passed(dve)
                        dve.max(m8[:], lg[:]).then_inc(s_tk, 1)
                        dve.wait_ge(s_tk, n * 3 + 3)
                        dve.wait_ge(s_row, n * 16 + 16)
                        passed(dve)
                        dve.max_index(ix[:], m8[:], lg[:]).then_inc(s_tk, 1)

                        def maxes(w, par):
                            for j in range(PAIRS):
                                dve.wait_ge(s_S, n * P2 + w + 2)
                                dve.tensor_reduce(nmx[:, par, j:j + 1], bank[j][:, 0:KEYS], AXX, ALU.max, negate=True)\
                                    .then_inc(s_mx, 1)

                        def norm(w, par):
                            dve.wait_ge(s_ex, (n * P2 + w) * PAIRS + PAIRS + 1)
                            dve.reciprocal(rden[:, par, :], den[:, par, :]).then_inc(s_rd, 1)
                            dve.wait_ge(s_rd, n * P2 + w + 1)
                            for j in range(PAIRS):
                                ins = dve.tensor_scalar(Pr[:, par, j, :], Pr[:, par, j, :], rden[:, par, j:j + 1], None,
                                                        ALU.mult)
                            ins.then_inc(s_nP, 1)

                        def turned(w, par):
                            dve.wait_ge(s_T, n * P2 + w + 2)
                            dve.wait_ge(s_O, n * P2 + w + 2)
                            dve.tensor_copy(PT[:, par, 512:1024], bank[5][:]).then_inc(s_Tc, 1)

                        def attended(w):
                            dve.wait_ge(s_O, n * P2 + w + 4)
                            dve.wait_ge(s_o, n * P2 + w + 1)
                            dve.tensor_scalar(oh[:], bank[6][:, 0:W2], eo[:, 0:1], None, ALU.mult).then_inc(s_om, 1)
                            dve.wait_ge(s_om, n * P2 + w + 1)
                            dve.scalar_tensor_tensor(oT[:, bass.ds(w * W2, W2)], bank[6][:, W2:2 * W2], eo[:, 1:2],
                                                     oh[:], ALU.mult, ALU.add).then_inc(s_o, 1)

                        maxes(0, 0)
                        norm(0, 0)
                        maxes(1, 1)
                        turned(0, 0)
                        norm(1, 1)
                        with dve.Fori(0, (P2 - 3) // 2) as k:
                            maxes(k * 2 + 2, 0)
                            turned(k * 2 + 1, 1)
                            attended(k * 2)
                            norm(k * 2 + 2, 0)
                            maxes(k * 2 + 3, 1)
                            turned(k * 2 + 2, 0)
                            attended(k * 2 + 1)
                            norm(k * 2 + 3, 1)
                        maxes(P2 - 1, 0)
                        turned(P2 - 2, 1)
                        attended(P2 - 3)
                        norm(P2 - 1, 0)
                        turned(P2 - 1, 0)
                        attended(P2 - 2)
                        attended(P2 - 1)
                        dve.wait_ge(s_mvw, n + B)
                        for b in range(NBLK):
                            dve.wait_ge(s_out, n * NBLK + b + 1)
                            dve.scalar_tensor_tensor(xblk(n, b), bank[b][:, 0:BLK], cb[:, 1:2], xblk(n, b),
                                                     ALU.add, ALU.add).then_inc(s_ev, 1)
                            dve.wait_ge(s_ev, n * NBLK + b + 2)
                            passed(dve)
                            ins = dve.bn_stats(bn[:, b, :], xblk(n, b))
                        ins.then_inc(s_bst, 1)
                        image_stats(dve, n, n + B)

                @block.tensor
                def _(pe):
                    gn_tensor(pe, 0)
                    pe.wait_ge(s_cst, 12)
                    pe.matmul(bank[1][:, 0:1], w_o[:], cb[:, 0:1], start=True, stop=True).then_inc(s_cp, 1)
                    pe.wait_ge(s_cst, 13)
                    pe.wait_ge(s_gd, GN_DVE)
                    pe.wait_ge(s_padz, 2)
                    with pe.Fori(0, B) as n:
                        pe.wait_ge(s_ev, n * NBLK + 1)
                        for b in range(NBLK):
                            par = b % 2
                            xs = xb[:, par, :]
                            bq, bk, bv, bV = bank[4 * par:4 * par + 4]
                            pe.wait_ge(s_xb, n * NBLK + b + 2)
                            if b >= 2:
                                pe.wait_ge(s_q, n * NBLK + b - 1)
                                pe.wait_ge(s_k, n * NBLK + b - 1)
                                pe.wait_ge(s_v, n * NBLK + b - 1)
                                pe.wait_ge(s_V, n * NBLK + b)
                            pe.matmul(bq[:, 0:BLK], w_qkv[:, 0:C], xs, start=True, stop=True).then_inc(s_pq, 1)
                            pe.matmul(bk[:, 0:BLK], w_qkv[:, C:2 * C], xs, start=True, stop=True).then_inc(s_pk, 1)
                            pe.matmul(bv[:, 0:BLK], w_qkv[:, 2 * C:3 * C], xs, start=True, stop=True).then_inc(s_pv, 1)
                            for i in range(4):
                                m = 128 if i < 3 else 64
                                ins = pe.matmul(bV[0:m, i * C:(i + 1) * C], xs[:, i * 128:i * 128 + m],
                                                w_qkv[:, 2 * C:3 * C], start=True, stop=True)
                            ins.then_inc(s_pV, 1)
                        pe.wait_ge(s_qs, n * 2 + 2)
                        pe.matmul(bank[0][0:P2, 0:P2], qs[:], ks[:], start=True, stop=True).then_inc(s_lg, 1)
                        pe.wait_ge(s_V, n * NBLK + NBLK + 1)
                        pe.wait_ge(s_v, n * NBLK + NBLK)
                        pe.wait_ge(s_tk, n * 3 + 2)

                        def scores(w, par):
                            pe.wait_ge(s_kg, n * P2 + w + 2)
                            pe.wait_ge(s_Q, n * P2 + w + 2)
                            for j in range(PAIRS):
                                if not (isinstance(w, int) and w == 0):
                                    pe.wait_ge(s_ex, (n * P2 + w - 1) * PAIRS + j + 2)
                                ins = pe.matmul(bank[j][:, 0:KEYS], Qs[:, par, j * C:(j + 1) * C], kg[:, par, :],
                                                start=True, stop=True)
                            ins.then_inc(s_S, 1)

                        def turn(w, par):
                            pe.wait_ge(s_nP, n * P2 + w + 2)
                            pe.wait_ge(s_Tc, (n * P2 + w) * 2 + 1)
                            for j in range(PAIRS):
                                for c in range(2):
                                    ins = pe.transpose(bank[4 + j // 2][:, (j % 2 * 2 + c) * C:(j % 2 * 2 + c + 1) * C],
                                                       Pr[:, par, j, c * C:(c + 1) * C], ident[:])
                            ins.then_inc(s_T, 1)

                        def attend(w, par, slot, third):
                            pe.wait_ge(s_Tc, (n * P2 + w) * 2 + 3)
                            pe.wait_ge(s_vg[slot], (n * (17 if slot == 0 else 16) + third) * 64 + 64)
                            pe.wait_ge(s_o, n * P2 + w + 1)
                            for j in range(PAIRS):
                                for c in range(2):
                                    ins = pe.matmul(bank[6][32 * j:32 * j + 32, 0:C],
                                                    vg[:, slot, c, 32 * j:32 * j + 32],
                                                    PT[:, par, (2 * j + c) * C:(2 * j + c + 1) * C],
                                                    start=(c == 0), stop=(c == 1))
                            ins.then_inc(s_O, 1)

                        scores(0, 0)
                        scores(1, 1)
                        turn(0, 0)
                        def three(w, i, third):
                            scores(w, i % 2)
                            turn(w - 1, (i + 1) % 2)
                            attend(w - 2, i % 2, i % 3, third)
                        NR = (P2 - 2) // 6
                        with pe.Fori(0, NR) as k:
                            for i in range(6):
                                three(k * 6 + 2 + i, i, k * 2 + i // 3)
                        for i in range((P2 - 2) % 6):
                            three(NR * 6 + 2 + i, i, NR * 2 + i // 3)
                        turn(P2 - 1, 0)
                        attend(P2 - 2, 1, (P2 - 2) % 3, (P2 - 2) // 3)
                        attend(P2 - 1, 0, (P2 - 1) % 3, (P2 - 1) // 3)
                        pe.wait_ge(s_o, n * P2 + P2 + 1)
                        for b in range(NBLK):
                            ps3 = bank[b][:, 0:BLK]
                            pe.matmul(ps3, w_o[:], oT[:, b * BLK:(b + 1) * BLK]
                                      .rearrange("p (w r c) -> p r w c", r=ROWS, c=WIN), start=True, stop=False)
                            for k in range(9):
                                dy, dx = divmod(k, 3)
                                ins = pe.matmul(ps3, w_tap[:, k, :],
                                                vpad[:, b * ROWS + dy:b * ROWS + dy + ROWS, dx:dx + W],
                                                start=False, stop=(k == 8))
                            ins.then_inc(s_out, 1)

        if last_stage > 1:
            rnn(nc, mk, {**a, "_mv": mv}, X, bank, A, Bb, gn_tensor, gn_vector, gn_scalar, x1_dram, s_gd, passed)
        if last_stage > 2:
            masked_conv(nc, mk, a, X, bank, A, Bb, gn_tensor, gn_vector, gn_scalar, s_gd, bn, s_bst, s_mvw, image_stats,
                        xblk, passed)
        if last_stage > 3:
            conv_pair(nc, mk, a, X, bank, A, Bb, gn_tensor, gn_vector, gn_scalar, xblk, passed, s_gd, out)
        else:
            with nc.semaphore("stored") as s_st, nc.Block() as block:
                @block.sync
                def _(sp):
                    sp.dma_start(out.rearrange("n c h w -> c n (h w)"),
                                 X[:, PAD:PAD + B * HW].rearrange("p (n k) -> p n k", n=B)).then_inc(s_st, 16)
                    sp.wait_ge(s_st, 16)


LAST_STAGE = 4


def kernel(**inputs):
    import numpy as np
    import concourse.bacc as bacc
    from concourse.bass_utils import run_bass_kernel_spmd

    def cols(v, n):
        return v.reshape(n, 128).T

    i = {k: np.asarray(v) for k, v in inputs.items()}
    ch = np.arange(128)
    one = np.float32(1)
    laid = {
        "x": i["x"],
        "w_qkv": i["L0_conv_W_qkv"],
        "b_qkv": cols(i["L0_conv_b_qkv"], 3),
        "b_q": i["L0_conv_b_qkv"][0:128].reshape(128, 1),
        "lepe_w": i["L0_conv_lepe_w"].reshape(128, 9),
        "lepe_b": i["L0_conv_lepe_b"].reshape(128, 1),
        "w_o": i["L0_conv_W_o"],
        "b_o": i["L0_conv_b_o"].reshape(128, 1),
        "gamma": i["L1_conv_gamma"].reshape(128, 1),
        "beta": i["L1_conv_beta"].reshape(128, 1),
        "w_in": i["L1_conv_w_in"].T,
        "b_in": cols(i["L1_conv_b_in"], 2),
        "w_ih": i["L1_conv_w_ih"].T.reshape(2, 128, 512).transpose(1, 0, 2),
        "b_ih": cols(i["L1_conv_b_ih"], 4),
        "w_hh": i["L1_conv_w_hh"].T.reshape(4, 128, 512).transpose(1, 0, 2),
        "b_hh": cols(i["L1_conv_b_hh"], 4),
        "w_out": i["L1_conv_w_out"].T.reshape(4, 128, 128).transpose(1, 0, 2),
        "b_out": i["L1_conv_b_out"].reshape(128, 1),
        "w3": i["L2_conv_w3"].transpose(1, 2, 3, 0).reshape(128, 9, 128),
        "w1": i["L2_conv_w1"].T,
        "b2": i["L2_conv_b"],
        "c1": i["L3_conv_w1"].transpose(1, 2, 3, 0).reshape(128, 9, 128),
        "c2": i["L3_conv_w2"].transpose(1, 2, 3, 0).reshape(128, 9, 128),
        "g1": i["L3_conv_gamma1"].reshape(128, 1), "h1": i["L3_conv_beta1"].reshape(128, 1),
        "m1": i["L3_conv_mean1"].reshape(128, 1), "v1": i["L3_conv_var1"].reshape(128, 1),
        "g2": i["L3_conv_gamma2"].reshape(128, 1), "h2": i["L3_conv_beta2"].reshape(128, 1),
        "m2": i["L3_conv_mean2"].reshape(128, 1), "v2": i["L3_conv_var2"].reshape(128, 1),
        "ident": np.eye(128, dtype=np.float32),
        "group4": (ch[:, None] // GROUP == ch[None, :] // GROUP).astype(np.float32) / np.float32(GROUP),
        "even_odd": np.stack([ch // HD % 2 == 0, ch // HD % 2 == 1], 1).astype(np.float32),
        "head_mask": (ch[:, None] // HD == np.arange(HEADS)[None, :]).astype(np.float32),
        "on_grid": ((ch[:, None] - ch[None, :]) % 4 == 0).astype(np.float32),
        "off_grid": ((ch[:, None] - ch[None, :]) % 4 != 0).astype(np.float32),
        "ones": np.full((128, 1), one),
    }
    nc = bacc.Bacc("TRN2", target_bir_lowering=False, num_devices=1)
    arrays, aps = {}, {}
    for k, v in laid.items():
        v = np.ascontiguousarray(v)
        arrays[f"in_{k}"] = v
        aps[k] = nc.dram_tensor(f"in_{k}", v.shape, F32, kind="ExternalInput").ap()
    out = nc.dram_tensor("out_0", (B, C, H, W), F32, kind="ExternalOutput").ap()
    program(nc, aps, out, LAST_STAGE)
    r = run_bass_kernel_spmd(nc, [arrays], core_ids=[0])
    return r.results[0]["out_0"]
```

```python
import concourse.bass as bass
from concourse import mybir
from contextlib import ExitStack

F32 = mybir.dt.float32
F32R = mybir.dt.float32r
U32 = mybir.dt.uint32
ACT = mybir.ActivationFunctionType
ALU = mybir.AluOpType
AXX = mybir.AxisListType.X

B, C, H, W = 8, 128, 56, 56
HW = H * W
ROWS = 8
BLK = ROWS * W
NBLK = H // ROWS
GROUP = 4
GN_EPS = 1e-5
NWIN = 7
WIN = H // NWIN
P2 = NWIN * NWIN
W2 = WIN * WIN
HEADS = 8
HD = C // HEADS
TOPK = 4
KEYS = TOPK * W2
PAIRS = HEADS // 2
QSCALE = float(C) ** -0.5
RIN, RH = 256, 512
NI, NH = RIN // 128, RH // 128
SEG = 16
L = HW // SEG
WARM = 64
COLS = B * SEG
PAD = WARM
HANDOVER_TOL = 2.0 ** -17
PW = WARM // 2
PM = L // 2
BN_EPS = 1e-5
BN_STEPS = 23


GN_DVE, GN_PE = 11, 2


def rsqrt_vector(e, r, v, tmp, done, d0):
    e.wait_ge(done, d0)
    e.reciprocal(r, r).then_inc(done, 1)
    e.wait_ge(done, d0 + 1)
    e.tensor_tensor(tmp, v, r, ALU.mult).then_inc(done, 1)
    e.wait_ge(done, d0 + 2)
    e.tensor_tensor(tmp, tmp, r, ALU.mult).then_inc(done, 1)
    e.wait_ge(done, d0 + 3)
    e.tensor_scalar(tmp, tmp, -0.5, 1.5, ALU.mult, ALU.add).then_inc(done, 1)
    e.wait_ge(done, d0 + 4)
    e.tensor_tensor(r, r, tmp, ALU.mult).then_inc(done, 1)
    e.wait_ge(done, d0 + 5)


def rnn(nc, mk, a, X, bank, A, Bb, gn_tensor, gn_vector, gn_scalar, x1_dram, s_gd, passed):
    CH = 2 * COLS
    with ExitStack() as ctx:
        sb, _, sem = mk(ctx)
        w_in = sb("w_in", [C, RIN])
        w_ih = sb("w_ih", [128, NI, RH])
        w_hh = sb("w_hh", [128, NH, RH])
        w_out = sb("w_out", [128, NH, C])
        vecs = sb("vecs", [C, 3])
        b_in = sb("b_in", [128, NI])
        bg = sb("bg", [128, 2, NH])
        ones = sb("ones", [128, 1])
        e1, e2, mu = sb("e1", [C, B]), sb("e2", [C, B]), sb("mu", [C, 4])
        A2 = sb("A2", [C, B, SEG])
        B2 = sb("B2", [C, B, SEG])
        mvp = sb("mvp", [C, B, 2])
        xa = sb("xa", [C, 2, 2, COLS])
        tz = sb("tz", [128, 2, NI, CH])
        inp = sb("inp", [128, 2, NI, CH])
        h = sb("h", [128, 4, NH, COLS])
        start = sb("start", [128, NH, COLS])
        okc = sb("okc", [128, 2])
        flag = sb("flag", [1, 1], U32)
        s_w = sem("rnn_weights_loaded")
        s_bn = sem("batchnorm_steps")
        s_bnr = sem("batchnorm_root")
        s_xm = sem("x_scaled")
        s_xa = sem("x_normalised")
        s_pre, s_tz, s_inp = sem("pre_product"), sem("pre_tanh"), sem("input_ready")
        s_g, s_h = sem("gates_product"), sem("state_ready")
        s_y, s_yd = sem("y_product"), sem("y_added")
        s_seed = sem("start_states")
        s_ver, s_verp, s_flag = sem("verify_steps"), sem("verify_product"), sem("verdict_ready")
        s_rel = sem("x1_reloaded")
        mvi = a["_mv"]

        def xcols(tok, k=2):
            return X[:, bass.ds(tok, COLS * L)].rearrange("p (c l) -> p l c", l=L)[:, 0:k, :]

        def pre_product(pe, P, q):
            pe.wait_ge(s_xa, P + 1)
            pe.wait_ge(s_inp, P * 2 + 2)
            for i in range(NI):
                ins = pe.matmul(bank[4 + q][:, i * CH:(i + 1) * CH], w_in[:, i * 128:(i + 1) * 128],
                                xa[:, q].rearrange("p t c -> p (t c)"), start=True, stop=True)
            ins.then_inc(s_pre, 1)

        def y_product(pe, Y, q):
            pe.wait_ge(s_yd, Y + 1)
            for k in range(NH):
                ins = pe.matmul(bank[6 + q][:, 0:CH], w_out[:, k, :], h[:, 2 * q:2 * q + 2, k, :],
                                start=(k == 0), stop=(k == NH - 1))
            ins.then_inc(s_y, 1)

        def tensor_pair(pe, P, q, y=None, more=True, seed=None):
            if more:
                pre_product(pe, P + 1, 1 - q)
            pe.wait_ge(s_inp, P * 2 + 6)
            if seed is not None:
                pe.wait_ge(s_seed, seed)
            for tt in range(2):
                prev = (2 * q + tt - 1) % 4
                for m in range(NH):
                    if m == 0:
                        pe.wait_ge(s_h, P * 8 + tt * 4 + 1)
                    for i in range(NI):
                        pe.matmul(bank[m][:, 0:COLS], w_ih[:, i, m * 128:(m + 1) * 128],
                                  inp[:, q, i, tt * COLS:(tt + 1) * COLS], start=(i == 0), stop=False)
                    for k in range(NH):
                        if m == 0:
                            pe.wait_ge(s_h, P * 8 + tt * 4 + k + 1)
                        ins = pe.matmul(bank[m][:, 0:COLS], w_hh[:, k, m * 128:(m + 1) * 128], h[:, prev, k, :],
                                        start=False, stop=(k == NH - 1))
                    ins.then_inc(s_g, 1)
                if tt == 0 and y is not None:
                    y_product(pe, y, 1 - q)

        def pre_tanh(act, P, q):
            act.wait_ge(s_pre, P + 3)
            act.wait_ge(s_inp, P * 2 + 2)
            for i in range(NI):
                act.activation(tz[:, q, i, :], bank[4 + q][:, i * CH:(i + 1) * CH], ACT.Tanh, bias=b_in[:, i:i + 1])\
                    .then_inc(s_tz, 1)

        def scalar_pair(act, P, q, more=True):
            if more:
                pre_tanh(act, P + 1, 1 - q)
            for tt in range(2):
                for m in range(NH):
                    act.wait_ge(s_g, P * 8 + tt * 4 + m + 17)
                    act.activation(h[:, 2 * q + tt, m, :], bank[m][:, 0:COLS], ACT.Tanh, bias=bg[:, 0, m:m + 1])\
                        .then_inc(s_h, 1)

        def normalise(dve, P, q, tok):
            dve.wait_ge(s_pre, P + 1)
            dve.tensor_tensor(xa[:, q], xcols(tok), A2[:].rearrange("p n s -> p (n s)").unsqueeze(1)
                              .to_broadcast([C, 2, COLS]), ALU.mult).then_inc(s_xm, 1)
            dve.wait_ge(s_xm, P + 1)
            dve.tensor_tensor(xa[:, q], xa[:, q], B2[:].rearrange("p n s -> p (n s)").unsqueeze(1)
                              .to_broadcast([C, 2, COLS]), ALU.add).then_inc(s_xa, 1)

        def shrink(dve, P, q):
            dve.wait_ge(s_g, P * 8 + 8)
            dve.wait_ge(s_tz, P * 2 + 2)
            for i in range(NI):
                dve.scalar_tensor_tensor(inp[:, q, i, :], bank[4 + q][:, i * CH:(i + 1) * CH], b_in[:, i:i + 1],
                                         tz[:, q, i, :], ALU.add, ALU.subtract).then_inc(s_inp, 1)

        def add_y(dve, Y, q, tok):
            dve.wait_ge(s_y, Y + 1)
            dve.scalar_tensor_tensor(xcols(tok), bank[6 + q][:, 0:CH].rearrange("p (t c) -> p t c", t=2), vecs[:, 2:3],
                                     xcols(tok), ALU.add, ALU.add).then_inc(s_yd, 1)

        def vector_pair(dve, P, q, tok, y=None, more=2):
            if more > 1:
                normalise(dve, P + 2, q, tok + 4)
            if more > 0:
                shrink(dve, P + 1, 1 - q)
            if y is not None:
                add_y(dve, y, 1 - q, tok - 2)

        PA = PW + PM
        RND, RNDW = PA // 2, PW // 2

        def run(e, first, P0, Y0, tok0, warm, seed, lead, body, tail):
            lead()
            if warm:
                with e.Fori(0, warm) as k:
                    body(k, False, False, None, False)
            body(warm, False, True, seed, False)
            with e.Fori(warm + 1, warm + PM // 2 - 1) as k:
                body(k, True, True, None, False)
            body(warm + PM // 2 - 1, True, True, None, True)
            tail(warm + PM // 2 - 1)

        def run_tensor(pe, P0, Y0, warm, seed):
            def body(k, y0, y1, sd, last):
                P = P0 + k * 2
                Y = Y0 + k * 2 - 2 * warm
                tensor_pair(pe, P, 0, Y - 1 if y0 else None, True, sd)
                tensor_pair(pe, P + 1, 1, Y if y1 else None, not last)

            def tail(k):
                pe.wait_ge(s_h, (P0 + 2 * k + 2) * 8 + 4)
                y_product(pe, Y0 + 2 * k - 2 * warm + 1, 1)
            run(pe, None, P0, Y0, None, warm, seed, lambda: pre_product(pe, P0, 0), body, tail)

        def run_scalar(act, P0, Y0, warm):
            def body(k, y0, y1, sd, last):
                P = P0 + k * 2
                scalar_pair(act, P, 0)
                scalar_pair(act, P + 1, 1, not last)
            run(act, None, P0, Y0, None, warm, None, lambda: pre_tanh(act, P0, 0), body, lambda k: None)

        def run_vector(dve, P0, Y0, warm, tok0, at_seed):
            def lead():
                normalise(dve, P0, 0, tok0)
                normalise(dve, P0 + 1, 1, tok0 + 2)
                shrink(dve, P0, 0)

            def body(k, y0, y1, sd, last):
                P = P0 + k * 2
                Y = Y0 + k * 2 - 2 * warm
                tok = tok0 + k * 4
                if sd and at_seed:
                    at_seed()
                vector_pair(dve, P, 0, tok, Y - 1 if y0 else None, 1 if last else 2)
                vector_pair(dve, P + 1, 1, tok + 2, Y if y1 else None, 0 if last else 2)

            def tail(k):
                add_y(dve, Y0 + 2 * k - 2 * warm + 1, 1, tok0 + 4 * k + 2)
            run(dve, None, P0, Y0, None, warm, 1, lead, body, tail)

        SEEDS, NWL = 2, 10
        hs = h[:].rearrange("p t k (n s) -> p t k n s", s=SEG)
        st4 = start[:].rearrange("p k (n s) -> p k n s", s=SEG)

        with nc.Block() as block:
            @block.sync
            def _(sp):
                for dst, src in ((w_in[:], a["w_in"]), (w_ih[:], a["w_ih"]), (w_hh[:], a["w_hh"]), (w_out[:], a["w_out"]),
                                 (vecs[:, 0:1], a["gamma"]), (vecs[:, 1:2], a["beta"]), (vecs[:, 2:3], a["b_out"]),
                                 (b_in[:], a["b_in"]), (bg[:, 0, :], a["b_ih"]), (bg[:, 1, :], a["b_hh"])):
                    sp.dma_start(dst, src, allow_slow_non_contiguous=True).then_inc(s_w, 16)
                sp.wait_ge(s_flag, 1)
                bad = sp.value_load(flag[0:1, 0:1], min_val=0, max_val=1)
                with sp.If(bad > 0):
                    with sp.Fori(0, SEG - 1) as r:
                        sp.wait_ge(s_yd, r * PM + PM + 2)
                        passed(sp)
                        sp.dma_start(X[:, PAD:PAD + B * HW].rearrange("p (n k) -> p n k", n=B),
                                     x1_dram.rearrange("n c k -> c n k")).then_inc(s_rel, 16)

            @block.gpsimd
            def _(pool):
                pool.sem_inc(s_g, 16)
                pool.sem_inc(s_pre, 2)
                pool.sem_inc(s_inp, 4)
                pool.sem_inc(s_yd, 2)
                pool.memset(ones[:], 1.0).then_inc(s_verp, 1)

            @block.scalar
            def _(act):
                gn_scalar(act, 1)
                act.wait_ge(s_bn, 11)
                act.activation(mu[:, 2:3], mu[:, 1:2], ACT.Sqrt).then_inc(s_bnr, 1)
                act.wait_ge(s_w, 16 * NWL)
                act.wait_ge(s_bn, BN_STEPS)
                run_scalar(act, 0, 0, RNDW)
                act.wait_ge(s_flag, 1)
                bad = act.value_load(flag[0:1, 0:1], min_val=0, max_val=1)
                with act.If(bad > 0):
                    with act.Fori(0, SEG - 1) as r:
                        run_scalar(act, r * PM + PA, r * PM + PM, 0)

            @block.vector
            def _(dve):
                gn_vector(dve, 1)
                dve.wait_ge(s_w, 16 * NWL)
                n_bn = [0]

                def link(ins):
                    n_bn[0] += 1
                    ins.then_inc(s_bn, 1)
                    dve.wait_ge(s_bn, n_bn[0])
                link(dve.tensor_tensor(e1[:], A[:], mvi[:, :, 0], ALU.mult))
                link(dve.tensor_tensor(e1[:], e1[:], Bb[:], ALU.add))
                link(dve.tensor_reduce(mu[:, 0:1], e1[:], AXX, ALU.add))
                link(dve.tensor_scalar(mu[:, 0:1], mu[:, 0:1], 1.0 / B, None, ALU.mult))
                link(dve.tensor_scalar(e1[:], e1[:], mu[:, 0:1], None, ALU.subtract))
                link(dve.tensor_tensor(e1[:], e1[:], e1[:], ALU.mult))
                link(dve.tensor_tensor(e2[:], A[:], A[:], ALU.mult))
                link(dve.tensor_tensor(e2[:], e2[:], mvi[:, :, 1], ALU.mult))
                link(dve.tensor_tensor(e2[:], e2[:], e1[:], ALU.add))
                link(dve.tensor_reduce(mu[:, 1:2], e2[:], AXX, ALU.add))
                link(dve.tensor_scalar(mu[:, 1:2], mu[:, 1:2], 1.0 / B, BN_EPS, ALU.mult, ALU.add))
                dve.wait_ge(s_bnr, 1)
                rsqrt_vector(dve, mu[:, 2:3], mu[:, 1:2], mu[:, 3:4], s_bn, n_bn[0])
                n_bn[0] += 5
                link(dve.tensor_tensor(mu[:, 2:3], mu[:, 2:3], vecs[:, 0:1], ALU.mult))
                link(dve.tensor_scalar(e1[:], A[:], mu[:, 2:3], None, ALU.mult))
                link(dve.tensor_scalar(e2[:], Bb[:], mu[:, 0:1], mu[:, 2:3], ALU.subtract, ALU.mult))
                link(dve.tensor_scalar(e2[:], e2[:], vecs[:, 1:2], None, ALU.add))
                link(dve.tensor_copy(A2[:], e1[:].unsqueeze(2).to_broadcast([C, B, SEG])))
                link(dve.tensor_copy(B2[:], e2[:].unsqueeze(2).to_broadcast([C, B, SEG])))
                link(dve.tensor_tensor(bg[:, 0, :], bg[:, 0, :], bg[:, 1, :], ALU.add))
                assert n_bn[0] == BN_STEPS
                dve.memset(h[:, 3], 0.0).then_inc(s_h, NH)

                def at_seed():
                    dve.wait_ge(s_h, 4 + NH * WARM)
                    dve.tensor_copy(start[:], h[:, 3]).then_inc(s_seed, 1)
                    dve.wait_ge(s_seed, 1)
                    dve.memset(hs[:, 3, :, :, 0:1], 0.0).then_inc(s_seed, 1)

                run_vector(dve, 0, 0, RNDW, 0, at_seed)
                d = inp[:].rearrange("p a b c -> p (a b c)")[:, 0:NH * B * (SEG - 1)]
                d4 = d.rearrange("p (k n s) -> p k n s", k=NH, n=B)
                dve.wait_ge(s_h, 4 + NH * 2 * PA)
                dve.wait_ge(s_g, 16 + NH * 2 * PA)
                for k in range(NH):
                    ins = dve.tensor_tensor(d4[:, k], hs[:, 3, k, :, 0:SEG - 1], st4[:, k, :, 1:SEG], ALU.subtract)
                ins.then_inc(s_ver, 1)
                dve.wait_ge(s_ver, 1)
                dve.tensor_tensor(d, d, d, ALU.mult).then_inc(s_ver, 1)
                dve.wait_ge(s_ver, 2)
                dve.tensor_scalar(d, d, HANDOVER_TOL ** 2, None, ALU.is_le).then_inc(s_ver, 1)
                dve.wait_ge(s_ver, 3)
                dve.tensor_reduce(okc[:, 0:1], d, AXX, ALU.min).then_inc(s_ver, 1)
                dve.wait_ge(s_verp, 2)
                dve.tensor_scalar(flag[:], bank[0][0:1, 0:1], 127.5, None, ALU.is_lt).then_inc(s_flag, 1)
                dve.wait_ge(s_flag, 1)
                bad = dve.value_load(flag[0:1, 0:1], min_val=0, max_val=1)
                with dve.If(bad > 0):
                    with dve.Fori(0, SEG - 1) as r:
                        dve.wait_ge(s_h, r * (NH * L) + 4 + NH * 2 * PA)
                        dve.wait_ge(s_yd, r * PM + PM + 2)
                        dve.tensor_copy(start[:], h[:, 3]).then_inc(s_seed, 1)
                        dve.wait_ge(s_seed, r * 3 + 3)
                        dve.tensor_copy(h[:, 3, :, 1:COLS], start[:, :, 0:COLS - 1]).then_inc(s_seed, 1)
                        dve.wait_ge(s_seed, r * 3 + 4)
                        dve.memset(hs[:, 3, :, :, 0:1], 0.0).then_inc(s_seed, 1)
                        dve.wait_ge(s_rel, r * 16 + 16)
                        run_vector(dve, r * PM + PA, r * PM + PM, 0, PAD, None)

            @block.tensor
            def _(pe):
                gn_tensor(pe, 1)
                pe.wait_ge(s_w, 16 * NWL)
                run_tensor(pe, 0, 0, RNDW, SEEDS)
                pe.wait_ge(s_ver, 4)
                pe.wait_ge(s_verp, 1)
                pe.matmul(bank[0][0:1, 0:1], okc[:, 0:1], ones[:], start=True, stop=True).then_inc(s_verp, 1)
                pe.wait_ge(s_flag, 1)
                bad = pe.value_load(flag[0:1, 0:1], min_val=0, max_val=1)
                with pe.If(bad > 0):
                    with pe.Fori(0, SEG - 1) as r:
                        run_tensor(pe, r * PM + PA, r * PM + PM, 0, r * 3 + 5)


def split_product(pe, ps, w, x, first, last):
    pe.matmul(ps, w[0], x[0], start=first, stop=False)
    pe.matmul(ps, w[0], x[1], start=False, stop=False)
    return pe.matmul(ps, w[1], x[0], start=False, stop=last)


def pad_blocks(b):
    return min(b + 1, NBLK - 1)


def masked_conv(nc, mk, a, X, bank, A, Bb, gn_tensor, gn_vector, gn_scalar, s_gd, bn, s_bst, s_mvw,
                image_stats, xblk, passed):
    with ExitStack() as ctx:
        sb, _, sem = mk(ctx)
        w3 = sb("w3", [C, 9, C])
        w1 = sb("w1", [C, C])
        on, off = sb("on_grid", [C, C]), sb("off_grid", [C, C])
        b2 = sb("b2", [C, C])
        bsum = sb("bsum", [C, 1])
        w_hi, w_lo = sb("w3_hi", [C, 9, C], F32R), sb("w3_lo", [C, 9, C], F32R)
        p_hi = sb("pad_hi", [C, 2, H + 2, W + 2], F32R)
        p_lo = sb("pad_lo", [C, 2, H + 2, W + 2], F32R)
        z = sb("z", [C, 2, BLK])
        s_w, s_wr, s_z = sem("conv_weights_loaded"), sem("conv_weights_masked"), sem("pad_zero")
        s_hi, s_pad, s_cv, s_ev = sem("pad_hi_ready"), sem("pad_ready"), sem("conv_product"), sem("conv_added")

        with nc.Block() as block:
            @block.sync
            def _(sp):
                for dst, src in ((w3[:], a["w3"]), (w1[:], a["w1"]), (on[:], a["on_grid"]), (off[:], a["off_grid"]),
                                 (b2[:], a["b2"])):
                    sp.dma_start(dst, src).then_inc(s_w, 16)

            @block.gpsimd
            def _(pool):
                pool.sem_inc(s_cv, 15)
                pool.sem_inc(s_ev, 8)
                pool.sem_inc(s_pad, 2)
                pool.memset(p_hi[:].bitcast(F32), 0.0).then_inc(s_z, 1)
                pool.memset(p_lo[:].bitcast(F32), 0.0).then_inc(s_z, 1)
                pool.wait_ge(s_z, 2)
                with pool.Fori(0, B // 2) as g:
                    for u in range(2):
                        for b in range(NBLK):
                            pool.wait_ge(s_hi, (g * 2 + u) * NBLK + b + 1)
                            passed(pool)
                            rows = slice(1 + b * ROWS, 1 + (b + 1) * ROWS)
                            pool.tensor_tensor(p_lo[:, u, rows, 1:1 + W], z[:, b % 2, :].rearrange("p (r c) -> p r c", c=W),
                                               p_hi[:, u, rows, 1:1 + W].bitcast(F32), ALU.subtract).then_inc(s_pad, 1)

            @block.scalar
            def _(act):
                gn_scalar(act, 2)
                act.wait_ge(s_gd, 3 * GN_DVE)
                act.wait_ge(s_z, 2)
                with act.Fori(0, B // 2) as g:
                    for u in range(2):
                        n = g * 2 + u
                        act.wait_ge(s_cv, n * NBLK + 8)
                        for b in range(NBLK):
                            act.wait_ge(s_pad, n * NBLK + b + (1 if b else 2))
                            act.activation(z[:, b % 2, :], xblk(n, b), ACT.Identity, bias=Bb[:, bass.ds(n, 1)],
                                           scale=A[:, bass.ds(n, 1)])
                            act.activation(p_hi[:, u, 1 + b * ROWS:1 + (b + 1) * ROWS, 1:1 + W],
                                           xblk(n, b).rearrange("p (r c) -> p r c", c=W), ACT.Identity,
                                           bias=Bb[:, bass.ds(n, 1)], scale=A[:, bass.ds(n, 1)]).then_inc(s_hi, 1)

            @block.vector
            def _(dve):
                with dve.Fori(0, B) as n:
                    dve.wait_ge(s_mvw, n + 2 * B)
                    passed(dve)
                    for b in range(NBLK):
                        ins = dve.bn_stats(bn[:, b, :], xblk(n, b))
                    ins.then_inc(s_bst, 1)
                    image_stats(dve, n, n + 2 * B)
                gn_vector(dve, 2)
                dve.wait_ge(s_w, 80)
                dve.tensor_tensor(w3[:], w3[:], on[:].unsqueeze(1).to_broadcast([C, 9, C]), ALU.mult).then_inc(s_wr, 1)
                dve.tensor_tensor(w1[:], w1[:], off[:], ALU.mult).then_inc(s_wr, 1)
                dve.wait_ge(s_wr, 2)
                dve.tensor_tensor(w3[:, 4, :], w3[:, 4, :], w1[:], ALU.add).then_inc(s_wr, 1)
                dve.tensor_reduce(bsum[:], b2[:], AXX, ALU.add).then_inc(s_wr, 1)
                dve.wait_ge(s_wr, 4)
                dve.tensor_copy(w_hi[:], w3[:]).then_inc(s_wr, 1)
                dve.wait_ge(s_wr, 5)
                dve.tensor_tensor(w_lo[:], w3[:], w_hi[:].bitcast(F32), ALU.subtract).then_inc(s_wr, 1)
                with dve.Fori(0, B) as n:
                    dve.wait_ge(s_mvw, n + 3 * B)
                    for b in range(NBLK):
                        dve.wait_ge(s_cv, n * NBLK + b + 16)
                        dve.scalar_tensor_tensor(xblk(n, b), bank[b][:, 0:BLK], bsum[:], xblk(n, b), ALU.add, ALU.add)\
                            .then_inc(s_ev, 1)
                        dve.wait_ge(s_ev, n * NBLK + b + 9)
                        passed(dve)
                        ins = dve.bn_stats(bn[:, b, :], xblk(n, b))
                    ins.then_inc(s_bst, 1)
                    image_stats(dve, n, n + 3 * B)

            @block.tensor
            def _(pe):
                gn_tensor(pe, 2)
                pe.wait_ge(s_wr, 6)
                with pe.Fori(0, B // 2) as g:
                    for u in range(2):
                        n = g * 2 + u
                        for b in range(NBLK):
                            pe.wait_ge(s_pad, n * NBLK + pad_blocks(b) + 3)
                            pe.wait_ge(s_ev, n * NBLK + b + 2)
                            for k in range(9):
                                dy, dx = divmod(k, 3)
                                at = (slice(None), u, slice(b * ROWS + dy, b * ROWS + dy + ROWS), slice(dx, dx + W))
                                ins = split_product(pe, bank[b][:, 0:BLK], (w_hi[:, k, :], w_lo[:, k, :]),
                                                    (p_hi[at], p_lo[at]), k == 0, k == 8)
                            ins.then_inc(s_cv, 1)


def conv_pair(nc, mk, a, X, bank, A, Bb, gn_tensor, gn_vector, gn_scalar, xblk, passed, s_gd, out):
    with ExitStack() as ctx:
        sb, _, sem = mk(ctx)
        c1, c2 = sb("c1", [C, 9, C]), sb("c2", [C, 9, C])
        bnv = sb("bnv", [C, 8])
        sv = sb("sv", [C, 2])
        tv = sb("tv", [C, 2])
        root, tmp = sb("root", [C, 2]), sb("tmp", [C, 2])
        w_hi = [sb(f"c{i}_hi", [C, 9, C], F32R) for i in (1, 2)]
        w_lo = [sb(f"c{i}_lo", [C, 9, C], F32R) for i in (1, 2)]
        pz = [sb(f"z_pad_{k}", [C, H + 2, W + 2], F32R) for k in ("hi", "lo")]
        pm = [sb(f"mid_pad_{k}", [C, H + 2, W + 2], F32R) for k in ("hi", "lo")]
        zr = sb("z_ring", [C, 2, BLK])
        mr = sb("mid_ring", [C, 2, BLK])
        res = sb("res", [C, 2, BLK])
        s_w, s_z = sem("pair_weights_loaded"), sem("pair_pads_zero")
        s_k, s_kr = sem("pair_bn_steps"), sem("pair_bn_root")
        s_pz, s_c1, s_m, s_c2 = sem("z_ready"), sem("conv1_product"), sem("mid_ready"), sem("conv2_product")
        s_zr, s_mr, s_r1 = sem("z_hi_ready"), sem("mid_hi_ready"), sem("residual_hi_added")
        s_r, s_rl, s_add, s_st = sem("residual_added"), sem("relu_done"), sem("x_added"), sem("stored")
        o = out.rearrange("n c h w -> n c (h w)")
        v4 = bnv[:].rearrange("p (j q) -> p j q", j=2)

        with nc.Block() as block:
            @block.sync
            def _(sp):
                for dst, src in ((c1[:], a["c1"]), (c2[:], a["c2"])) + tuple(
                        (bnv[:, i:i + 1], a[k]) for i, k in enumerate(("g1", "h1", "m1", "v1", "g2", "h2", "m2", "v2"))):
                    sp.dma_start(dst, src, allow_slow_non_contiguous=True).then_inc(s_w, 16)
                with sp.Fori(0, B) as n:
                    sp.wait_ge(s_add, n * NBLK + NBLK + 2)
                    passed(sp)
                    sp.dma_start(o[bass.ds(n, 1)].rearrange("u c k -> (u c) k"), X[:, bass.ds(PAD + n * HW, HW)])\
                        .then_inc(s_st, 16)
                sp.wait_ge(s_st, 16 * B)

            @block.gpsimd
            def _(pool):
                pool.sem_inc(s_c1, 8)
                pool.sem_inc(s_c2, 15)
                pool.sem_inc(s_m, 8)
                pool.sem_inc(s_r, 8)
                pool.sem_inc(s_rl, 2)
                pool.sem_inc(s_add, 2)
                pool.sem_inc(s_pz, 2)
                for k in range(2):
                    pool.memset(pz[k][:].bitcast(F32), 0.0).then_inc(s_z, 1)
                    pool.memset(pm[k][:].bitcast(F32), 0.0).then_inc(s_z, 1)
                pool.wait_ge(s_z, 4)

                def lo(pads, ring, b, done):
                    rows = slice(1 + b * ROWS, 1 + (b + 1) * ROWS)
                    pool.tensor_tensor(pads[1][:, rows, 1:1 + W], ring[:, b % 2, :].rearrange("p (r c) -> p r c", c=W),
                                       pads[0][:, rows, 1:1 + W].bitcast(F32), ALU.subtract).then_inc(done, 1)

                for b in range(NBLK):
                    pool.wait_ge(s_zr, b + 1)
                    lo(pz, zr, b, s_pz)
                with pool.Fori(0, B - 1) as n:
                    for b in range(NBLK):
                        pool.wait_ge(s_mr, n * NBLK + b + 1)
                        passed(pool)
                        lo(pm, mr, b, s_m)
                    for b in range(NBLK):
                        pool.wait_ge(s_zr, n * NBLK + NBLK + b + 1)
                        passed(pool)
                        lo(pz, zr, b, s_pz)
                for b in range(NBLK):
                    pool.wait_ge(s_mr, (B - 1) * NBLK + b + 1)
                    lo(pm, mr, b, s_m)

            @block.scalar
            def _(act):
                gn_scalar(act, 3)
                act.wait_ge(s_k, 1)
                act.activation(root[:], tmp[:], ACT.Sqrt).then_inc(s_kr, 1)
                act.wait_ge(s_gd, 4 * GN_DVE)
                act.wait_ge(s_k, 9)
                act.wait_ge(s_z, 4)

                def z_block(n, b):
                    act.wait_ge(s_pz, n * NBLK + b + (1 if b else 2))
                    act.activation(zr[:, b % 2, :], xblk(n, b), ACT.Identity, bias=Bb[:, bass.ds(n, 1)],
                                   scale=A[:, bass.ds(n, 1)])
                    act.activation(pz[0][:, 1 + b * ROWS:1 + (b + 1) * ROWS, 1:1 + W],
                                   xblk(n, b).rearrange("p (r c) -> p r c", c=W), ACT.Identity,
                                   bias=Bb[:, bass.ds(n, 1)], scale=A[:, bass.ds(n, 1)]).then_inc(s_zr, 1)

                for b in range(NBLK):
                    z_block(0, b)

                def image(n, more):
                    for b in range(NBLK):
                        act.wait_ge(s_c1, n * NBLK + b + 9)
                        act.wait_ge(s_m, n * NBLK + b + (7 if b else 8))
                        act.activation(mr[:, b % 2, :], bank[b][:, 0:BLK], ACT.Relu, bias=tv[:, 0:1], scale=sv[:, 0:1])
                        act.activation(pm[0][:, 1 + b * ROWS:1 + (b + 1) * ROWS, 1:1 + W],
                                       bank[b][:, 0:BLK].rearrange("p (r c) -> p r c", c=W), ACT.Relu,
                                       bias=tv[:, 0:1], scale=sv[:, 0:1]).then_inc(s_mr, 1)
                    for b in range(NBLK):
                        act.wait_ge(s_r, n * NBLK + b + 9)
                        act.activation(res[:, b % 2, :], res[:, b % 2, :], ACT.Relu, bias=tv[:, 1:2]).then_inc(s_rl, 1)
                        if more:
                            z_block(n + 1, b)

                with act.Fori(0, B - 1) as n:
                    image(n, True)
                image(B - 1, False)

            @block.vector
            def _(dve):
                gn_vector(dve, 3)
                dve.wait_ge(s_w, 160)
                dve.tensor_scalar(tmp[:], v4[:, :, 3], BN_EPS, None, ALU.add).then_inc(s_k, 1)
                dve.wait_ge(s_kr, 1)
                rsqrt_vector(dve, root[:], tmp[:], sv[:], s_k, 1)
                dve.tensor_tensor(sv[:], root[:], v4[:, :, 0], ALU.mult).then_inc(s_k, 1)
                dve.wait_ge(s_k, 7)
                dve.tensor_tensor(tmp[:], sv[:], v4[:, :, 2], ALU.mult).then_inc(s_k, 1)
                dve.wait_ge(s_k, 8)
                dve.tensor_tensor(tv[:], v4[:, :, 1], tmp[:], ALU.subtract).then_inc(s_k, 1)
                dve.wait_ge(s_k, 9)

                def add_x(n, b):
                    dve.wait_ge(s_rl, n * NBLK + b + 3)
                    dve.tensor_tensor(xblk(n, b), xblk(n, b), res[:, b % 2, :], ALU.add).then_inc(s_add, 1)

                for i, c in enumerate((c1, c2)):
                    dve.tensor_copy(w_hi[i][:], c[:]).then_inc(s_k, 1)
                    dve.wait_ge(s_k, 10 + 2 * i)
                    dve.tensor_tensor(w_lo[i][:], c[:], w_hi[i][:].bitcast(F32), ALU.subtract).then_inc(s_k, 1)

                with dve.Fori(0, B) as n:
                    for b in range(NBLK):
                        dve.wait_ge(s_c2, n * NBLK + b + 16)
                        dve.wait_ge(s_add, n * NBLK + b + (1 if b else 2))
                        rb = res[:, b % 2, :].rearrange("p (r c) -> p r c", c=W)
                        at = (slice(None), slice(1 + b * ROWS, 1 + (b + 1) * ROWS), slice(1, 1 + W))
                        dve.scalar_tensor_tensor(rb, bank[b][:, 0:BLK].rearrange("p (r c) -> p r c", c=W), sv[:, 1:2],
                                                 pz[0][at].bitcast(F32), ALU.mult, ALU.add).then_inc(s_r1, 1)
                        dve.wait_ge(s_r1, n * NBLK + b + 1)
                        dve.tensor_tensor(rb, rb, pz[1][at].bitcast(F32), ALU.add).then_inc(s_r, 1)
                        if b:
                            add_x(n, b - 1)
                    add_x(n, NBLK - 1)

            @block.tensor
            def _(pe):
                gn_tensor(pe, 3)
                pe.wait_ge(s_w, 160)

                pe.wait_ge(s_k, 13)

                def conv(b, i, src):
                    for k in range(9):
                        dy, dx = divmod(k, 3)
                        at = (slice(None), slice(b * ROWS + dy, b * ROWS + dy + ROWS), slice(dx, dx + W))
                        ins = split_product(pe, bank[b][:, 0:BLK], (w_hi[i][:, k, :], w_lo[i][:, k, :]),
                                            (src[0][at], src[1][at]), k == 0, k == 8)
                    return ins

                with pe.Fori(0, B) as n:
                    for b in range(NBLK):
                        pe.wait_ge(s_pz, n * NBLK + pad_blocks(b) + 3)
                        pe.wait_ge(s_r, n * NBLK + b + 2)
                        conv(b, 0, pz).then_inc(s_c1, 1)
                    for b in range(NBLK):
                        pe.wait_ge(s_m, n * NBLK + pad_blocks(b) + 9)
                        conv(b, 1, pm).then_inc(s_c2, 1)


def program(nc, a, out, last_stage=4):
    root = ExitStack()
    with root:
        def mk(ctx):
            def sb(n, s, d=F32):
                return ctx.enter_context(nc.sbuf_tensor(n, s, d))

            def ps(n, s, d=F32):
                return ctx.enter_context(nc.psum_tensor(n, s, d))

            def sem(n):
                return ctx.enter_context(nc.semaphore(n))
            return sb, ps, sem

        sb, psm, sem = mk(root)
        x_in = a["x"].rearrange("n c h w -> n c (h w)")
        x1_dram = nc.dram_tensor("x1_backup", [B, C, HW], F32, kind="Internal").ap()
        v_dram = nc.dram_tensor("v_windows", [B * P2, W2, C], F32, kind="Internal").ap()

        s_root = sem("groupnorm_root")
        s_passed = sem("waits_passed")
        s_w4 = sem("group_matrix_loaded")
        X = sb("X", [C, PAD + B * HW + L])
        bank = [psm(f"bank{i}", [128, 512]) for i in range(8)]
        t = {k: sb(k, [C, B]) for k in ("gn_gm", "gn_d", "gn_v")}
        t["group4"] = sb("group4", [C, C])
        mv = sb("mv", [C, B, 2])
        A = sb("A", [C, B])
        Bb = sb("Bb", [C, B])
        bn = sb("bn", [C, NBLK, 6])
        mv1 = sb("mv1", [C, 2])
        gm, gd, gv, group4 = t["gn_gm"], t["gn_d"], t["gn_v"], t["group4"]
        s_gd = sem("groupnorm_vector")
        s_gp = sem("groupnorm_tensor")
        s_mv1 = sem("image_aggregated")
        s_bst = sem("block_stats")
        s_mvw = sem("image_stats")

        def passed(e):
            e.sem_inc(s_passed, 1)

        def gn_tensor(e, g):
            e.wait_ge(s_mvw, B * (g + 1))
            e.wait_ge(s_w4, 16)
            e.matmul(bank[7][:, 0:B], group4[:], mv[:, :, 0], start=True, stop=True).then_inc(s_gp, 1)
            e.wait_ge(s_gd, GN_DVE * g + 4)
            e.matmul(bank[7][:, 0:B], group4[:], gv[:], start=True, stop=True).then_inc(s_gp, 1)

        def gn_vector(e, g):
            d0 = GN_DVE * g
            e.wait_ge(s_mvw, B * (g + 1))
            e.wait_ge(s_gp, GN_PE * g + 1)
            e.tensor_copy(gm[:], bank[7][:, 0:B]).then_inc(s_gd, 1)
            e.wait_ge(s_gd, d0 + 1)
            e.tensor_tensor(gd[:], mv[:, :, 0], gm[:], ALU.subtract).then_inc(s_gd, 1)
            e.wait_ge(s_gd, d0 + 2)
            e.tensor_tensor(gv[:], gd[:], gd[:], ALU.mult).then_inc(s_gd, 1)
            e.wait_ge(s_gd, d0 + 3)
            e.tensor_tensor(gv[:], gv[:], mv[:, :, 1], ALU.add).then_inc(s_gd, 1)
            e.wait_ge(s_gp, GN_PE * g + 2)
            e.tensor_scalar(gv[:], bank[7][:, 0:B], GN_EPS, None, ALU.add).then_inc(s_gd, 1)
            e.wait_ge(s_root, g + 1)
            rsqrt_vector(e, A[:], gv[:], gd[:], s_gd, d0 + 5)
            e.scalar_tensor_tensor(Bb[:], gm[:], -1.0, A[:], ALU.mult, ALU.mult).then_inc(s_gd, 1)
            e.wait_ge(s_gd, d0 + 11)

        def gn_scalar(e, g):
            e.wait_ge(s_gd, GN_DVE * g + 5)
            e.activation(A[:], gv[:], ACT.Sqrt).then_inc(s_root, 1)

        def image_stats(e, n, done):
            e.wait_ge(s_bst, done + 1)
            passed(e)
            e.bn_aggr(mv1[:], bn[:].rearrange("p b s -> p (b s)")).then_inc(s_mv1, 1)
            e.wait_ge(s_mv1, done + 1)
            e.tensor_copy(mv[:, bass.ds(n, 1), :], mv1[:].unsqueeze(1)).then_inc(s_mvw, 1)

        def xblk(n, b):
            return X[:, bass.ds(PAD + n * HW + b * BLK, BLK)]

        with ExitStack() as c0:
            sb, _, sem = mk(c0)
            s_ldx = [sem(f"x_loaded{n}") for n in range(B)]
            s_w = sem("weights_loaded")
            s_padz = sem("pads_zero")
            s_xb = sem("xb_ready")
            s_pq, s_pk, s_pv, s_pV = sem("q_product"), sem("k_product"), sem("v_product"), sem("vtok_product")
            s_q, s_k, s_v, s_V = sem("q_ready"), sem("k_ready"), sem("v_ready"), sem("vtok_ready")
            s_vh = sem("v_hi_ready")
            s_vst = [sem("v_stored_even"), sem("v_stored_odd")]
            s_qs = sem("window_sums")
            s_lg = sem("logits_product")
            s_tk = sem("topk_steps")
            s_row = sem("routes_ready")
            s_kg, s_Q, s_vg = sem("keys_gathered"), sem("queries_spread"), [sem(f"values_gathered{i}") for i in range(3)]
            s_S = sem("scores_product")
            s_mx, s_ex, s_rd = sem("score_max"), sem("exp_done"), sem("sum_reciprocal")
            s_nP = sem("probs_normalised")
            s_T, s_Tc = sem("probs_turned"), sem("turned_copied")
            s_O, s_o, s_om = sem("attended_product"), sem("attended_ready"), sem("attended_half")
            s_out, s_ev = sem("out_product"), sem("out_added")
            s_cst, s_cp = sem("consts_ready"), sem("consts_product")
            s_bak = sem("x1_saved")

            w_qkv = sb("w_qkv", [C, 3 * C])
            w_o = sb("w_o", [C, C])
            lw = sb("lw", [C, 9])
            w_tap = [sb(f"w_tap_{k}", [C, 9, C], F32R) for k in ("hi", "lo")]
            vec = sb("vec", [C, 6])
            cb = sb("cb", [C, 2])
            eo = sb("eo", [C, 2])
            hmask = sb("hmask", [C, HEADS, W2])
            ident = sb("ident", [C, C])
            qT = sb("qT", [C, HW])
            kT = sb("kT", [C, HW])
            oT = sb("oT", [C, HW])
            vpad = [sb(f"vpad_{k}", [C, H + 2, W + 2], F32R) for k in ("hi", "lo")]
            vst = sb("vst", [C, 2, 4, C])
            qs = sb("qs", [C, P2])
            ks = sb("ks", [C, P2])
            lg = sb("lg", [P2, P2])
            m8 = sb("m8", [P2, 8])
            ix = sb("ix", [P2, 8], U32)
            row = sb("row", [1, P2 * TOPK], U32)
            Qs = sb("Qs", [C, 2, HEADS * W2])
            kg = sb("kg", [C, 2, KEYS])
            vg = sb("vg", [C, 3, 2, C])
            Pr = sb("Pr", [C, 2, PAIRS, KEYS])
            PT = sb("PT", [C, 2, PAIRS * 2 * C])
            xb = PT[:, 0, 0:2 * BLK].rearrange("p (s k) -> p s k", s=2)
            nmx = sb("nmx", [C, 2, PAIRS])
            den = sb("den", [C, 2, PAIRS])
            rden = sb("rden", [C, 2, PAIRS])
            oh = sb("oh", [C, W2])

            NW = 10
            STORED = 32

            def routes(e, w):
                return nc.values_load_multi_w_load_instructions(
                    row[0:1, bass.ds(w * TOPK, TOPK)], engines=[e.engine], min_val=0, max_val=P2 - 1,
                    skip_runtime_bounds_check_because="positions among P2 values")[1]

            def fetch(e, source, r, slot):
                e.dma_start(vg[64 * (r % 2):64 * (r % 2) + 64, slot, r // 2, :],
                            v_dram[bass.ds(source, 1)].rearrange("u k c -> (u k) c")).then_inc(s_vg[slot], 16)

            with nc.Block() as block:
                @block.sync
                def _(sp):
                    sp.dma_start(group4[:], a["group4"]).then_inc(s_w4, 16)
                    for n in range(B):
                        sp.dma_start(X[:, PAD + n * HW:PAD + (n + 1) * HW], x_in[n]).then_inc(s_ldx[n], 16)
                    for dst, src in ((w_qkv[:], a["w_qkv"]), (w_o[:], a["w_o"]), (lw[:], a["lepe_w"]),
                                     (vec[:, 0:3], a["b_qkv"]), (vec[:, 3:4], a["lepe_b"]), (vec[:, 4:5], a["b_o"]),
                                     (eo[:], a["even_odd"]), (hmask[:, :, 0], a["head_mask"]),
                                     (ident[:], a["ident"]),
                                     (vec[:, 5:6], a["b_q"])):
                        sp.dma_start(dst, src, allow_slow_non_contiguous=True).then_inc(s_w, 16)
                    with sp.Fori(0, B) as n:
                        for b in range(NBLK):
                            sp.wait_ge(s_V, n * NBLK + b + 2)
                            passed(sp)
                            sp.dma_start(v_dram[bass.ds(n * P2 + b * NWIN, 6)].rearrange("(i u) k c -> (u k) i c", u=2),
                                         vst[:, b % 2, 0:3, :]).then_inc(s_vst[b % 2], 16)
                            sp.dma_start(v_dram[bass.ds(n * P2 + b * NWIN + 6, 1)].rearrange("u k c -> (u k) c"),
                                         vst[0:64, b % 2, 3, :]).then_inc(s_vst[b % 2], 16)
                        sp.wait_ge(s_tk, n * 3 + 4)
                        passed(sp)
                        sp.wait_ge(s_kg, (n * P2) + 1)
                        passed(sp)
                        sp.wait_ge(s_Tc, (n * P2) * 2 + 1)
                        passed(sp)
                        sp.dma_start(row[0:1, :], ix[:, 0:TOPK]).then_inc(s_row, 16)
                        sp.wait_ge(s_vst[0], n * (STORED * 4) + STORED * 4 + 16)
                        passed(sp)
                        sp.wait_ge(s_vst[1], n * (STORED * 3) + STORED * 3 + 16)
                        passed(sp)
                        sp.wait_ge(s_row, n * 16 + 32)
                        passed(sp)
                        sp.wait_ge(s_O, n * P2 + 3)
                        passed(sp)

                        def gather(w, slot):
                            idx = routes(sp, w)
                            sp.wait_ge(s_O, n * P2 + w + 1)
                            passed(sp)
                            for r in range(TOPK - 1):
                                fetch(sp, idx[r] + n * P2, r, slot)

                        with sp.Fori(0, P2 // 3) as k:
                            for i in range(3):
                                gather(k * 3 + i, i)
                        gather(P2 - 1, (P2 - 1) % 3)
                        sp.wait_ge(s_ev, n * NBLK + NBLK + 1)
                        passed(sp)
                        sp.dma_start(x1_dram[bass.ds(n, 1)].rearrange("u c k -> (u c) k"),
                                     X[:, bass.ds(PAD + n * HW, HW)]).then_inc(s_bak, 16)
                    sp.wait_ge(s_bak, 16 * B)

                @block.gpsimd
                def _(pool):
                    pool.memset(X[:, 0:PAD], 0.0).then_inc(s_padz, 1)
                    for k in range(2):
                        pool.memset(vpad[k][:].bitcast(F32), 0.0).then_inc(s_padz, 1)
                    for sm in (s_xb, s_V, s_tk, s_kg, s_S, s_O, s_T, s_ev, s_nP, s_ex, s_o, s_Tc, s_mx, s_Q):
                        pool.sem_inc(sm, 1)
                    pool.sem_inc(s_O, 2)
                    pool.sem_inc(s_S, PAIRS - 1)
                    pool.sem_inc(s_pV, 2)
                    pool.sem_inc(s_vst[0], 16)
                    pool.sem_inc(s_vst[1], 16)
                    pool.sem_inc(s_row, 16)
                    pool.wait_ge(s_cst, 21)
                    with pool.Fori(0, B) as n:
                        pool.wait_ge(s_row, n * 16 + 32)
                        pool.wait_ge(s_q, n * NBLK + NBLK)
                        pool.wait_ge(s_k, n * NBLK + NBLK)
                        passed(pool)

                        def window(w, par):
                            if not isinstance(w, int):
                                pool.wait_ge(s_S, (n * P2 + w) * PAIRS)
                            passed(pool)
                            for r, i in enumerate(routes(pool, w)):
                                ins = pool.tensor_copy(kg[:, par, r * W2:(r + 1) * W2], kT[:, bass.ds(i * W2, W2)])
                            ins.then_inc(s_kg, 1)
                            pool.tensor_tensor(Qs[:, par, :].rearrange("p (h k) -> p h k", h=HEADS),
                                               qT[:, bass.ds(w * W2, W2)].unsqueeze(1).to_broadcast([C, HEADS, W2]),
                                               hmask[:], ALU.mult).then_inc(s_Q, 1)

                        pool.wait_ge(s_S, n * (P2 * PAIRS) + PAIRS)
                        passed(pool)
                        window(0, 0)
                        with pool.Fori(0, (P2 - 1) // 2) as k:
                            window(k * 2 + 1, 1)
                            window(k * 2 + 2, 0)
                    pool.wait_ge(s_S, (B * P2 + 1) * PAIRS)

                @block.scalar
                def _(act):
                    def evac_act(act, n, b):
                        par = b % 2
                        act.wait_ge(s_pq, n * NBLK + b + 1)
                        act.wait_ge(s_Q, n * P2 + 1)
                        act.activation(qT[:, b * BLK:(b + 1) * BLK], bank[4 * par][:, 0:BLK], ACT.Identity,
                                       bias=vec[:, 5:6], scale=QSCALE).then_inc(s_q, 1)
                        act.wait_ge(s_pV, n * NBLK + b + 3)
                        act.wait_ge(s_vst[par], n * (STORED * (4 - par)) + STORED * (b // 2) + 16)
                        act.activation(vst[:, par, 0:3, :], bank[4 * par + 3][:, 0:384].rearrange("p (i c) -> p i c", c=C),
                                       ACT.Copy)
                        act.activation(vst[0:64, par, 3, :], bank[4 * par + 3][0:64, 384:512], ACT.Copy).then_inc(s_V, 1)

                    gn_scalar(act, 0)
                    act.wait_ge(s_cst, 21)
                    act.wait_ge(s_gd, GN_DVE)
                    with act.Fori(0, B) as n:
                        act.wait_ge(s_O, n * P2 + 3)
                        for b in range(NBLK):
                            act.wait_ge(s_pV, n * NBLK + b + 1)
                            xw = xblk(n, b).rearrange("p (r w c) -> p w r c", r=ROWS, c=WIN)
                            act.activation(xb[:, b % 2, :].rearrange("p (w r c) -> p w r c", r=ROWS, c=WIN), xw,
                                           ACT.Identity, bias=Bb[:, bass.ds(n, 1)], scale=A[:, bass.ds(n, 1)])\
                                .then_inc(s_xb, 1)
                            if b >= 1:
                                evac_act(act, n, b - 1)
                        evac_act(act, n, NBLK - 1)

                        def exps(w, par):
                            if not isinstance(w, int):
                                act.wait_ge(s_T, n * P2 + w)
                            for j in range(PAIRS):
                                act.wait_ge(s_mx, (n * P2 + w) * PAIRS + j + 2)
                                act.activation(Pr[:, par, j, :], bank[j][:, 0:KEYS], ACT.Exp,
                                               bias=nmx[:, par, j:j + 1], accum_out=den[:, par, j:j + 1])\
                                    .then_inc(s_ex, 1)

                        def turned(w, par):
                            act.wait_ge(s_T, n * P2 + w + 2)
                            act.wait_ge(s_O, n * P2 + w + 2)
                            for i in range(2):
                                act.activation(PT[:, par, i * 512:(i + 1) * 512], bank[4 + i][:], ACT.Copy)\
                                    .then_inc(s_Tc, 1)

                        def fourth(w, slot):
                            idx = routes(act, w)
                            fetch(act, idx[TOPK - 1] + n * P2, TOPK - 1, slot)

                        act.wait_ge(s_vst[0], n * (STORED * 4) + STORED * 4 + 16)
                        passed(act)
                        act.wait_ge(s_vst[1], n * (STORED * 3) + STORED * 3 + 16)
                        passed(act)
                        act.wait_ge(s_row, n * 16 + 32)
                        passed(act)
                        fourth(0, 0)

                        act.wait_ge(s_T, n * P2 + 1)
                        exps(0, 0)
                        with act.Fori(0, (P2 - 1) // 6) as k:
                            for i in range(6):
                                exps(k * 6 + i + 1, (i + 1) % 2)
                                turned(k * 6 + i, i % 2)
                                fourth(k * 6 + i + 1, (i + 1) % 3)
                        turned(P2 - 1, 0)

                @block.vector
                def _(dve):
                    for n in range(B):
                        dve.wait_ge(s_ldx[n], 16)
                        if n:
                            dve.wait_ge(s_mvw, n)
                        for b in range(NBLK):
                            ins = dve.bn_stats(bn[:, b, :], X[:, PAD + n * HW + b * BLK:PAD + n * HW + (b + 1) * BLK])
                        ins.then_inc(s_bst, 1)
                        image_stats(dve, n, n)
                    dve.wait_ge(s_mvw, B)
                    dve.wait_ge(s_w, 16 * NW)
                    dve.tensor_scalar(vec[:, 5:6], vec[:, 5:6], QSCALE, None, ALU.mult).then_inc(s_cst, 1)
                    dve.tensor_copy(hmask[:, :, 1:W2], hmask[:, :, 0:1].to_broadcast([C, HEADS, W2 - 1]))\
                        .then_inc(s_cst, 1)
                    for k in range(9):
                        dve.tensor_scalar(w_tap[0][:, k, :], w_o[:], lw[:, k:k + 1], None, ALU.mult).then_inc(s_cst, 1)
                        dve.wait_ge(s_cst, 2 * k + 3)
                        dve.scalar_tensor_tensor(w_tap[1][:, k, :], w_o[:], lw[:, k:k + 1],
                                                 w_tap[0][:, k, :].bitcast(F32), ALU.mult, ALU.subtract)\
                            .then_inc(s_cst, 1)
                    dve.tensor_tensor(cb[:, 0:1], vec[:, 2:3], vec[:, 3:4], ALU.add).then_inc(s_cst, 1)
                    gn_vector(dve, 0)
                    dve.wait_ge(s_cp, 1)
                    dve.tensor_tensor(cb[:, 1:2], bank[1][:, 0:1], vec[:, 4:5], ALU.add).then_inc(s_cst, 1)
                    dve.wait_ge(s_cst, 22)
                    dve.wait_ge(s_padz, 3)
                    with dve.Fori(0, B) as n:
                        for b in range(NBLK):
                            par = b % 2
                            dve.wait_ge(s_pk, n * NBLK + b + 1)
                            dve.wait_ge(s_kg, n * P2 + 1)
                            dve.tensor_scalar(kT[:, b * BLK:(b + 1) * BLK], bank[4 * par + 1][:, 0:BLK], vec[:, 1:2],
                                              None, ALU.add).then_inc(s_k, 1)
                            dve.wait_ge(s_pv, n * NBLK + b + 1)
                            vp = [v[:, 1 + b * ROWS:1 + (b + 1) * ROWS, 1:1 + W] for v in vpad]
                            vps = bank[4 * par + 2][:, 0:BLK].rearrange("p (r c) -> p r c", c=W)
                            dve.tensor_scalar(vp[0], vps, vec[:, 2:3], None, ALU.add).then_inc(s_vh, 1)
                            dve.wait_ge(s_k, n * NBLK + b + 1)
                            dve.tensor_reduce(ks[:, b * NWIN:(b + 1) * NWIN], kT[:, b * BLK:(b + 1) * BLK]
                                              .rearrange("p (w k) -> p w k", k=W2), AXX, ALU.add).then_inc(s_qs, 1)
                            dve.wait_ge(s_vh, n * NBLK + b + 1)
                            dve.scalar_tensor_tensor(vp[1], vps, vec[:, 2:3], vp[0].bitcast(F32), ALU.add, ALU.subtract)\
                                .then_inc(s_v, 1)
                            dve.wait_ge(s_q, n * NBLK + b + 1)
                            dve.tensor_reduce(qs[:, b * NWIN:(b + 1) * NWIN], qT[:, b * BLK:(b + 1) * BLK]
                                              .rearrange("p (w k) -> p w k", k=W2), AXX, ALU.add).then_inc(s_qs, 1)
                        dve.wait_ge(s_lg, n + 1)
                        dve.tensor_scalar(lg[:], bank[0][0:P2, 0:P2], 1.0 / (W2 * W2), None, ALU.mult).then_inc(s_tk, 1)
                        dve.wait_ge(s_tk, n * 3 + 2)
                        passed(dve)
                        dve.max(m8[:], lg[:]).then_inc(s_tk, 1)
                        dve.wait_ge(s_tk, n * 3 + 3)
                        dve.wait_ge(s_row, n * 16 + 16)
                        passed(dve)
                        dve.max_index(ix[:], m8[:], lg[:]).then_inc(s_tk, 1)

                        def maxes(w, par):
                            for j in range(PAIRS):
                                dve.wait_ge(s_S, (n * P2 + w + 1) * PAIRS + j + 1)
                                dve.tensor_reduce(nmx[:, par, j:j + 1], bank[j][:, 0:KEYS], AXX, ALU.max, negate=True)\
                                    .then_inc(s_mx, 1)

                        def norm(w, par, att=None):
                            for i in range(2):
                                dve.wait_ge(s_ex, (n * P2 + w) * PAIRS + 2 * i + 3)
                                dve.reciprocal(rden[:, par, 2 * i:2 * i + 2], den[:, par, 2 * i:2 * i + 2])\
                                    .then_inc(s_rd, 1)
                                if i == 0 and att is not None:
                                    dve.wait_ge(s_O, n * P2 + att + 4)
                                    dve.wait_ge(s_o, n * P2 + att + 1)
                                    dve.tensor_scalar(oh[:], bank[6][:, 0:W2], eo[:, 0:1], None, ALU.mult)\
                                        .then_inc(s_om, 1)
                                dve.wait_ge(s_rd, (n * P2 + w) * 2 + i + 1)
                                for j in (2 * i, 2 * i + 1):
                                    ins = dve.tensor_scalar(Pr[:, par, j, :], Pr[:, par, j, :],
                                                            rden[:, par, j:j + 1], None, ALU.mult)
                                if i == 0 and att is not None:
                                    second(att)
                            ins.then_inc(s_nP, 1)

                        def second(w):
                            dve.wait_ge(s_om, n * P2 + w + 1)
                            dve.scalar_tensor_tensor(oT[:, bass.ds(w * W2, W2)], bank[6][:, W2:2 * W2], eo[:, 1:2],
                                                     oh[:], ALU.mult, ALU.add).then_inc(s_o, 1)

                        def attended(w):
                            dve.wait_ge(s_O, n * P2 + w + 4)
                            dve.wait_ge(s_o, n * P2 + w + 1)
                            dve.tensor_scalar(oh[:], bank[6][:, 0:W2], eo[:, 0:1], None, ALU.mult).then_inc(s_om, 1)
                            second(w)

                        maxes(0, 0)
                        norm(0, 0)
                        maxes(1, 1)
                        norm(1, 1)
                        with dve.Fori(0, (P2 - 3) // 2) as k:
                            maxes(k * 2 + 2, 0)
                            norm(k * 2 + 2, 0, k * 2)
                            maxes(k * 2 + 3, 1)
                            norm(k * 2 + 3, 1, k * 2 + 1)
                        maxes(P2 - 1, 0)
                        norm(P2 - 1, 0, P2 - 3)
                        attended(P2 - 2)
                        attended(P2 - 1)
                        dve.wait_ge(s_mvw, n + B)
                        for b in range(NBLK):
                            dve.wait_ge(s_out, n * NBLK + b + 1)
                            dve.scalar_tensor_tensor(xblk(n, b), bank[b][:, 0:BLK], cb[:, 1:2], xblk(n, b),
                                                     ALU.add, ALU.add).then_inc(s_ev, 1)
                            dve.wait_ge(s_ev, n * NBLK + b + 2)
                            passed(dve)
                            ins = dve.bn_stats(bn[:, b, :], xblk(n, b))
                        ins.then_inc(s_bst, 1)
                        image_stats(dve, n, n + B)

                @block.tensor
                def _(pe):
                    gn_tensor(pe, 0)
                    pe.wait_ge(s_cst, 21)
                    pe.matmul(bank[1][:, 0:1], w_o[:], cb[:, 0:1], start=True, stop=True).then_inc(s_cp, 1)
                    pe.wait_ge(s_cst, 22)
                    pe.wait_ge(s_gd, GN_DVE)
                    pe.wait_ge(s_padz, 3)
                    with pe.Fori(0, B) as n:
                        pe.wait_ge(s_ev, n * NBLK + 1)
                        for b in range(NBLK):
                            par = b % 2
                            xs = xb[:, par, :]
                            bq, bk, bv, bV = bank[4 * par:4 * par + 4]
                            pe.wait_ge(s_xb, n * NBLK + b + 2)
                            if b >= 2:
                                pe.wait_ge(s_q, n * NBLK + b - 1)
                                pe.wait_ge(s_k, n * NBLK + b - 1)
                                pe.wait_ge(s_v, n * NBLK + b - 1)
                                pe.wait_ge(s_V, n * NBLK + b)
                            pe.matmul(bq[:, 0:BLK], w_qkv[:, 0:C], xs, start=True, stop=True).then_inc(s_pq, 1)
                            pe.matmul(bk[:, 0:BLK], w_qkv[:, C:2 * C], xs, start=True, stop=True).then_inc(s_pk, 1)
                            pe.matmul(bv[:, 0:BLK], w_qkv[:, 2 * C:3 * C],
                                      xs.rearrange("p (w r c) -> p r w c", r=ROWS, c=WIN), start=True, stop=True)\
                                .then_inc(s_pv, 1)
                            for i in range(4):
                                m = 128 if i < 3 else 64
                                ins = pe.matmul(bV[0:m, i * C:(i + 1) * C], xs[:, i * 128:i * 128 + m],
                                                w_qkv[:, 2 * C:3 * C], start=True, stop=True)
                            ins.then_inc(s_pV, 1)
                        pe.wait_ge(s_qs, (n + 1) * (2 * NBLK))
                        pe.matmul(bank[0][0:P2, 0:P2], qs[:], ks[:], start=True, stop=True).then_inc(s_lg, 1)
                        pe.wait_ge(s_V, n * NBLK + NBLK + 1)
                        pe.wait_ge(s_v, n * NBLK + NBLK)
                        pe.wait_ge(s_tk, n * 3 + 2)

                        def scores(w, par):
                            pe.wait_ge(s_kg, n * P2 + w + 2)
                            pe.wait_ge(s_Q, n * P2 + w + 2)
                            for j in range(PAIRS):
                                if not (isinstance(w, int) and w == 0):
                                    pe.wait_ge(s_ex, (n * P2 + w - 1) * PAIRS + j + 2)
                                pe.matmul(bank[j][:, 0:KEYS], Qs[:, par, j * C:(j + 1) * C], kg[:, par, :],
                                          start=True, stop=True).then_inc(s_S, 1)

                        def turn(w, par):
                            pe.wait_ge(s_nP, n * P2 + w + 2)
                            pe.wait_ge(s_Tc, (n * P2 + w) * 2 + 1)
                            for j in range(PAIRS):
                                for c in range(2):
                                    ins = pe.transpose(bank[4 + j // 2][:, (j % 2 * 2 + c) * C:(j % 2 * 2 + c + 1) * C],
                                                       Pr[:, par, j, c * C:(c + 1) * C], ident[:])
                            ins.then_inc(s_T, 1)

                        def attend(w, par, slot, third):
                            pe.wait_ge(s_Tc, (n * P2 + w) * 2 + 3)
                            pe.wait_ge(s_vg[slot], (n * (17 if slot == 0 else 16) + third) * 64 + 64)
                            pe.wait_ge(s_o, n * P2 + w + 1)
                            for j in range(PAIRS):
                                for c in range(2):
                                    ins = pe.matmul(bank[6][32 * j:32 * j + 32, 0:C],
                                                    vg[:, slot, c, 32 * j:32 * j + 32],
                                                    PT[:, par, (2 * j + c) * C:(2 * j + c + 1) * C],
                                                    start=(c == 0), stop=(c == 1))
                            ins.then_inc(s_O, 1)

                        scores(0, 0)
                        scores(1, 1)
                        turn(0, 0)
                        def three(w, i, third):
                            scores(w, i % 2)
                            attend(w - 2, i % 2, i % 3, third)
                            turn(w - 1, (i + 1) % 2)
                        NR = (P2 - 2) // 6
                        with pe.Fori(0, NR) as k:
                            for i in range(6):
                                three(k * 6 + 2 + i, i, k * 2 + i // 3)
                        for i in range((P2 - 2) % 6):
                            three(NR * 6 + 2 + i, i, NR * 2 + i // 3)
                        attend(P2 - 2, 1, (P2 - 2) % 3, (P2 - 2) // 3)
                        turn(P2 - 1, 0)
                        attend(P2 - 1, 0, (P2 - 1) % 3, (P2 - 1) // 3)
                        pe.wait_ge(s_o, n * P2 + P2 + 1)
                        for b in range(NBLK):
                            ps3 = bank[b][:, 0:BLK]
                            pe.matmul(ps3, w_o[:], oT[:, b * BLK:(b + 1) * BLK]
                                      .rearrange("p (w r c) -> p r w c", r=ROWS, c=WIN), start=True, stop=False)
                            for k in range(9):
                                dy, dx = divmod(k, 3)
                                at = (slice(None), slice(b * ROWS + dy, b * ROWS + dy + ROWS), slice(dx, dx + W))
                                ins = split_product(pe, ps3, (w_tap[0][:, k, :], w_tap[1][:, k, :]),
                                                    (vpad[0][at], vpad[1][at]), False, k == 8)
                            ins.then_inc(s_out, 1)

        if last_stage > 1:
            rnn(nc, mk, {**a, "_mv": mv}, X, bank, A, Bb, gn_tensor, gn_vector, gn_scalar, x1_dram, s_gd, passed)
        if last_stage > 2:
            masked_conv(nc, mk, a, X, bank, A, Bb, gn_tensor, gn_vector, gn_scalar, s_gd, bn, s_bst, s_mvw, image_stats,
                        xblk, passed)
        if last_stage > 3:
            conv_pair(nc, mk, a, X, bank, A, Bb, gn_tensor, gn_vector, gn_scalar, xblk, passed, s_gd, out)
        else:
            with nc.semaphore("stored") as s_st, nc.Block() as block:
                @block.sync
                def _(sp):
                    sp.dma_start(out.rearrange("n c h w -> c n (h w)"),
                                 X[:, PAD:PAD + B * HW].rearrange("p (n k) -> p n k", n=B)).then_inc(s_st, 16)
                    sp.wait_ge(s_st, 16)


LAST_STAGE = 4


def kernel(**inputs):
    import numpy as np
    import concourse.bacc as bacc
    from concourse.bass_utils import run_bass_kernel_spmd

    def cols(v, n):
        return v.reshape(n, 128).T

    i = {k: np.asarray(v) for k, v in inputs.items()}
    ch = np.arange(128)
    one = np.float32(1)
    laid = {
        "x": i["x"],
        "w_qkv": i["L0_conv_W_qkv"],
        "b_qkv": cols(i["L0_conv_b_qkv"], 3),
        "b_q": i["L0_conv_b_qkv"][0:128].reshape(128, 1),
        "lepe_w": i["L0_conv_lepe_w"].reshape(128, 9),
        "lepe_b": i["L0_conv_lepe_b"].reshape(128, 1),
        "w_o": i["L0_conv_W_o"],
        "b_o": i["L0_conv_b_o"].reshape(128, 1),
        "gamma": i["L1_conv_gamma"].reshape(128, 1),
        "beta": i["L1_conv_beta"].reshape(128, 1),
        "w_in": i["L1_conv_w_in"].T,
        "b_in": cols(i["L1_conv_b_in"], 2),
        "w_ih": i["L1_conv_w_ih"].T.reshape(2, 128, 512).transpose(1, 0, 2),
        "b_ih": cols(i["L1_conv_b_ih"], 4),
        "w_hh": i["L1_conv_w_hh"].T.reshape(4, 128, 512).transpose(1, 0, 2),
        "b_hh": cols(i["L1_conv_b_hh"], 4),
        "w_out": i["L1_conv_w_out"].T.reshape(4, 128, 128).transpose(1, 0, 2),
        "b_out": i["L1_conv_b_out"].reshape(128, 1),
        "w3": i["L2_conv_w3"].transpose(1, 2, 3, 0).reshape(128, 9, 128),
        "w1": i["L2_conv_w1"].T,
        "b2": i["L2_conv_b"],
        "c1": i["L3_conv_w1"].transpose(1, 2, 3, 0).reshape(128, 9, 128),
        "c2": i["L3_conv_w2"].transpose(1, 2, 3, 0).reshape(128, 9, 128),
        "g1": i["L3_conv_gamma1"].reshape(128, 1), "h1": i["L3_conv_beta1"].reshape(128, 1),
        "m1": i["L3_conv_mean1"].reshape(128, 1), "v1": i["L3_conv_var1"].reshape(128, 1),
        "g2": i["L3_conv_gamma2"].reshape(128, 1), "h2": i["L3_conv_beta2"].reshape(128, 1),
        "m2": i["L3_conv_mean2"].reshape(128, 1), "v2": i["L3_conv_var2"].reshape(128, 1),
        "ident": np.eye(128, dtype=np.float32),
        "group4": (ch[:, None] // GROUP == ch[None, :] // GROUP).astype(np.float32) / np.float32(GROUP),
        "even_odd": np.stack([ch // HD % 2 == 0, ch // HD % 2 == 1], 1).astype(np.float32),
        "head_mask": (ch[:, None] // HD == np.arange(HEADS)[None, :]).astype(np.float32),
        "on_grid": ((ch[:, None] - ch[None, :]) % 4 == 0).astype(np.float32),
        "off_grid": ((ch[:, None] - ch[None, :]) % 4 != 0).astype(np.float32),
        "ones": np.full((128, 1), one),
    }
    nc = bacc.Bacc("TRN2", target_bir_lowering=False, num_devices=1)
    arrays, aps = {}, {}
    for k, v in laid.items():
        v = np.ascontiguousarray(v)
        arrays[f"in_{k}"] = v
        aps[k] = nc.dram_tensor(f"in_{k}", v.shape, F32, kind="ExternalInput").ap()
    out = nc.dram_tensor("out_0", (B, C, H, W), F32, kind="ExternalOutput").ap()
    program(nc, aps, out, LAST_STAGE)
    r = run_bass_kernel_spmd(nc, [arrays], core_ids=[0])
    return r.results[0]["out_0"]
```

```python
import concourse.bass as bass
from concourse import mybir
from contextlib import ExitStack

F32 = mybir.dt.float32
F32R = mybir.dt.float32r
U32 = mybir.dt.uint32
ACT = mybir.ActivationFunctionType
ALU = mybir.AluOpType
AXX = mybir.AxisListType.X

B, C, H, W = 8, 128, 56, 56
HW = H * W
ROWS = 8
BLK = ROWS * W
NBLK = H // ROWS
GROUP = 4
GN_EPS = 1e-5
NWIN = 7
WIN = H // NWIN
P2 = NWIN * NWIN
W2 = WIN * WIN
HEADS = 8
HD = C // HEADS
TOPK = 4
KEYS = TOPK * W2
PAIRS = HEADS // 2
QSCALE = float(C) ** -0.5
RIN, RH = 256, 512
NI, NH = RIN // 128, RH // 128
SEG = 16
L = HW // SEG
WARM = 64
COLS = B * SEG
PAD = WARM
HANDOVER_TOL = 2.0 ** -17
PW = WARM // 2
PM = L // 2
STAT = L // NBLK
BN_EPS = 1e-5
BN_STEPS = 23


GN_DVE, GN_PE = 11, 2
IN_DVE = 12


def rsqrt_vector(e, r, v, tmp, done, d0):
    e.wait_ge(done, d0)
    e.reciprocal(r, r).then_inc(done, 1)
    e.wait_ge(done, d0 + 1)
    e.tensor_tensor(tmp, v, r, ALU.mult).then_inc(done, 1)
    e.wait_ge(done, d0 + 2)
    e.tensor_tensor(tmp, tmp, r, ALU.mult).then_inc(done, 1)
    e.wait_ge(done, d0 + 3)
    e.tensor_scalar(tmp, tmp, -0.5, 1.5, ALU.mult, ALU.add).then_inc(done, 1)
    e.wait_ge(done, d0 + 4)
    e.tensor_tensor(r, r, tmp, ALU.mult).then_inc(done, 1)
    e.wait_ge(done, d0 + 5)


def rnn(nc, mk, a, X, bank, A, Bb, gn_tensor, gn_vector, gn_scalar, x1_dram, s_gd, s_mvw, passed):
    CH = 2 * COLS
    with ExitStack() as ctx:
        sb, _, sem = mk(ctx)
        w_in = sb("w_in", [C, RIN])
        w_ih = sb("w_ih", [128, NI, RH])
        w_hh = sb("w_hh", [128, NH, RH])
        w_out = sb("w_out", [128, NH, C])
        vecs = sb("vecs", [C, 3])
        b_in = sb("b_in", [128, NI])
        bg = sb("bg", [128, 2, NH])
        ones = sb("ones", [128, 1])
        e1, e2, mu = sb("e1", [C, B]), sb("e2", [C, B]), sb("mu", [C, 4])
        A2 = sb("A2", [C, B, SEG])
        B2 = sb("B2", [C, B, SEG])
        mvp = sb("mvp", [C, B, 2])
        pin = [sb(f"w_in_{k}", [C, RIN], F32R) for k in ("hi", "lo")]
        pih = [sb(f"w_ih_{k}", [128, NI, RH], F32R) for k in ("hi", "lo")]
        pout = [sb(f"w_out_{k}", [128, NH, C], F32R) for k in ("hi", "lo")]
        xa = sb("xa", [C, 2, COLS])
        xp = [sb(f"xa_{k}", [C, 2, 2, COLS], F32R) for k in ("hi", "lo")]
        tz = sb("tz", [128, 2, NI, CH])
        inp = sb("inp", [128, NI, CH])
        ip = [sb(f"inp_{k}", [128, 2, NI, CH], F32R) for k in ("hi", "lo")]
        h = sb("h", [128, 4, NH, COLS])
        hp = [sb(f"h_{k}", [128, 4, NH, COLS], F32R) for k in ("hi", "lo")]
        start = sb("start", [128, NH, COLS])
        okc = sb("okc", [128, 2])
        flag = sb("flag", [1, 1], U32)
        s_w = sem("rnn_weights_loaded")
        s_bn = sem("batchnorm_steps")
        s_bnr = sem("batchnorm_root")
        s_xm = sem("x_scaled")
        s_xa = sem("x_normalised")
        s_pre, s_tz, s_inp = sem("pre_product"), sem("pre_tanh"), sem("input_ready")
        s_i32, s_ihi = sem("input_formed"), sem("input_hi_ready")
        s_g, s_h = sem("gates_product"), sem("state_ready")
        s_hhi, s_sp = sem("state_hi_ready"), sem("state_split")
        s_wh, s_ws = sem("weights_hi_ready"), sem("weights_split")
        s_st = sem("x2_piece_stats")
        x2s = sb("x2_stats", [C, B * NBLK * 6])
        s_y, s_yd = sem("y_product"), sem("y_added")
        s_seed = sem("start_states")
        s_ver, s_verp, s_flag = sem("verify_steps"), sem("verify_product"), sem("verdict_ready")
        s_rel = sem("x1_reloaded")
        mvi = a["_mv"]

        def xcols(tok, k=2):
            return X[:, bass.ds(tok, COLS * L)].rearrange("p (c l) -> p l c", l=L)[:, 0:k, :]

        def pre_product(pe, P, q):
            pe.wait_ge(s_xa, P + 2)
            pe.wait_ge(s_inp, P + 1)
            x = [v[:, q].rearrange("p t c -> p (t c)") for v in xp]
            for i in range(NI):
                ins = split_product(pe, bank[4 + q][:, i * CH:(i + 1) * CH], [w[:, i * 128:(i + 1) * 128] for w in pin],
                                    x, True, True)
            ins.then_inc(s_pre, 1)

        def y_product(pe, Y, q):
            pe.wait_ge(s_yd, Y + 1)
            pe.wait_ge(s_sp, Y * 2 + 6)
            for k in range(NH):
                ins = split_product(pe, bank[6 + q][:, 0:CH], [w[:, k, :] for w in pout],
                                    [v[:, 2 * q:2 * q + 2, k, :] for v in hp], k == 0, k == NH - 1)
            ins.then_inc(s_y, 1)

        def tensor_pair(pe, P, q, y=None, more=True, seed=None):
            pe.wait_ge(s_inp, P + 3)
            for m in range(NH):
                pe.wait_ge(s_h, P * 8 + m + 1)
                for i in range(NI):
                    split_product(pe, bank[m][:, 0:CH], [w[:, i, m * 128:(m + 1) * 128] for w in pih],
                                  [v[:, q, i, :] for v in ip], i == 0, False)
            if seed is not None:
                pe.wait_ge(s_seed, seed)
            for tt in range(2):
                prev = (2 * q + tt - 1) % 4
                for m in range(NH):
                    for k in range(NH):
                        if tt == 1 and m == 0:
                            pe.wait_ge(s_h, P * 8 + 4 + k + 1)
                        ins = pe.matmul(bank[m][:, tt * COLS:(tt + 1) * COLS], w_hh[:, k, m * 128:(m + 1) * 128],
                                        h[:, prev, k, :], start=False, stop=(k == NH - 1),
                                        skip_group_check=(tt == 1))
                    ins.then_inc(s_g, 1)
                if tt == 0:
                    if more:
                        pre_product(pe, P + 1, 1 - q)
                    if y is not None:
                        y_product(pe, y, 1 - q)

        def pre_tanh(act, P, q):
            act.wait_ge(s_pre, P + 3)
            act.wait_ge(s_inp, P + 1)
            for i in range(NI):
                act.activation(tz[:, q, i, :], bank[4 + q][:, i * CH:(i + 1) * CH], ACT.Tanh, bias=b_in[:, i:i + 1])\
                    .then_inc(s_tz, 1)

        def scalar_pair(act, P, q, Y=None, more=True):
            for tt in range(2):
                if Y is not None:
                    act.wait_ge(s_sp, Y * 2 + tt + 1)
                for m in range(NH):
                    act.wait_ge(s_g, P * 8 + tt * 4 + m + 17)
                    act.activation(h[:, 2 * q + tt, m, :], bank[m][:, tt * COLS:(tt + 1) * COLS], ACT.Tanh,
                                   bias=bg[:, 0, m:m + 1]).then_inc(s_h, 1)
                if more and tt == 0:
                    pre_tanh(act, P + 1, 1 - q)

        def split_pair(pool, P, Y, q):
            pool.wait_ge(s_yd, Y + 1)
            for tt in range(2):
                pool.wait_ge(s_h, P * 8 + tt * 4 + 8)
                passed(pool)
                pool.tensor_copy(hp[0][:, 2 * q + tt], h[:, 2 * q + tt]).then_inc(s_hhi, 1)
                pool.wait_ge(s_hhi, Y * 2 + tt + 1)
                passed(pool)
                pool.tensor_tensor(hp[1][:, 2 * q + tt], h[:, 2 * q + tt], hp[0][:, 2 * q + tt].bitcast(F32),
                                   ALU.subtract).then_inc(s_sp, 1)

        def normalise(dve, P, q, tok):
            dve.wait_ge(s_xa, P + 1)
            dve.tensor_tensor(xa[:], xcols(tok), A2[:].rearrange("p n s -> p (n s)").unsqueeze(1)
                              .to_broadcast([C, 2, COLS]), ALU.mult).then_inc(s_xm, 1)
            dve.wait_ge(s_xm, P * 3 + 1)
            dve.tensor_tensor(xa[:], xa[:], B2[:].rearrange("p n s -> p (n s)").unsqueeze(1)
                              .to_broadcast([C, 2, COLS]), ALU.add).then_inc(s_xm, 1)
            dve.wait_ge(s_pre, P + 1)
            dve.wait_ge(s_xm, P * 3 + 2)
            dve.tensor_copy(xp[0][:, q], xa[:]).then_inc(s_xm, 1)
            dve.wait_ge(s_xm, P * 3 + 3)
            dve.tensor_tensor(xp[1][:, q], xa[:], xp[0][:, q].bitcast(F32), ALU.subtract).then_inc(s_xa, 1)

        def shrink(dve, P, q):
            dve.wait_ge(s_inp, P + 2)
            dve.wait_ge(s_tz, P * 2 + 2)
            for i in range(NI):
                dve.scalar_tensor_tensor(inp[:, i, :], bank[4 + q][:, i * CH:(i + 1) * CH], b_in[:, i:i + 1],
                                         tz[:, q, i, :], ALU.add, ALU.subtract).then_inc(s_i32, 1)
            dve.wait_ge(s_g, P * 8 + 8)
            dve.wait_ge(s_i32, P * 2 + 2)
            dve.tensor_copy(ip[0][:, q], inp[:]).then_inc(s_ihi, 1)
            dve.wait_ge(s_ihi, P + 1)
            dve.tensor_tensor(ip[1][:, q], inp[:], ip[0][:, q].bitcast(F32), ALU.subtract).then_inc(s_inp, 1)

        def add_y(dve, Y, q, tok):
            dve.wait_ge(s_y, Y + 1)
            dve.scalar_tensor_tensor(xcols(tok), bank[6 + q][:, 0:CH].rearrange("p (t c) -> p t c", t=2), vecs[:, 2:3],
                                     xcols(tok), ALU.add, ALU.add).then_inc(s_yd, 1)

        def vector_pair(dve, P, q, tok, y=None, more=2):
            if more > 0:
                shrink(dve, P + 1, 1 - q)
            if y is not None:
                add_y(dve, y, 1 - q, tok - 2)
            if more > 1:
                normalise(dve, P + 2, q, tok + 4)

        PA = PW + PM
        RND, RNDW = PA // 2, PW // 2

        def run(e, first, P0, Y0, tok0, warm, seed, lead, body, tail):
            lead()
            if warm:
                with e.Fori(0, warm) as k:
                    body(k, False, False, None, False)
            body(warm, False, True, seed, False)
            with e.Fori(warm + 1, warm + PM // 2 - 1) as k:
                body(k, True, True, None, False)
            body(warm + PM // 2 - 1, True, True, None, True)
            tail(warm + PM // 2 - 1)

        def run_tensor(pe, P0, Y0, warm, seed):
            def body(k, y0, y1, sd, last):
                P = P0 + k * 2
                Y = Y0 + k * 2 - 2 * warm
                tensor_pair(pe, P, 0, Y - 1 if y0 else None, True, sd)
                tensor_pair(pe, P + 1, 1, Y if y1 else None, not last)

            def tail(k):
                y_product(pe, Y0 + 2 * k - 2 * warm + 1, 1)
            run(pe, None, P0, Y0, None, warm, seed, lambda: pre_product(pe, P0, 0), body, tail)

        def run_scalar(act, P0, Y0, warm):
            def body(k, y0, y1, sd, last):
                P = P0 + k * 2
                Y = Y0 + k * 2 - 2 * warm
                scalar_pair(act, P, 0, Y if y1 else None)
                scalar_pair(act, P + 1, 1, Y + 1 if y1 else None, not last)
            run(act, None, P0, Y0, None, warm, None, lambda: pre_tanh(act, P0, 0), body, lambda k: None)

        def piece_stats(dve, n, piece, Y0):
            dve.wait_ge(s_yd, piece * (STAT // 2) + (Y0 + STAT // 2 + 2))
            passed(dve)
            dve.bn_stats(x2s[:, bass.ds((n * NBLK + piece) * 6, 6)],
                         X[:, bass.ds(PAD + n * HW + piece * STAT, HW)].rearrange("p (s l) -> p s l", l=L)[:, :, 0:STAT])\
                .then_inc(s_st, 1)

        def run_pool(pool, P0, Y0, warm):
            with pool.Fori(0, PM // 2) as k:
                for q in range(2):
                    split_pair(pool, k * 2 + (P0 + 2 * warm + q), k * 2 + (Y0 + q), q)

        def run_vector(dve, P0, Y0, warm, tok0, at_seed, st0):
            def lead():
                normalise(dve, P0, 0, tok0)
                shrink(dve, P0, 0)
                normalise(dve, P0 + 1, 1, tok0 + 2)

            def body(k, y0, y1, sd, last):
                P = P0 + k * 2
                Y = Y0 + k * 2 - 2 * warm
                tok = tok0 + k * 4
                if sd and at_seed:
                    at_seed()
                vector_pair(dve, P, 0, tok, Y - 1 if y0 else None, 1 if last else 2)
                vector_pair(dve, P + 1, 1, tok + 2, Y if y1 else None, 0 if last else 2)

            RS = STAT // 4
            lead()
            if warm:
                with dve.Fori(0, warm) as k:
                    body(k, False, False, None, False)
            body(warm, False, True, 1, False)
            with dve.Fori(warm + 1, warm + RS) as k:
                body(k, True, True, None, False)
            with dve.Fori(1, NBLK - 1) as piece:
                with dve.Fori(0, RS) as r:
                    body(piece * RS + r + warm, True, True, None, False)
                    piece_stats(dve, r, piece - 1, Y0)
                piece_stats(dve, RS, piece - 1, Y0)
            with dve.Fori(0, RS - 1) as r:
                body(r + ((NBLK - 1) * RS + warm), True, True, None, False)
                piece_stats(dve, r, NBLK - 2, Y0)
            k = warm + NBLK * RS - 1
            body(k, True, True, None, True)
            add_y(dve, Y0 + 2 * k - 2 * warm + 1, 1, tok0 + 4 * k + 2)
            for n in range(RS - 1, B):
                piece_stats(dve, n, NBLK - 2, Y0)
            for n in range(B):
                piece_stats(dve, n, NBLK - 1, Y0)
            dve.wait_ge(s_st, st0 + B * NBLK)
            passed(dve)

        SEEDS, NWL = 2, 10
        hs = h[:].rearrange("p t k (n s) -> p t k n s", s=SEG)
        st4 = start[:].rearrange("p k (n s) -> p k n s", s=SEG)

        with nc.Block() as block:
            @block.sync
            def _(sp):
                for dst, src in ((w_in[:], a["w_in"]), (w_ih[:], a["w_ih"]), (w_hh[:], a["w_hh"]), (w_out[:], a["w_out"]),
                                 (vecs[:, 0:1], a["gamma"]), (vecs[:, 1:2], a["beta"]), (vecs[:, 2:3], a["b_out"]),
                                 (b_in[:], a["b_in"]), (bg[:, 0, :], a["b_ih"]), (bg[:, 1, :], a["b_hh"])):
                    sp.dma_start(dst, src, allow_slow_non_contiguous=True).then_inc(s_w, 16)
                sp.wait_ge(s_flag, 1)
                bad = sp.value_load(flag[0:1, 0:1], min_val=0, max_val=1)
                with sp.If(bad > 0):
                    with sp.Fori(0, SEG - 1) as r:
                        sp.wait_ge(s_yd, r * PM + PM + 2)
                        passed(sp)
                        sp.wait_ge(s_st, r * (B * NBLK) + B * NBLK)
                        passed(sp)
                        sp.dma_start(X[:, PAD:PAD + B * HW].rearrange("p (n k) -> p n k", n=B),
                                     x1_dram.rearrange("n c k -> c n k")).then_inc(s_rel, 16)

            @block.gpsimd
            def _(pool):
                pool.sem_inc(s_g, 16)
                pool.sem_inc(s_pre, 2)
                pool.sem_inc(s_inp, 2)
                pool.sem_inc(s_xa, 1)
                pool.sem_inc(s_yd, 2)
                pool.sem_inc(s_sp, 4)
                pool.memset(ones[:], 1.0).then_inc(s_verp, 1)
                pool.wait_ge(s_w, 16 * NWL)
                for n, (w, parts) in enumerate(((w_in, pin), (w_ih, pih), (w_out, pout))):
                    pool.wait_ge(s_wh, n + 1)
                    pool.tensor_tensor(parts[1][:], w[:], parts[0][:].bitcast(F32), ALU.subtract).then_inc(s_ws, 1)
                run_pool(pool, 0, 0, RNDW)
                pool.wait_ge(s_flag, 1)
                bad = pool.value_load(flag[0:1, 0:1], min_val=0, max_val=1)
                with pool.If(bad > 0):
                    with pool.Fori(0, SEG - 1) as r:
                        run_pool(pool, r * PM + PA, r * PM + PM, 0)

            @block.scalar
            def _(act):
                gn_scalar(act, 0)
                act.wait_ge(s_w, 16 * NWL)
                for w, parts in ((w_in, pin), (w_ih, pih), (w_out, pout)):
                    act.activation(parts[0][:], w[:], ACT.Copy).then_inc(s_wh, 1)
                act.wait_ge(s_bn, 11)
                act.activation(mu[:, 2:3], mu[:, 1:2], ACT.Sqrt).then_inc(s_bnr, 1)
                act.activation(okc[:, 1:2], vecs[:, 0:1], ACT.Tanh)
                act.wait_ge(s_bn, BN_STEPS)
                run_scalar(act, 0, 0, RNDW)
                act.wait_ge(s_flag, 1)
                bad = act.value_load(flag[0:1, 0:1], min_val=0, max_val=1)
                with act.If(bad > 0):
                    with act.Fori(0, SEG - 1) as r:
                        run_scalar(act, r * PM + PA, r * PM + PM, 0)

            @block.vector
            def _(dve):
                dve.memset(h[:, 3], 0.0).then_inc(s_h, NH)
                gn_vector(dve, 0)
                dve.wait_ge(s_w, 16 * NWL)
                n_bn = [0]

                def link(ins):
                    n_bn[0] += 1
                    ins.then_inc(s_bn, 1)
                    dve.wait_ge(s_bn, n_bn[0])
                link(dve.tensor_tensor(e1[:], A[:], mvi[:, :, 0], ALU.mult))
                link(dve.tensor_tensor(e1[:], e1[:], Bb[:], ALU.add))
                link(dve.tensor_reduce(mu[:, 0:1], e1[:], AXX, ALU.add))
                link(dve.tensor_scalar(mu[:, 0:1], mu[:, 0:1], 1.0 / B, None, ALU.mult))
                link(dve.tensor_scalar(e1[:], e1[:], mu[:, 0:1], None, ALU.subtract))
                link(dve.tensor_tensor(e1[:], e1[:], e1[:], ALU.mult))
                link(dve.tensor_tensor(e2[:], A[:], A[:], ALU.mult))
                link(dve.tensor_tensor(e2[:], e2[:], mvi[:, :, 1], ALU.mult))
                link(dve.tensor_tensor(e2[:], e2[:], e1[:], ALU.add))
                link(dve.tensor_reduce(mu[:, 1:2], e2[:], AXX, ALU.add))
                link(dve.tensor_scalar(mu[:, 1:2], mu[:, 1:2], 1.0 / B, BN_EPS, ALU.mult, ALU.add))
                dve.wait_ge(s_bnr, 1)
                rsqrt_vector(dve, mu[:, 2:3], mu[:, 1:2], mu[:, 3:4], s_bn, n_bn[0])
                n_bn[0] += 5
                link(dve.tensor_tensor(mu[:, 2:3], mu[:, 2:3], vecs[:, 0:1], ALU.mult))
                link(dve.tensor_scalar(e1[:], A[:], mu[:, 2:3], None, ALU.mult))
                link(dve.tensor_scalar(e2[:], Bb[:], mu[:, 0:1], mu[:, 2:3], ALU.subtract, ALU.mult))
                link(dve.tensor_scalar(e2[:], e2[:], vecs[:, 1:2], None, ALU.add))
                link(dve.tensor_copy(A2[:], e1[:].unsqueeze(2).to_broadcast([C, B, SEG])))
                link(dve.tensor_copy(B2[:], e2[:].unsqueeze(2).to_broadcast([C, B, SEG])))
                link(dve.tensor_tensor(bg[:, 0, :], bg[:, 0, :], bg[:, 1, :], ALU.add))
                assert n_bn[0] == BN_STEPS
                def at_seed():
                    dve.wait_ge(s_h, 4 + NH * WARM)
                    dve.tensor_copy(start[:], h[:, 3]).then_inc(s_seed, 1)
                    dve.wait_ge(s_seed, 1)
                    dve.memset(hs[:, 3, :, :, 0:1], 0.0).then_inc(s_seed, 1)

                run_vector(dve, 0, 0, RNDW, 0, at_seed, 0)
                d = inp[:].rearrange("p a c -> p (a c)")[:, 0:NH * B * (SEG - 1)]
                d4 = d.rearrange("p (k n s) -> p k n s", k=NH, n=B)
                dve.wait_ge(s_h, 4 + NH * 2 * PA)
                dve.wait_ge(s_inp, PA + 2)
                for k in range(NH):
                    ins = dve.tensor_tensor(d4[:, k], hs[:, 3, k, :, 0:SEG - 1], st4[:, k, :, 1:SEG], ALU.subtract)
                ins.then_inc(s_ver, 1)
                dve.wait_ge(s_ver, 1)
                dve.tensor_tensor(d, d, d, ALU.mult).then_inc(s_ver, 1)
                dve.wait_ge(s_ver, 2)
                dve.tensor_scalar(d, d, HANDOVER_TOL ** 2, None, ALU.is_le).then_inc(s_ver, 1)
                dve.wait_ge(s_ver, 3)
                dve.tensor_reduce(okc[:, 0:1], d, AXX, ALU.min).then_inc(s_ver, 1)
                dve.wait_ge(s_verp, 2)
                dve.tensor_scalar(flag[:], bank[0][0:1, 0:1], 127.5, None, ALU.is_lt).then_inc(s_flag, 1)
                dve.wait_ge(s_flag, 1)
                bad = dve.value_load(flag[0:1, 0:1], min_val=0, max_val=1)
                with dve.If(bad > 0):
                    with dve.Fori(0, SEG - 1) as r:
                        dve.wait_ge(s_h, r * (NH * L) + 4 + NH * 2 * PA)
                        dve.wait_ge(s_yd, r * PM + PM + 2)
                        dve.tensor_copy(start[:], h[:, 3]).then_inc(s_seed, 1)
                        dve.wait_ge(s_seed, r * 3 + 3)
                        dve.tensor_copy(h[:, 3, :, 1:COLS], start[:, :, 0:COLS - 1]).then_inc(s_seed, 1)
                        dve.wait_ge(s_seed, r * 3 + 4)
                        dve.memset(hs[:, 3, :, :, 0:1], 0.0).then_inc(s_seed, 1)
                        dve.wait_ge(s_rel, r * 16 + 16)
                        run_vector(dve, r * PM + PA, r * PM + PM, 0, PAD, None, r * (B * NBLK) + B * NBLK)
                for n in range(B):
                    dve.bn_aggr(mvi[:, n, :], x2s[:, n * NBLK * 6:(n + 1) * NBLK * 6]).then_inc(s_mvw, 1)

            @block.tensor
            def _(pe):
                gn_tensor(pe, 0)
                pe.wait_ge(s_w, 16 * NWL)
                pe.wait_ge(s_ws, 3)
                run_tensor(pe, 0, 0, RNDW, SEEDS)
                pe.wait_ge(s_ver, 4)
                pe.wait_ge(s_verp, 1)
                pe.matmul(bank[0][0:1, 0:1], okc[:, 0:1], ones[:], start=True, stop=True).then_inc(s_verp, 1)
                pe.wait_ge(s_flag, 1)
                bad = pe.value_load(flag[0:1, 0:1], min_val=0, max_val=1)
                with pe.If(bad > 0):
                    with pe.Fori(0, SEG - 1) as r:
                        run_tensor(pe, r * PM + PA, r * PM + PM, 0, r * 3 + 5)


def split_product(pe, ps, w, x, first, last):
    pe.matmul(ps, w[0], x[0], start=first, stop=False)
    pe.matmul(ps, w[0], x[1], start=False, stop=False)
    return pe.matmul(ps, w[1], x[0], start=False, stop=last)


BORDERS = 4


def zero_border(e, pad, done):
    for edge in (0, H + 1):
        e.memset(pad[:, :, edge, :].bitcast(F32), 0.0).then_inc(done, 1)
    for edge in (0, W + 1):
        e.memset(pad[:, :, 1:1 + H, edge:edge + 1].bitcast(F32), 0.0).then_inc(done, 1)


def pad_blocks(b):
    return min(b + 1, NBLK - 1)


def masked_conv(nc, mk, a, X, bank, A, Bb, gn_tensor, gn_vector, gn_scalar, s_gd, bn, s_bst, s_mvw,
                image_stats, xblk, passed):
    with ExitStack() as ctx:
        sb, _, sem = mk(ctx)
        w3 = sb("w3", [C, 9, C])
        w1 = sb("w1", [C, C])
        on, off = sb("on_grid", [C, C]), sb("off_grid", [C, C])
        b2 = sb("b2", [C, C])
        bsum = sb("bsum", [C, 1])
        w_hi, w_lo = sb("w3_hi", [C, 9, C], F32R), sb("w3_lo", [C, 9, C], F32R)
        p_hi = sb("pad_hi", [C, 2, H + 2, W + 2], F32R)
        p_lo = sb("pad_lo", [C, 2, H + 2, W + 2], F32R)
        z = sb("z", [C, 2, BLK])
        s_w, s_wr, s_z = sem("conv_weights_loaded"), sem("conv_weights_masked"), sem("pad_zero")
        s_hi, s_pad, s_cv, s_ev = sem("pad_hi_ready"), sem("pad_ready"), sem("conv_product"), sem("conv_added")

        with nc.Block() as block:
            @block.sync
            def _(sp):
                for dst, src in ((w3[:], a["w3"]), (w1[:], a["w1"]), (on[:], a["on_grid"]), (off[:], a["off_grid"]),
                                 (b2[:], a["b2"])):
                    sp.dma_start(dst, src).then_inc(s_w, 16)

            @block.gpsimd
            def _(pool):
                pool.sem_inc(s_cv, 15)
                pool.sem_inc(s_ev, 8)
                pool.sem_inc(s_pad, 2)
                zero_border(pool, p_hi, s_z)
                zero_border(pool, p_lo, s_z)
                pool.wait_ge(s_z, 2 * BORDERS)
                with pool.Fori(0, B // 2) as g:
                    for u in range(2):
                        for b in range(NBLK):
                            pool.wait_ge(s_hi, (g * 2 + u) * NBLK + b + 1)
                            passed(pool)
                            rows = slice(1 + b * ROWS, 1 + (b + 1) * ROWS)
                            pool.tensor_tensor(p_lo[:, u, rows, 1:1 + W], z[:, b % 2, :].rearrange("p (r c) -> p r c", c=W),
                                               p_hi[:, u, rows, 1:1 + W].bitcast(F32), ALU.subtract).then_inc(s_pad, 1)

            @block.scalar
            def _(act):
                gn_scalar(act, 1)
                act.wait_ge(s_gd, 2 * GN_DVE)
                act.wait_ge(s_z, 2 * BORDERS)
                with act.Fori(0, B // 2) as g:
                    for u in range(2):
                        n = g * 2 + u
                        act.wait_ge(s_cv, n * NBLK + 8)
                        for b in range(NBLK):
                            act.wait_ge(s_pad, n * NBLK + b + (1 if b else 2))
                            act.activation(z[:, b % 2, :], xblk(n, b), ACT.Identity, bias=Bb[:, bass.ds(n, 1)],
                                           scale=A[:, bass.ds(n, 1)])
                            act.activation(p_hi[:, u, 1 + b * ROWS:1 + (b + 1) * ROWS, 1:1 + W],
                                           xblk(n, b).rearrange("p (r c) -> p r c", c=W), ACT.Identity,
                                           bias=Bb[:, bass.ds(n, 1)], scale=A[:, bass.ds(n, 1)]).then_inc(s_hi, 1)

            @block.vector
            def _(dve):
                gn_vector(dve, 1)
                dve.wait_ge(s_w, 80)
                dve.tensor_tensor(w3[:], w3[:], on[:].unsqueeze(1).to_broadcast([C, 9, C]), ALU.mult).then_inc(s_wr, 1)
                dve.tensor_tensor(w1[:], w1[:], off[:], ALU.mult).then_inc(s_wr, 1)
                dve.wait_ge(s_wr, 2)
                dve.tensor_tensor(w3[:, 4, :], w3[:, 4, :], w1[:], ALU.add).then_inc(s_wr, 1)
                dve.tensor_reduce(bsum[:], b2[:], AXX, ALU.add).then_inc(s_wr, 1)
                dve.wait_ge(s_wr, 4)
                dve.tensor_copy(w_hi[:], w3[:]).then_inc(s_wr, 1)
                dve.wait_ge(s_wr, 5)
                dve.tensor_tensor(w_lo[:], w3[:], w_hi[:].bitcast(F32), ALU.subtract).then_inc(s_wr, 1)
                with dve.Fori(0, B) as n:
                    dve.wait_ge(s_mvw, n + 2 * B)
                    for b in range(NBLK):
                        dve.wait_ge(s_cv, n * NBLK + b + 16)
                        dve.scalar_tensor_tensor(xblk(n, b), bank[b][:, 0:BLK], bsum[:], xblk(n, b), ALU.add, ALU.add)\
                            .then_inc(s_ev, 1)
                        dve.wait_ge(s_ev, n * NBLK + b + 9)
                        passed(dve)
                        ins = dve.bn_stats(bn[:, b, :], xblk(n, b))
                    ins.then_inc(s_bst, 1)
                    image_stats(dve, n, n + B)

            @block.tensor
            def _(pe):
                gn_tensor(pe, 1)
                pe.wait_ge(s_wr, 6)
                with pe.Fori(0, B // 2) as g:
                    for u in range(2):
                        n = g * 2 + u
                        for b in range(NBLK):
                            pe.wait_ge(s_pad, n * NBLK + pad_blocks(b) + 3)
                            pe.wait_ge(s_ev, n * NBLK + b + 2)
                            for k in range(9):
                                dy, dx = divmod(k, 3)
                                at = (slice(None), u, slice(b * ROWS + dy, b * ROWS + dy + ROWS), slice(dx, dx + W))
                                ins = split_product(pe, bank[b][:, 0:BLK], (w_hi[:, k, :], w_lo[:, k, :]),
                                                    (p_hi[at], p_lo[at]), k == 0, k == 8)
                            ins.then_inc(s_cv, 1)


def conv_pair(nc, mk, a, X, bank, A, Bb, gn_tensor, gn_vector, gn_scalar, xblk, passed, s_gd, out):
    with ExitStack() as ctx:
        sb, _, sem = mk(ctx)
        c1, c2 = sb("c1", [C, 9, C]), sb("c2", [C, 9, C])
        bnv = sb("bnv", [C, 8])
        sv = sb("sv", [C, 2])
        tv = sb("tv", [C, 2])
        root, tmp = sb("root", [C, 2]), sb("tmp", [C, 2])
        w_hi = [sb(f"c{i}_hi", [C, 9, C], F32R) for i in (1, 2)]
        w_lo = [sb(f"c{i}_lo", [C, 9, C], F32R) for i in (1, 2)]
        pz = [sb(f"z_pad_{k}", [C, H + 2, W + 2], F32R) for k in ("hi", "lo")]
        pm = [sb(f"mid_pad_{k}", [C, H + 2, W + 2], F32R) for k in ("hi", "lo")]
        zr = sb("z_ring", [C, 2, BLK])
        mr = sb("mid_ring", [C, 2, BLK])
        res = sb("res", [C, 2, BLK])
        s_w, s_z = sem("pair_weights_loaded"), sem("pair_pads_zero")
        s_k, s_kr = sem("pair_bn_steps"), sem("pair_bn_root")
        s_pz, s_c1, s_m, s_c2 = sem("z_ready"), sem("conv1_product"), sem("mid_ready"), sem("conv2_product")
        s_zr, s_mr, s_r1 = sem("z_hi_ready"), sem("mid_hi_ready"), sem("residual_hi_added")
        s_r, s_rl, s_add, s_st = sem("residual_added"), sem("relu_done"), sem("x_added"), sem("stored")
        o = out.rearrange("n c h w -> n c (h w)")
        v4 = bnv[:].rearrange("p (j q) -> p j q", j=2)

        with nc.Block() as block:
            @block.sync
            def _(sp):
                for dst, src in ((c1[:], a["c1"]), (c2[:], a["c2"])) + tuple(
                        (bnv[:, i:i + 1], a[k]) for i, k in enumerate(("g1", "h1", "m1", "v1", "g2", "h2", "m2", "v2"))):
                    sp.dma_start(dst, src, allow_slow_non_contiguous=True).then_inc(s_w, 16)
                with sp.Fori(0, B) as n:
                    sp.wait_ge(s_add, n * NBLK + NBLK + 2)
                    passed(sp)
                    sp.dma_start(o[bass.ds(n, 1)].rearrange("u c k -> (u c) k"), X[:, bass.ds(PAD + n * HW, HW)])\
                        .then_inc(s_st, 16)
                sp.wait_ge(s_st, 16 * B)

            @block.gpsimd
            def _(pool):
                pool.sem_inc(s_c1, 8)
                pool.sem_inc(s_c2, 15)
                pool.sem_inc(s_m, 8)
                pool.sem_inc(s_r, 8)
                pool.sem_inc(s_rl, 2)
                pool.sem_inc(s_add, 2)
                pool.sem_inc(s_pz, 2)
                for p in pz + pm:
                    zero_border(pool, p[:].unsqueeze(1), s_z)
                pool.wait_ge(s_z, 4 * BORDERS)

                def lo(pads, ring, b, done):
                    rows = slice(1 + b * ROWS, 1 + (b + 1) * ROWS)
                    pool.tensor_tensor(pads[1][:, rows, 1:1 + W], ring[:, b % 2, :].rearrange("p (r c) -> p r c", c=W),
                                       pads[0][:, rows, 1:1 + W].bitcast(F32), ALU.subtract).then_inc(done, 1)

                for b in range(NBLK):
                    pool.wait_ge(s_zr, b + 1)
                    lo(pz, zr, b, s_pz)
                with pool.Fori(0, B - 1) as n:
                    for b in range(NBLK):
                        pool.wait_ge(s_mr, n * NBLK + b + 1)
                        passed(pool)
                        lo(pm, mr, b, s_m)
                    for b in range(NBLK):
                        pool.wait_ge(s_zr, n * NBLK + NBLK + b + 1)
                        passed(pool)
                        lo(pz, zr, b, s_pz)
                for b in range(NBLK):
                    pool.wait_ge(s_mr, (B - 1) * NBLK + b + 1)
                    lo(pm, mr, b, s_m)

            @block.scalar
            def _(act):
                gn_scalar(act, 2)
                act.wait_ge(s_k, 1)
                act.activation(root[:], tmp[:], ACT.Sqrt).then_inc(s_kr, 1)
                act.wait_ge(s_gd, 3 * GN_DVE)
                act.wait_ge(s_k, 9)
                act.wait_ge(s_z, 4 * BORDERS)

                def z_block(n, b):
                    act.wait_ge(s_pz, n * NBLK + b + (1 if b else 2))
                    act.activation(zr[:, b % 2, :], xblk(n, b), ACT.Identity, bias=Bb[:, bass.ds(n, 1)],
                                   scale=A[:, bass.ds(n, 1)])
                    act.activation(pz[0][:, 1 + b * ROWS:1 + (b + 1) * ROWS, 1:1 + W],
                                   xblk(n, b).rearrange("p (r c) -> p r c", c=W), ACT.Identity,
                                   bias=Bb[:, bass.ds(n, 1)], scale=A[:, bass.ds(n, 1)]).then_inc(s_zr, 1)

                for b in range(NBLK):
                    z_block(0, b)

                def image(n, more):
                    for b in range(NBLK):
                        act.wait_ge(s_c1, n * NBLK + b + 9)
                        act.wait_ge(s_m, n * NBLK + b + (7 if b else 8))
                        act.activation(mr[:, b % 2, :], bank[b][:, 0:BLK], ACT.Relu, bias=tv[:, 0:1], scale=sv[:, 0:1])
                        act.activation(pm[0][:, 1 + b * ROWS:1 + (b + 1) * ROWS, 1:1 + W],
                                       bank[b][:, 0:BLK].rearrange("p (r c) -> p r c", c=W), ACT.Relu,
                                       bias=tv[:, 0:1], scale=sv[:, 0:1]).then_inc(s_mr, 1)
                    for b in range(NBLK):
                        act.wait_ge(s_r, n * NBLK + b + 9)
                        act.activation(res[:, b % 2, :], res[:, b % 2, :], ACT.Relu, bias=tv[:, 1:2]).then_inc(s_rl, 1)
                        if more:
                            z_block(n + 1, b)

                with act.Fori(0, B - 1) as n:
                    image(n, True)
                image(B - 1, False)

            @block.vector
            def _(dve):
                gn_vector(dve, 2)
                dve.wait_ge(s_w, 160)
                dve.tensor_scalar(tmp[:], v4[:, :, 3], BN_EPS, None, ALU.add).then_inc(s_k, 1)
                dve.wait_ge(s_kr, 1)
                rsqrt_vector(dve, root[:], tmp[:], sv[:], s_k, 1)
                dve.tensor_tensor(sv[:], root[:], v4[:, :, 0], ALU.mult).then_inc(s_k, 1)
                dve.wait_ge(s_k, 7)
                dve.tensor_tensor(tmp[:], sv[:], v4[:, :, 2], ALU.mult).then_inc(s_k, 1)
                dve.wait_ge(s_k, 8)
                dve.tensor_tensor(tv[:], v4[:, :, 1], tmp[:], ALU.subtract).then_inc(s_k, 1)
                dve.wait_ge(s_k, 9)

                def add_x(n, b):
                    dve.wait_ge(s_rl, n * NBLK + b + 3)
                    dve.tensor_tensor(xblk(n, b), xblk(n, b), res[:, b % 2, :], ALU.add).then_inc(s_add, 1)

                for i, c in enumerate((c1, c2)):
                    dve.tensor_copy(w_hi[i][:], c[:]).then_inc(s_k, 1)
                    dve.wait_ge(s_k, 10 + 2 * i)
                    dve.tensor_tensor(w_lo[i][:], c[:], w_hi[i][:].bitcast(F32), ALU.subtract).then_inc(s_k, 1)

                with dve.Fori(0, B) as n:
                    for b in range(NBLK):
                        dve.wait_ge(s_c2, n * NBLK + b + 16)
                        dve.wait_ge(s_add, n * NBLK + b + (1 if b else 2))
                        rb = res[:, b % 2, :].rearrange("p (r c) -> p r c", c=W)
                        at = (slice(None), slice(1 + b * ROWS, 1 + (b + 1) * ROWS), slice(1, 1 + W))
                        dve.scalar_tensor_tensor(rb, bank[b][:, 0:BLK].rearrange("p (r c) -> p r c", c=W), sv[:, 1:2],
                                                 pz[0][at].bitcast(F32), ALU.mult, ALU.add).then_inc(s_r1, 1)
                        dve.wait_ge(s_r1, n * NBLK + b + 1)
                        dve.tensor_tensor(rb, rb, pz[1][at].bitcast(F32), ALU.add).then_inc(s_r, 1)
                        if b:
                            add_x(n, b - 1)
                    add_x(n, NBLK - 1)

            @block.tensor
            def _(pe):
                gn_tensor(pe, 2)
                pe.wait_ge(s_k, 11)

                def conv(b, i, src):
                    for k in range(9):
                        dy, dx = divmod(k, 3)
                        at = (slice(None), slice(b * ROWS + dy, b * ROWS + dy + ROWS), slice(dx, dx + W))
                        ins = split_product(pe, bank[b][:, 0:BLK], (w_hi[i][:, k, :], w_lo[i][:, k, :]),
                                            (src[0][at], src[1][at]), k == 0, k == 8)
                    return ins

                with pe.Fori(0, B) as n:
                    for b in range(NBLK):
                        pe.wait_ge(s_pz, n * NBLK + pad_blocks(b) + 3)
                        pe.wait_ge(s_r, n * NBLK + b + 2)
                        conv(b, 0, pz).then_inc(s_c1, 1)
                    pe.wait_ge(s_k, 13)
                    for b in range(NBLK):
                        pe.wait_ge(s_m, n * NBLK + pad_blocks(b) + 9)
                        conv(b, 1, pm).then_inc(s_c2, 1)


def program(nc, a, out, last_stage=4):
    root = ExitStack()
    with root:
        def mk(ctx):
            def sb(n, s, d=F32):
                return ctx.enter_context(nc.sbuf_tensor(n, s, d))

            def ps(n, s, d=F32):
                return ctx.enter_context(nc.psum_tensor(n, s, d))

            def sem(n):
                return ctx.enter_context(nc.semaphore(n))
            return sb, ps, sem

        sb, psm, sem = mk(root)
        x_in = a["x"].rearrange("n c h w -> n c (h w)")
        x1_dram = nc.dram_tensor("x1_backup", [B, C, HW], F32, kind="Internal").ap()
        v_dram = nc.dram_tensor("v_windows", [B * P2, W2, C], F32, kind="Internal").ap()

        s_root = sem("groupnorm_root")
        s_passed = sem("waits_passed")
        s_w4 = sem("group_matrix_loaded")
        X = sb("X", [C, PAD + B * HW + L])
        bank = [psm(f"bank{i}", [128, 512]) for i in range(8)]
        t = {k: sb(k, [C, B]) for k in ("gn_gm", "gn_d", "gn_v")}
        t["group4"] = sb("group4", [C, C])
        mv = sb("mv", [C, B, 2])
        A = sb("A", [C, B])
        Bb = sb("Bb", [C, B])
        bn = sb("bn", [C, NBLK, 6])
        mv1 = sb("mv1", [C, 2])
        gm, gd, gv, group4 = t["gn_gm"], t["gn_d"], t["gn_v"], t["group4"]
        s_gd = sem("groupnorm_vector")
        s_gp = sem("groupnorm_tensor")
        s_mv1 = sem("image_aggregated")
        s_bst = sem("block_stats")
        s_mvw = sem("image_stats")

        def passed(e):
            e.sem_inc(s_passed, 1)

        def gn_tensor(e, g):
            e.wait_ge(s_mvw, B * (g + 1))
            e.wait_ge(s_w4, 16)
            e.matmul(bank[7][:, 0:B], group4[:], mv[:, :, 0], start=True, stop=True).then_inc(s_gp, 1)
            e.wait_ge(s_gd, GN_DVE * g + 4)
            e.matmul(bank[7][:, 0:B], group4[:], gv[:], start=True, stop=True).then_inc(s_gp, 1)

        def gn_vector(e, g):
            d0 = GN_DVE * g
            e.wait_ge(s_mvw, B * (g + 1))
            e.wait_ge(s_gp, GN_PE * g + 1)
            e.tensor_copy(gm[:], bank[7][:, 0:B]).then_inc(s_gd, 1)
            e.wait_ge(s_gd, d0 + 1)
            e.tensor_tensor(gd[:], mv[:, :, 0], gm[:], ALU.subtract).then_inc(s_gd, 1)
            e.wait_ge(s_gd, d0 + 2)
            e.tensor_tensor(gv[:], gd[:], gd[:], ALU.mult).then_inc(s_gd, 1)
            e.wait_ge(s_gd, d0 + 3)
            e.tensor_tensor(gv[:], gv[:], mv[:, :, 1], ALU.add).then_inc(s_gd, 1)
            e.wait_ge(s_gp, GN_PE * g + 2)
            e.tensor_scalar(gv[:], bank[7][:, 0:B], GN_EPS, None, ALU.add).then_inc(s_gd, 1)
            e.wait_ge(s_root, g + 1)
            rsqrt_vector(e, A[:], gv[:], gd[:], s_gd, d0 + 5)
            e.scalar_tensor_tensor(Bb[:], gm[:], -1.0, A[:], ALU.mult, ALU.mult).then_inc(s_gd, 1)
            e.wait_ge(s_gd, d0 + 11)

        def gn_scalar(e, g):
            e.wait_ge(s_gd, GN_DVE * g + 5)
            e.activation(A[:], gv[:], ACT.Sqrt).then_inc(s_root, 1)

        def image_stats(e, n, done):
            e.wait_ge(s_bst, done + 1)
            passed(e)
            e.bn_aggr(mv1[:], bn[:].rearrange("p b s -> p (b s)")).then_inc(s_mv1, 1)
            e.wait_ge(s_mv1, done + 1)
            e.tensor_copy(mv[:, bass.ds(n, 1), :], mv1[:].unsqueeze(1)).then_inc(s_mvw, 1)

        def xblk(n, b):
            return X[:, bass.ds(PAD + n * HW + b * BLK, BLK)]

        with ExitStack() as c0:
            sb, _, sem = mk(c0)
            s_ldx = [sem("first_image_loaded"), sem("images_loaded")]
            s_ib, s_ia = sem("input_block_stats"), sem("input_aggregated")
            s_id, s_ip, s_ir = sem("input_norm_vector"), sem("input_norm_tensor"), sem("input_norm_root")
            bni, inorm = sb("bn_in", [C, NBLK, 6]), sb("input_norm", [C, 6])
            mi = inorm[:, 0:2]
            im, iv, ir, it = (inorm[:, i:i + 1] for i in range(2, 6))
            s_w = sem("weights_loaded")
            s_padz = sem("pads_zero")
            s_xb = sem("xb_ready")
            s_pq, s_pk, s_pv, s_pV = sem("q_product"), sem("k_product"), sem("v_product"), sem("vtok_product")
            s_q, s_k, s_v, s_V = sem("q_ready"), sem("k_ready"), sem("v_ready"), sem("vtok_ready")
            s_vh = sem("v_hi_ready")
            s_vst = [sem("v_stored_even"), sem("v_stored_odd")]
            s_qs = sem("window_sums")
            s_lg = sem("logits_product")
            s_tk = sem("topk_steps")
            s_row = sem("routes_ready")
            s_kg, s_Q, s_vg = sem("keys_gathered"), sem("queries_spread"), [sem(f"values_gathered{i}") for i in range(3)]
            s_S = sem("scores_product")
            s_mx, s_ex, s_rd = sem("score_max"), sem("exp_done"), sem("sum_reciprocal")
            s_nP = sem("probs_normalised")
            s_T, s_Tc = sem("probs_turned"), sem("turned_copied")
            s_O, s_o, s_om = sem("attended_product"), sem("attended_ready"), sem("attended_half")
            s_out, s_ev = sem("out_product"), sem("out_added")
            s_cst, s_cp = sem("consts_ready"), sem("consts_product")
            s_bak = sem("x1_saved")

            w_qkv = sb("w_qkv", [C, 3 * C])
            w_o = sb("w_o", [C, C])
            lw = sb("lw", [C, 9])
            w_tap = [sb(f"w_tap_{k}", [C, 9, C], F32R) for k in ("hi", "lo")]
            vec = sb("vec", [C, 6])
            cb = sb("cb", [C, 2])
            eo = sb("eo", [C, 2])
            hmask = sb("hmask", [C, HEADS, W2])
            ident = sb("ident", [C, C])
            qT = sb("qT", [C, HW])
            kT = sb("kT", [C, HW])
            oT = sb("oT", [C, HW])
            vpad = [sb(f"vpad_{k}", [C, H + 2, W + 2], F32R) for k in ("hi", "lo")]
            vst = sb("vst", [C, 2, 4, C])
            qs = sb("qs", [C, P2])
            ks = sb("ks", [C, P2])
            lg = sb("lg", [P2, P2])
            m8 = sb("m8", [P2, 8])
            ix = sb("ix", [P2, 8], U32)
            row = sb("row", [1, P2 * TOPK], U32)
            Qs = sb("Qs", [C, 2, HEADS * W2])
            kg = sb("kg", [C, 2, KEYS])
            vg = sb("vg", [C, 3, 2, C])
            Pr = sb("Pr", [C, 2, PAIRS, KEYS])
            PT = sb("PT", [C, 2, PAIRS * 2 * C])
            xb = PT[:, 0, 0:2 * BLK].rearrange("p (s k) -> p s k", s=2)
            nmx = sb("nmx", [C, 2, PAIRS])
            den = sb("den", [C, 2, PAIRS])
            rden = sb("rden", [C, 2, PAIRS])
            oh = sb("oh", [C, W2])

            NW = 10
            STORED = 32

            def routes(e, w):
                return nc.values_load_multi_w_load_instructions(
                    row[0:1, bass.ds(w * TOPK, TOPK)], engines=[e.engine], min_val=0, max_val=P2 - 1,
                    skip_runtime_bounds_check_because="positions among P2 values")[1]

            def input_stats(dve, m):
                for b in range(NBLK):
                    ins = dve.bn_stats(bni[:, b, :], xblk(m, b))
                ins.then_inc(s_ib, 1)
                dve.wait_ge(s_ib, m + 1)
                passed(dve)
                dve.bn_aggr(mi, bni[:].rearrange("p b s -> p (b s)")).then_inc(s_ia, 1)

            def input_mean_tensor(pe, m):
                pe.wait_ge(s_ia, m + 1)
                pe.matmul(bank[6][:, 0:1], group4[:], mi[:, 0:1], start=True, stop=True).then_inc(s_ip, 1)

            def input_mean(dve, m):
                d0 = m * IN_DVE
                dve.wait_ge(s_ip, m * 2 + 1)
                dve.tensor_copy(im, bank[6][:, 0:1]).then_inc(s_id, 1)
                dve.wait_ge(s_id, d0 + 1)
                dve.tensor_tensor(it, mi[:, 0:1], im, ALU.subtract).then_inc(s_id, 1)
                dve.wait_ge(s_id, d0 + 2)
                dve.scalar_tensor_tensor(iv, it, it, mi[:, 1:2], ALU.mult, ALU.add).then_inc(s_id, 1)

            def input_var_tensor(pe, m):
                pe.wait_ge(s_id, m * IN_DVE + 3)
                pe.matmul(bank[6][:, 0:1], group4[:], iv, start=True, stop=True).then_inc(s_ip, 1)

            def input_var(dve, m):
                dve.wait_ge(s_ip, m * 2 + 2)
                dve.tensor_scalar(iv, bank[6][:, 0:1], GN_EPS, None, ALU.add).then_inc(s_id, 1)

            def input_root(act, m):
                act.wait_ge(s_id, m * IN_DVE + 4)
                act.activation(ir, iv, ACT.Sqrt).then_inc(s_ir, 1)

            def input_scale(dve, m):
                d0 = m * IN_DVE
                dve.wait_ge(s_ir, m + 1)
                rsqrt_vector(dve, ir, iv, it, s_id, d0 + 4)
                dve.scalar_tensor_tensor(it, im, -1.0, ir, ALU.mult, ALU.mult).then_inc(s_id, 1)
                dve.tensor_copy(A[:, bass.ds(m, 1)], ir).then_inc(s_id, 1)
                dve.wait_ge(s_id, d0 + 11)
                dve.tensor_copy(Bb[:, bass.ds(m, 1)], it).then_inc(s_id, 1)

            def following(n):
                return nc.s_assert_within(n + 1, 1, B - 1, skip_runtime_bounds_check_because="n < B - 1 here")

            def fetch(e, source, r, slot):
                e.dma_start(vg[64 * (r % 2):64 * (r % 2) + 64, slot, r // 2, :],
                            v_dram[bass.ds(source, 1)].rearrange("u k c -> (u k) c")).then_inc(s_vg[slot], 16)

            with nc.Block() as block:
                @block.sync
                def _(sp):
                    sp.dma_start(group4[:], a["group4"]).then_inc(s_w4, 16)
                    sp.dma_start(X[:, PAD:PAD + HW], x_in[0]).then_inc(s_ldx[0], 16)
                    for dst, src in ((w_qkv[:], a["w_qkv"]), (w_o[:], a["w_o"]), (lw[:], a["lepe_w"]),
                                     (vec[:, 0:3], a["b_qkv"]), (vec[:, 3:4], a["lepe_b"]), (vec[:, 4:5], a["b_o"]),
                                     (eo[:], a["even_odd"]), (hmask[:, :, 0], a["head_mask"]),
                                     (ident[:], a["ident"]),
                                     (vec[:, 5:6], a["b_q"])):
                        sp.dma_start(dst, src, allow_slow_non_contiguous=True).then_inc(s_w, 16)
                    for n in range(1, B):
                        sp.dma_start(X[:, PAD + n * HW:PAD + (n + 1) * HW], x_in[n]).then_inc(s_ldx[1], 16)
                    with sp.Fori(0, B) as n:
                        for b in range(NBLK):
                            sp.wait_ge(s_V, n * NBLK + b + 2)
                            passed(sp)
                            sp.dma_start(v_dram[bass.ds(n * P2 + b * NWIN, 6)].rearrange("(i u) k c -> (u k) i c", u=2),
                                         vst[:, b % 2, 0:3, :]).then_inc(s_vst[b % 2], 16)
                            sp.dma_start(v_dram[bass.ds(n * P2 + b * NWIN + 6, 1)].rearrange("u k c -> (u k) c"),
                                         vst[0:64, b % 2, 3, :]).then_inc(s_vst[b % 2], 16)
                        sp.wait_ge(s_tk, n * 3 + 4)
                        passed(sp)
                        sp.wait_ge(s_kg, (n * P2) + 1)
                        passed(sp)
                        sp.wait_ge(s_Tc, (n * P2) * 2 + 1)
                        passed(sp)
                        sp.dma_start(row[0:1, :], ix[:, 0:TOPK]).then_inc(s_row, 16)
                        sp.wait_ge(s_vst[0], n * (STORED * 4) + STORED * 4 + 16)
                        passed(sp)
                        sp.wait_ge(s_vst[1], n * (STORED * 3) + STORED * 3 + 16)
                        passed(sp)
                        sp.wait_ge(s_row, n * 16 + 32)
                        passed(sp)
                        sp.wait_ge(s_O, n * P2 + 3)
                        passed(sp)

                        def gather(w, slot):
                            idx = routes(sp, w)
                            sp.wait_ge(s_O, n * P2 + w + 1)
                            passed(sp)
                            for r in range(TOPK - 1):
                                fetch(sp, idx[r] + n * P2, r, slot)

                        with sp.Fori(0, P2 // 3) as k:
                            for i in range(3):
                                gather(k * 3 + i, i)
                        gather(P2 - 1, (P2 - 1) % 3)
                        sp.wait_ge(s_ev, n * NBLK + NBLK + 4)
                        passed(sp)
                        sp.dma_start(x1_dram[bass.ds(n, 1)].rearrange("u c k -> (u c) k"),
                                     X[:, bass.ds(PAD + n * HW, HW)]).then_inc(s_bak, 16)
                    sp.wait_ge(s_bak, 16 * B)

                @block.gpsimd
                def _(pool):
                    pool.memset(X[:, 0:PAD], 0.0).then_inc(s_padz, 1)
                    for k in range(2):
                        zero_border(pool, vpad[k][:].unsqueeze(1), s_padz)
                    for sm in (s_xb, s_V, s_tk, s_kg, s_S, s_O, s_T, s_ev, s_nP, s_ex, s_o, s_Tc, s_mx, s_Q):
                        pool.sem_inc(sm, 1)
                    pool.sem_inc(s_O, 2)
                    pool.sem_inc(s_ev, 3)
                    pool.sem_inc(s_S, PAIRS - 1)
                    pool.sem_inc(s_pV, 2)
                    pool.sem_inc(s_vst[0], 16)
                    pool.sem_inc(s_vst[1], 16)
                    pool.sem_inc(s_row, 16)
                    pool.wait_ge(s_cst, 21)
                    with pool.Fori(0, B) as n:
                        pool.wait_ge(s_row, n * 16 + 32)
                        pool.wait_ge(s_q, n * NBLK + NBLK)
                        pool.wait_ge(s_k, n * NBLK + NBLK)
                        passed(pool)

                        def window(w, par):
                            if not isinstance(w, int):
                                pool.wait_ge(s_S, (n * P2 + w) * PAIRS)
                            passed(pool)
                            for r, i in enumerate(routes(pool, w)):
                                ins = pool.tensor_copy(kg[:, par, r * W2:(r + 1) * W2], kT[:, bass.ds(i * W2, W2)])
                            ins.then_inc(s_kg, 1)
                            pool.tensor_tensor(Qs[:, par, :].rearrange("p (h k) -> p h k", h=HEADS),
                                               qT[:, bass.ds(w * W2, W2)].unsqueeze(1).to_broadcast([C, HEADS, W2]),
                                               hmask[:], ALU.mult).then_inc(s_Q, 1)

                        pool.wait_ge(s_S, n * (P2 * PAIRS) + PAIRS)
                        passed(pool)
                        window(0, 0)
                        with pool.Fori(0, (P2 - 1) // 2) as k:
                            window(k * 2 + 1, 1)
                            window(k * 2 + 2, 0)
                    pool.wait_ge(s_S, (B * P2 + 1) * PAIRS)

                @block.scalar
                def _(act):
                    def evac_act(act, n, b):
                        par = b % 2
                        act.wait_ge(s_pq, n * NBLK + b + 1)
                        act.wait_ge(s_Q, n * P2 + 1)
                        act.activation(qT[:, b * BLK:(b + 1) * BLK], bank[4 * par][:, 0:BLK], ACT.Identity,
                                       bias=vec[:, 5:6], scale=QSCALE).then_inc(s_q, 1)
                        act.wait_ge(s_pV, n * NBLK + b + 3)
                        act.wait_ge(s_vst[par], n * (STORED * (4 - par)) + STORED * (b // 2) + 16)
                        act.activation(vst[:, par, 0:3, :], bank[4 * par + 3][:, 0:384].rearrange("p (i c) -> p i c", c=C),
                                       ACT.Copy)
                        act.activation(vst[0:64, par, 3, :], bank[4 * par + 3][0:64, 384:512], ACT.Copy).then_inc(s_V, 1)

                    input_root(act, 0)
                    act.wait_ge(s_cst, 21)
                    with act.Fori(0, B) as n:
                        act.wait_ge(s_id, n * IN_DVE + IN_DVE)
                        act.wait_ge(s_O, n * P2 + 3)
                        for b in range(NBLK):
                            act.wait_ge(s_pV, n * NBLK + b + 1)
                            xw = xblk(n, b).rearrange("p (r w c) -> p w r c", r=ROWS, c=WIN)
                            act.activation(xb[:, b % 2, :].rearrange("p (w r c) -> p w r c", r=ROWS, c=WIN), xw,
                                           ACT.Identity, bias=Bb[:, bass.ds(n, 1)], scale=A[:, bass.ds(n, 1)])\
                                .then_inc(s_xb, 1)
                            if b >= 1:
                                evac_act(act, n, b - 1)
                        evac_act(act, n, NBLK - 1)

                        def exps(w, par):
                            if not isinstance(w, int):
                                act.wait_ge(s_T, n * P2 + w)
                            for j in range(PAIRS):
                                act.wait_ge(s_mx, (n * P2 + w) * PAIRS + j + 2)
                                act.activation(Pr[:, par, j, :], bank[j][:, 0:KEYS], ACT.Exp,
                                               bias=nmx[:, par, j:j + 1], accum_out=den[:, par, j:j + 1])\
                                    .then_inc(s_ex, 1)

                        def turned(w, par):
                            act.wait_ge(s_T, n * P2 + w + 2)
                            act.wait_ge(s_O, n * P2 + w + 2)
                            for i in range(2):
                                act.activation(PT[:, par, i * 512:(i + 1) * 512], bank[4 + i][:], ACT.Copy)\
                                    .then_inc(s_Tc, 1)

                        def fourth(w, slot):
                            idx = routes(act, w)
                            fetch(act, idx[TOPK - 1] + n * P2, TOPK - 1, slot)

                        act.wait_ge(s_vst[0], n * (STORED * 4) + STORED * 4 + 16)
                        passed(act)
                        act.wait_ge(s_vst[1], n * (STORED * 3) + STORED * 3 + 16)
                        passed(act)
                        act.wait_ge(s_row, n * 16 + 32)
                        passed(act)
                        fourth(0, 0)

                        act.wait_ge(s_T, n * P2 + 1)
                        exps(0, 0)
                        with act.Fori(0, (P2 - 1) // 6) as k:
                            for i in range(6):
                                exps(k * 6 + i + 1, (i + 1) % 2)
                                turned(k * 6 + i, i % 2)
                                fourth(k * 6 + i + 1, (i + 1) % 3)
                        turned(P2 - 1, 0)
                        with act.If(n < B - 1):
                            input_root(act, following(n))

                @block.vector
                def _(dve):
                    dve.wait_ge(s_ldx[0], 16)
                    input_stats(dve, 0)
                    dve.wait_ge(s_w, 16 * NW)
                    dve.tensor_scalar(vec[:, 5:6], vec[:, 5:6], QSCALE, None, ALU.mult).then_inc(s_cst, 1)
                    dve.tensor_copy(hmask[:, :, 1:W2], hmask[:, :, 0:1].to_broadcast([C, HEADS, W2 - 1]))\
                        .then_inc(s_cst, 1)
                    for k in range(9):
                        dve.tensor_scalar(w_tap[0][:, k, :], w_o[:], lw[:, k:k + 1], None, ALU.mult).then_inc(s_cst, 1)
                        dve.wait_ge(s_cst, 2 * k + 3)
                        dve.scalar_tensor_tensor(w_tap[1][:, k, :], w_o[:], lw[:, k:k + 1],
                                                 w_tap[0][:, k, :].bitcast(F32), ALU.mult, ALU.subtract)\
                            .then_inc(s_cst, 1)
                    dve.tensor_tensor(cb[:, 0:1], vec[:, 2:3], vec[:, 3:4], ALU.add).then_inc(s_cst, 1)
                    input_mean(dve, 0)
                    input_var(dve, 0)
                    input_scale(dve, 0)
                    dve.wait_ge(s_cp, 1)
                    dve.tensor_tensor(cb[:, 1:2], bank[1][:, 0:1], vec[:, 4:5], ALU.add).then_inc(s_cst, 1)
                    dve.wait_ge(s_cst, 22)
                    dve.wait_ge(s_padz, 1 + 2 * BORDERS)
                    with dve.Fori(0, B) as n:
                        for b in range(NBLK):
                            par = b % 2
                            dve.wait_ge(s_pk, n * NBLK + b + 1)
                            dve.wait_ge(s_kg, n * P2 + 1)
                            dve.tensor_scalar(kT[:, b * BLK:(b + 1) * BLK], bank[4 * par + 1][:, 0:BLK], vec[:, 1:2],
                                              None, ALU.add).then_inc(s_k, 1)
                            dve.wait_ge(s_pv, n * NBLK + b + 1)
                            vp = [v[:, 1 + b * ROWS:1 + (b + 1) * ROWS, 1:1 + W] for v in vpad]
                            vps = bank[4 * par + 2][:, 0:BLK].rearrange("p (r c) -> p r c", c=W)
                            dve.tensor_scalar(vp[0], vps, vec[:, 2:3], None, ALU.add).then_inc(s_vh, 1)
                            dve.wait_ge(s_k, n * NBLK + b + 1)
                            dve.tensor_reduce(ks[:, b * NWIN:(b + 1) * NWIN], kT[:, b * BLK:(b + 1) * BLK]
                                              .rearrange("p (w k) -> p w k", k=W2), AXX, ALU.add).then_inc(s_qs, 1)
                            dve.wait_ge(s_vh, n * NBLK + b + 1)
                            dve.scalar_tensor_tensor(vp[1], vps, vec[:, 2:3], vp[0].bitcast(F32), ALU.add, ALU.subtract)\
                                .then_inc(s_v, 1)
                            dve.wait_ge(s_q, n * NBLK + b + 1)
                            dve.tensor_reduce(qs[:, b * NWIN:(b + 1) * NWIN], qT[:, b * BLK:(b + 1) * BLK]
                                              .rearrange("p (w k) -> p w k", k=W2), AXX, ALU.add).then_inc(s_qs, 1)
                        dve.wait_ge(s_lg, n + 1)
                        dve.tensor_scalar(lg[:], bank[0][0:P2, 0:P2], 1.0 / (W2 * W2), None, ALU.mult).then_inc(s_tk, 1)
                        dve.wait_ge(s_tk, n * 3 + 2)
                        passed(dve)
                        dve.max(m8[:], lg[:]).then_inc(s_tk, 1)
                        dve.wait_ge(s_tk, n * 3 + 3)
                        dve.wait_ge(s_row, n * 16 + 16)
                        passed(dve)
                        dve.max_index(ix[:], m8[:], lg[:]).then_inc(s_tk, 1)

                        def maxes(w, par):
                            for j in range(PAIRS):
                                dve.wait_ge(s_S, (n * P2 + w + 1) * PAIRS + j + 1)
                                dve.tensor_reduce(nmx[:, par, j:j + 1], bank[j][:, 0:KEYS], AXX, ALU.max, negate=True)\
                                    .then_inc(s_mx, 1)

                        def norm(w, par, att=None):
                            for i in range(2):
                                dve.wait_ge(s_ex, (n * P2 + w) * PAIRS + 2 * i + 3)
                                dve.reciprocal(rden[:, par, 2 * i:2 * i + 2], den[:, par, 2 * i:2 * i + 2])\
                                    .then_inc(s_rd, 1)
                                if i == 0 and att is not None:
                                    dve.wait_ge(s_O, n * P2 + att + 4)
                                    dve.wait_ge(s_o, n * P2 + att + 1)
                                    dve.tensor_scalar(oh[:], bank[6][:, 0:W2], eo[:, 0:1], None, ALU.mult)\
                                        .then_inc(s_om, 1)
                                dve.wait_ge(s_rd, (n * P2 + w) * 2 + i + 1)
                                for j in (2 * i, 2 * i + 1):
                                    ins = dve.tensor_scalar(Pr[:, par, j, :], Pr[:, par, j, :],
                                                            rden[:, par, j:j + 1], None, ALU.mult)
                                if i == 0 and att is not None:
                                    second(att)
                            ins.then_inc(s_nP, 1)

                        def second(w):
                            dve.wait_ge(s_om, n * P2 + w + 1)
                            dve.scalar_tensor_tensor(oT[:, bass.ds(w * W2, W2)], bank[6][:, W2:2 * W2], eo[:, 1:2],
                                                     oh[:], ALU.mult, ALU.add).then_inc(s_o, 1)

                        def attended(w):
                            dve.wait_ge(s_O, n * P2 + w + 4)
                            dve.wait_ge(s_o, n * P2 + w + 1)
                            dve.tensor_scalar(oh[:], bank[6][:, 0:W2], eo[:, 0:1], None, ALU.mult).then_inc(s_om, 1)
                            second(w)

                        maxes(0, 0)
                        norm(0, 0)
                        maxes(1, 1)
                        norm(1, 1)
                        with dve.Fori(0, (P2 - 3) // 2) as k:
                            maxes(k * 2 + 2, 0)
                            norm(k * 2 + 2, 0, k * 2)
                            maxes(k * 2 + 3, 1)
                            norm(k * 2 + 3, 1, k * 2 + 1)
                        maxes(P2 - 1, 0)
                        norm(P2 - 1, 0, P2 - 3)
                        attended(P2 - 2)
                        attended(P2 - 1)
                        more = n < B - 1
                        with dve.If(more):
                            dve.wait_ge(s_ldx[1], 16 * (B - 1))
                            input_stats(dve, following(n))
                        for b in range(NBLK):
                            if b == 3:
                                with dve.If(more):
                                    input_mean(dve, following(n))
                            if b == 4:
                                with dve.If(more):
                                    input_var(dve, following(n))
                            if b == 5:
                                with dve.If(more):
                                    input_scale(dve, following(n))
                            dve.wait_ge(s_out, n * NBLK + b + 1)
                            dve.scalar_tensor_tensor(xblk(n, b), bank[b if b < NBLK - 1 else 7][:, 0:BLK], cb[:, 1:2], xblk(n, b),
                                                     ALU.add, ALU.add).then_inc(s_ev, 1)
                            dve.wait_ge(s_ev, n * NBLK + b + 5)
                            passed(dve)
                            ins = dve.bn_stats(bn[:, b, :], xblk(n, b))
                        ins.then_inc(s_bst, 1)
                        image_stats(dve, n, n)
                        dve.wait_ge(s_mvw, n + 1)

                @block.tensor
                def _(pe):
                    pe.wait_ge(s_w4, 16)
                    input_mean_tensor(pe, 0)
                    input_var_tensor(pe, 0)
                    pe.wait_ge(s_cst, 21)
                    pe.matmul(bank[1][:, 0:1], w_o[:], cb[:, 0:1], start=True, stop=True).then_inc(s_cp, 1)
                    pe.wait_ge(s_cst, 22)
                    pe.wait_ge(s_padz, 1 + 2 * BORDERS)
                    with pe.Fori(0, B) as n:
                        for b in range(NBLK):
                            if b < 2:
                                pe.wait_ge(s_ev, n * NBLK + (1 if b == 0 else 4))
                            par = b % 2
                            xs = xb[:, par, :]
                            bq, bk, bv, bV = bank[4 * par:4 * par + 4]
                            pe.wait_ge(s_xb, n * NBLK + b + 2)
                            if b >= 2:
                                pe.wait_ge(s_q, n * NBLK + b - 1)
                                pe.wait_ge(s_k, n * NBLK + b - 1)
                                pe.wait_ge(s_v, n * NBLK + b - 1)
                                pe.wait_ge(s_V, n * NBLK + b)
                            pe.matmul(bq[:, 0:BLK], w_qkv[:, 0:C], xs, start=True, stop=True).then_inc(s_pq, 1)
                            pe.matmul(bk[:, 0:BLK], w_qkv[:, C:2 * C], xs, start=True, stop=True).then_inc(s_pk, 1)
                            pe.matmul(bv[:, 0:BLK], w_qkv[:, 2 * C:3 * C],
                                      xs.rearrange("p (w r c) -> p r w c", r=ROWS, c=WIN), start=True, stop=True)\
                                .then_inc(s_pv, 1)
                            for i in range(4):
                                m = 128 if i < 3 else 64
                                ins = pe.matmul(bV[0:m, i * C:(i + 1) * C], xs[:, i * 128:i * 128 + m],
                                                w_qkv[:, 2 * C:3 * C], start=True, stop=True)
                            ins.then_inc(s_pV, 1)
                        pe.wait_ge(s_qs, (n + 1) * (2 * NBLK))
                        pe.matmul(bank[0][0:P2, 0:P2], qs[:], ks[:], start=True, stop=True).then_inc(s_lg, 1)
                        pe.wait_ge(s_V, n * NBLK + NBLK + 1)
                        pe.wait_ge(s_v, n * NBLK + NBLK)

                        def depthwise(b, ps, first, last):
                            for k in range(9):
                                dy, dx = divmod(k, 3)
                                at = (slice(None), slice(b * ROWS + dy, b * ROWS + dy + ROWS), slice(dx, dx + W))
                                ins = split_product(pe, ps, (w_tap[0][:, k, :], w_tap[1][:, k, :]),
                                                    (vpad[0][at], vpad[1][at]), first and k == 0, last and k == 8)
                            return ins

                        depthwise(NBLK - 1, bank[7][:, 0:BLK], True, False)
                        pe.wait_ge(s_tk, n * 3 + 2)

                        def scores(w, par):
                            pe.wait_ge(s_kg, n * P2 + w + 2)
                            pe.wait_ge(s_Q, n * P2 + w + 2)
                            for j in range(PAIRS):
                                if not (isinstance(w, int) and w == 0):
                                    pe.wait_ge(s_ex, (n * P2 + w - 1) * PAIRS + j + 2)
                                pe.matmul(bank[j][:, 0:KEYS], Qs[:, par, j * C:(j + 1) * C], kg[:, par, :],
                                          start=True, stop=True).then_inc(s_S, 1)

                        def turn(w, par):
                            pe.wait_ge(s_nP, n * P2 + w + 2)
                            pe.wait_ge(s_Tc, (n * P2 + w) * 2 + 1)
                            for j in range(PAIRS):
                                for c in range(2):
                                    ins = pe.transpose(bank[4 + j // 2][:, (j % 2 * 2 + c) * C:(j % 2 * 2 + c + 1) * C],
                                                       Pr[:, par, j, c * C:(c + 1) * C], ident[:])
                            ins.then_inc(s_T, 1)

                        def attend(w, par, slot, third):
                            pe.wait_ge(s_Tc, (n * P2 + w) * 2 + 3)
                            pe.wait_ge(s_vg[slot], (n * (17 if slot == 0 else 16) + third) * 64 + 64)
                            pe.wait_ge(s_o, n * P2 + w + 1)
                            for j in range(PAIRS):
                                for c in range(2):
                                    ins = pe.matmul(bank[6][32 * j:32 * j + 32, 0:C],
                                                    vg[:, slot, c, 32 * j:32 * j + 32],
                                                    PT[:, par, (2 * j + c) * C:(2 * j + c + 1) * C],
                                                    start=(c == 0), stop=(c == 1))
                            ins.then_inc(s_O, 1)

                        scores(0, 0)
                        scores(1, 1)
                        turn(0, 0)
                        def three(w, i, third):
                            scores(w, i % 2)
                            attend(w - 2, i % 2, i % 3, third)
                            turn(w - 1, (i + 1) % 2)
                        NR = (P2 - 2) // 6
                        with pe.Fori(0, NR) as k:
                            for i in range(6):
                                three(k * 6 + 2 + i, i, k * 2 + i // 3)
                        for i in range((P2 - 2) % 6):
                            three(NR * 6 + 2 + i, i, NR * 2 + i // 3)
                        attend(P2 - 2, 1, (P2 - 2) % 3, (P2 - 2) // 3)
                        pe.wait_ge(s_ex, (n * P2 + P2 - 1) * PAIRS + 2)
                        depthwise(0, bank[0][:, 0:BLK], True, False)
                        turn(P2 - 1, 0)
                        pe.wait_ge(s_ex, (n * P2 + P2 - 1) * PAIRS + 3)
                        depthwise(1, bank[1][:, 0:BLK], True, False)
                        attend(P2 - 1, 0, (P2 - 1) % 3, (P2 - 1) // 3)
                        pe.wait_ge(s_o, n * P2 + P2 + 1)
                        for b in range(NBLK):
                            if b == 3:
                                with pe.If(n < B - 1):
                                    input_mean_tensor(pe, following(n))
                            if b == 4:
                                with pe.If(n < B - 1):
                                    input_var_tensor(pe, following(n))
                            kept = b in (0, 1, NBLK - 1)
                            ps = bank[b if b < NBLK - 1 else 7][:, 0:BLK]
                            ins = pe.matmul(ps, w_o[:], oT[:, b * BLK:(b + 1) * BLK]
                                            .rearrange("p (w r c) -> p r w c", r=ROWS, c=WIN), start=not kept, stop=kept)
                            if not kept:
                                ins = depthwise(b, ps, False, True)
                            ins.then_inc(s_out, 1)

        if last_stage > 1:
            rnn(nc, mk, {**a, "_mv": mv}, X, bank, A, Bb, gn_tensor, gn_vector, gn_scalar, x1_dram, s_gd, s_mvw, passed)
        if last_stage > 2:
            masked_conv(nc, mk, a, X, bank, A, Bb, gn_tensor, gn_vector, gn_scalar, s_gd, bn, s_bst, s_mvw, image_stats,
                        xblk, passed)
        if last_stage > 3:
            conv_pair(nc, mk, a, X, bank, A, Bb, gn_tensor, gn_vector, gn_scalar, xblk, passed, s_gd, out)
        else:
            with nc.semaphore("stored") as s_st, nc.Block() as block:
                @block.sync
                def _(sp):
                    sp.dma_start(out.rearrange("n c h w -> c n (h w)"),
                                 X[:, PAD:PAD + B * HW].rearrange("p (n k) -> p n k", n=B)).then_inc(s_st, 16)
                    sp.wait_ge(s_st, 16)


LAST_STAGE = 4


def kernel(**inputs):
    import numpy as np
    import concourse.bacc as bacc
    from concourse.bass_utils import run_bass_kernel_spmd

    def cols(v, n):
        return v.reshape(n, 128).T

    i = {k: np.asarray(v) for k, v in inputs.items()}
    ch = np.arange(128)
    one = np.float32(1)
    laid = {
        "x": i["x"],
        "w_qkv": i["L0_conv_W_qkv"],
        "b_qkv": cols(i["L0_conv_b_qkv"], 3),
        "b_q": i["L0_conv_b_qkv"][0:128].reshape(128, 1),
        "lepe_w": i["L0_conv_lepe_w"].reshape(128, 9),
        "lepe_b": i["L0_conv_lepe_b"].reshape(128, 1),
        "w_o": i["L0_conv_W_o"],
        "b_o": i["L0_conv_b_o"].reshape(128, 1),
        "gamma": i["L1_conv_gamma"].reshape(128, 1),
        "beta": i["L1_conv_beta"].reshape(128, 1),
        "w_in": i["L1_conv_w_in"].T,
        "b_in": cols(i["L1_conv_b_in"], 2),
        "w_ih": i["L1_conv_w_ih"].T.reshape(2, 128, 512).transpose(1, 0, 2),
        "b_ih": cols(i["L1_conv_b_ih"], 4),
        "w_hh": i["L1_conv_w_hh"].T.reshape(4, 128, 512).transpose(1, 0, 2),
        "b_hh": cols(i["L1_conv_b_hh"], 4),
        "w_out": i["L1_conv_w_out"].T.reshape(4, 128, 128).transpose(1, 0, 2),
        "b_out": i["L1_conv_b_out"].reshape(128, 1),
        "w3": i["L2_conv_w3"].transpose(1, 2, 3, 0).reshape(128, 9, 128),
        "w1": i["L2_conv_w1"].T,
        "b2": i["L2_conv_b"],
        "c1": i["L3_conv_w1"].transpose(1, 2, 3, 0).reshape(128, 9, 128),
        "c2": i["L3_conv_w2"].transpose(1, 2, 3, 0).reshape(128, 9, 128),
        "g1": i["L3_conv_gamma1"].reshape(128, 1), "h1": i["L3_conv_beta1"].reshape(128, 1),
        "m1": i["L3_conv_mean1"].reshape(128, 1), "v1": i["L3_conv_var1"].reshape(128, 1),
        "g2": i["L3_conv_gamma2"].reshape(128, 1), "h2": i["L3_conv_beta2"].reshape(128, 1),
        "m2": i["L3_conv_mean2"].reshape(128, 1), "v2": i["L3_conv_var2"].reshape(128, 1),
        "ident": np.eye(128, dtype=np.float32),
        "group4": (ch[:, None] // GROUP == ch[None, :] // GROUP).astype(np.float32) / np.float32(GROUP),
        "even_odd": np.stack([ch // HD % 2 == 0, ch // HD % 2 == 1], 1).astype(np.float32),
        "head_mask": (ch[:, None] // HD == np.arange(HEADS)[None, :]).astype(np.float32),
        "on_grid": ((ch[:, None] - ch[None, :]) % 4 == 0).astype(np.float32),
        "off_grid": ((ch[:, None] - ch[None, :]) % 4 != 0).astype(np.float32),
        "ones": np.full((128, 1), one),
    }
    nc = bacc.Bacc("TRN2", target_bir_lowering=False, num_devices=1)
    arrays, aps = {}, {}
    for k, v in laid.items():
        v = np.ascontiguousarray(v)
        arrays[f"in_{k}"] = v
        aps[k] = nc.dram_tensor(f"in_{k}", v.shape, F32, kind="ExternalInput").ap()
    out = nc.dram_tensor("out_0", (B, C, H, W), F32, kind="ExternalOutput").ap()
    program(nc, aps, out, LAST_STAGE)
    r = run_bass_kernel_spmd(nc, [arrays], core_ids=[0])
    return r.results[0]["out_0"]
```
